# Optimizing a Trainium2 kernel written in Bass

```python
import numpy as np
import jax
import jax.numpy as jnp

def _softmax(x, axis=-1):
    return jax.nn.softmax(x, axis=axis)

def _gelu(x):
    return jax.nn.gelu(x, approximate=True)

def _silu(x):
    return jax.nn.silu(x)

def _sigmoid(x):
    return jax.nn.sigmoid(x)

def _layernorm(x, axis=-1, eps=1e-05):
    m = jnp.mean(x, axis=axis, keepdims=True)
    v = jnp.var(x, axis=axis, keepdims=True)
    return (x - m) / jnp.sqrt(v + eps)

def _scatter_add(tgt, idx, src, axis=0):
    return tgt.at[idx].add(src)

def _segment_sum(src, seg, n):
    return jax.ops.segment_sum(src, seg, n)
kernel_name = 'mk_prb_d2_jaxref_r8_cd4c79'

def setup_inputs(seed: int=0):
    np.random.seed(seed)
    _w = jnp.asarray

    def _L0_attn_setup():
        import jax, jax.numpy as jnp
        import numpy as np
        B, N = (2, 256)
        H, R = (8, 64)
        IN_DIM, OUT_DIM = (64, 64)
        D = IN_DIM + OUT_DIM
        INIT = 1.0
        key = jax.random.key(seed)
        k1, k2, k3, k4 = jax.random.split(key, 4)
        x = jax.random.normal(k1, (B, N, D), dtype=jnp.float32)
        Wq = jax.random.normal(k2, (H * R, D), dtype=jnp.float32) * (INIT / np.sqrt(H * R * D))
        Wk = jax.random.normal(k3, (H * R, D), dtype=jnp.float32) * (INIT / np.sqrt(H * R * D))
        Wv = jax.random.normal(k4, (H * D, D), dtype=jnp.float32) * (INIT / np.sqrt(H * D * D))
        Wk = Wk.at[:, -1].set(0.0)
        rows = np.arange(1, H + 1) * D - 1
        Wv = Wv.at[rows, :IN_DIM].set(0.0)
        return {'x': x, 'Wq': Wq, 'Wk': Wk, 'Wv': Wv}
    _L0_attn_in = _L0_attn_setup()

    def _L0_ffn_setup():
        import jax, jax.numpy as jnp
        import numpy as np
        NUM_EXPERTS = 8
        CAPACITY = 80
        key = jax.random.key(seed)
        ks = jax.random.split(key, 5)
        D, E, F = (128, NUM_EXPERTS, 512)
        inputs = jax.random.normal(ks[0], (2, 256, D), dtype=jnp.float32)
        gate_w = jax.random.normal(ks[1], (D, E), dtype=jnp.float32) * 0.02
        gate_b = jnp.zeros((E,), dtype=jnp.float32)
        w1 = jax.random.normal(ks[2], (E, D, F), dtype=jnp.float32) * 0.02
        b1 = jnp.zeros((E, F), dtype=jnp.float32)
        w2 = jax.random.normal(ks[3], (E, F, D), dtype=jnp.float32) * 0.02
        b2 = jnp.zeros((E, D), dtype=jnp.float32)
        return {'inputs': inputs, 'gate_w': gate_w, 'gate_b': gate_b, 'w1': w1, 'b1': b1, 'w2': w2, 'b2': b2}
    _L0_ffn_in = _L0_ffn_setup()

    def _L1_attn_setup():
        import jax, jax.numpy as jnp
        import numpy as np
        EPS_RHO = 1e-08
        EPS_DEN = 1e-09

        def _rho_signed_sqrt(x):
            return jnp.sqrt(jax.nn.relu(x) + EPS_RHO) - jnp.sqrt(jax.nn.relu(-x) + EPS_RHO)
        key = jax.random.key(seed)
        ks = jax.random.split(key, 8)
        B, N, C, A = (2, 64, 128, 64)
        s_c = 1.0 / np.sqrt(C)
        s_a = 1.0 / np.sqrt(A)
        return {'X': jax.random.normal(ks[0], (B, N, C), jnp.float32), 'Wq': jax.random.normal(ks[1], (A, C), jnp.float32) * s_c, 'Wk': jax.random.normal(ks[2], (A, C), jnp.float32) * s_c, 'Wphi': jax.random.normal(ks[3], (A,), jnp.float32) * s_a, 'Wy_w': jax.random.normal(ks[4], (C, C), jnp.float32) * s_c, 'Wy_b': jax.random.normal(ks[5], (C,), jnp.float32) * s_c, 'We_w': jax.random.normal(ks[6], (C, A), jnp.float32) * s_a, 'We_b': jax.random.normal(ks[7], (C,), jnp.float32) * s_a}
    _L1_attn_in = _L1_attn_setup()

    def _L1_ffn_setup():
        import jax, jax.numpy as jnp
        import numpy as np
        B, S, H = (2, 128, 128)
        DFF = 256
        E = 8
        TOPK = 2

        def _expert_ffn(x, w1, b1, w2, b2, wg, bg, w3, b3):
            x1 = jnp.einsum('bsh,hf->bsf', x, w1) + b1
            x2 = jnp.einsum('bsh,hf->bsf', x, w2) + b2
            z = x1 * x2
            s = jax.nn.silu(jnp.einsum('bsf,fg->bsg', z, wg) + bg)
            return jnp.einsum('bsg,gh->bsh', s, w3) + b3
        key = jax.random.key(seed)
        ks = jax.random.split(key, 12)
        sc = 0.02
        return {'x': jax.random.normal(ks[0], (B, S, H), jnp.float32), 'gate_w': jax.random.normal(ks[1], (H, E), jnp.float32) * sc, 'gate_b': jnp.zeros((E,), jnp.float32), 'w1': jax.random.normal(ks[2], (E, H, DFF), jnp.float32) * sc, 'b1': jnp.zeros((E, DFF), jnp.float32), 'w2': jax.random.normal(ks[3], (E, H, DFF), jnp.float32) * sc, 'b2': jnp.zeros((E, DFF), jnp.float32), 'wg': jax.random.normal(ks[4], (E, DFF, DFF), jnp.float32) * sc, 'bg': jnp.zeros((E, DFF), jnp.float32), 'w3': jax.random.normal(ks[5], (E, DFF, H), jnp.float32) * sc, 'b3': jnp.zeros((E, H), jnp.float32)}
    _L1_ffn_in = _L1_ffn_setup()
    _d = {'L0_attn_x': _L0_attn_in['x'], 'L0_attn_Wq': _L0_attn_in['Wq'], 'L0_attn_Wk': _L0_attn_in['Wk'], 'L0_attn_Wv': _L0_attn_in['Wv'], 'L0_ffn_gate_w': _L0_ffn_in['gate_w'], 'L0_ffn_gate_b': _L0_ffn_in['gate_b'], 'L0_ffn_w1': _L0_ffn_in['w1'], 'L0_ffn_b1': _L0_ffn_in['b1'], 'L0_ffn_w2': _L0_ffn_in['w2'], 'L0_ffn_b2': _L0_ffn_in['b2'], 'L1_attn_Wq': _L1_attn_in['Wq'], 'L1_attn_Wk': _L1_attn_in['Wk'], 'L1_attn_Wphi': _L1_attn_in['Wphi'], 'L1_attn_Wy_w': _L1_attn_in['Wy_w'], 'L1_attn_Wy_b': _L1_attn_in['Wy_b'], 'L1_attn_We_w': _L1_attn_in['We_w'], 'L1_attn_We_b': _L1_attn_in['We_b'], 'L1_ffn_gate_w': _L1_ffn_in['gate_w'], 'L1_ffn_gate_b': _L1_ffn_in['gate_b'], 'L1_ffn_w1': _L1_ffn_in['w1'], 'L1_ffn_b1': _L1_ffn_in['b1'], 'L1_ffn_w2': _L1_ffn_in['w2'], 'L1_ffn_b2': _L1_ffn_in['b2'], 'L1_ffn_wg': _L1_ffn_in['wg'], 'L1_ffn_bg': _L1_ffn_in['bg'], 'L1_ffn_w3': _L1_ffn_in['w3'], 'L1_ffn_b3': _L1_ffn_in['b3']}
    _x0 = _d['L0_attn_x']
    _d['L0_attn_x'] = jax.random.normal(jax.random.fold_in(jax.random.key(seed), 1), (4, 512, 128), dtype=_x0.dtype)
    del _x0
    return _d

def reference(L0_attn_x, L0_attn_Wq, L0_attn_Wk, L0_attn_Wv, L0_ffn_gate_w, L0_ffn_gate_b, L0_ffn_w1, L0_ffn_b1, L0_ffn_w2, L0_ffn_b2, L1_attn_Wq, L1_attn_Wk, L1_attn_Wphi, L1_attn_Wy_w, L1_attn_Wy_b, L1_attn_We_w, L1_attn_We_b, L1_ffn_gate_w, L1_ffn_gate_b, L1_ffn_w1, L1_ffn_b1, L1_ffn_w2, L1_ffn_b2, L1_ffn_wg, L1_ffn_bg, L1_ffn_w3, L1_ffn_b3):

    def _L0_attn_ref(x, Wq, Wk, Wv):
        import jax, jax.numpy as jnp
        import numpy as np
        B, N = (2, 256)
        H, R = (8, 64)
        IN_DIM, OUT_DIM = (64, 64)
        D = IN_DIM + OUT_DIM
        INIT = 1.0
        b, n, d = x.shape
        Q = (x @ Wq.T).reshape(b, n, H, R)
        K = (x @ Wk.T).reshape(b, n, H, R)
        V = (x @ Wv.T).reshape(b, n, H, d)
        attn = jnp.einsum('bnhr,bmhr->bhnm', Q, K)
        attn = jax.nn.softmax(attn, axis=-1)
        out = jnp.einsum('bhnm,bmhd->bnd', attn, V)
        return out

    def _L0_ffn_ref(inputs, gate_w, gate_b, w1, b1, w2, b2):
        import jax, jax.numpy as jnp
        import numpy as np
        NUM_EXPERTS = 8
        CAPACITY = 80
        D = inputs.shape[-1]
        tokens = inputs.reshape(-1, D)
        logits = tokens @ gate_w + gate_b
        probs = jax.nn.softmax(logits, axis=-1)
        expert_idx = jnp.argmax(probs, axis=-1)
        mask1 = jax.nn.one_hot(expert_idx, NUM_EXPERTS, dtype=jnp.float32)
        pos = jnp.sum(jnp.cumsum(mask1, axis=0) * mask1, axis=-1) - 1.0
        pos = pos.astype(jnp.int32)
        keep = (pos < CAPACITY).astype(jnp.float32)
        gate_prob = jnp.sum(probs * mask1, axis=-1)
        pos_oh = jax.nn.one_hot(pos, CAPACITY, dtype=jnp.float32)
        sec_mask = mask1[:, :, None] * pos_oh[:, None, :] * keep[:, None, None]
        combine_weights = sec_mask * gate_prob[:, None, None]
        dispatch = jnp.einsum('nec,nd->ecd', sec_mask, tokens)
        h = jax.nn.gelu(jnp.einsum('ecd,edf->ecf', dispatch, w1) + b1[:, None, :])
        expert_out = jnp.einsum('ecf,efd->ecd', h, w2) + b2[:, None, :]
        out = jnp.einsum('nec,ecd->nd', combine_weights, expert_out)
        return out.reshape(inputs.shape)

    def _L1_attn_ref(X, Wq, Wk, Wphi, Wy_w, Wy_b, We_w, We_b):
        import jax, jax.numpy as jnp
        import numpy as np
        EPS_RHO = 1e-08
        EPS_DEN = 1e-09

        def _rho_signed_sqrt(x):
            return jnp.sqrt(jax.nn.relu(x) + EPS_RHO) - jnp.sqrt(jax.nn.relu(-x) + EPS_RHO)
        q = jnp.einsum('bnc,ac->bna', X, Wq)
        k = jnp.einsum('bnc,ac->bna', X, Wk)
        Vy = jnp.einsum('bnc,dc->bnd', X, Wy_w) + Wy_b
        e = jax.nn.relu(_rho_signed_sqrt(q[:, :, None, :] + k[:, None, :, :]))
        scores = jnp.einsum('bija,a->bij', e, Wphi)
        m = jnp.max(scores, axis=-1, keepdims=True)
        ex = jnp.exp(scores - m)
        denom = jnp.sum(ex, axis=-1)
        part1 = jnp.einsum('bij,bjc->bic', ex, Vy)
        Ew = jnp.einsum('bij,bija->bia', ex, e)
        part2 = jnp.einsum('bia,ca->bic', Ew, We_w) + We_b * denom[..., None]
        return (part1 + part2) / (denom[..., None] + EPS_DEN)

    def _L1_ffn_ref(x, gate_w, gate_b, w1, b1, w2, b2, wg, bg, w3, b3):
        import jax, jax.numpy as jnp
        import numpy as np
        B, S, H = (2, 128, 128)
        DFF = 256
        E = 8
        TOPK = 2

        def _expert_ffn(x, w1, b1, w2, b2, wg, bg, w3, b3):
            x1 = jnp.einsum('bsh,hf->bsf', x, w1) + b1
            x2 = jnp.einsum('bsh,hf->bsf', x, w2) + b2
            z = x1 * x2
            s = jax.nn.silu(jnp.einsum('bsf,fg->bsg', z, wg) + bg)
            return jnp.einsum('bsg,gh->bsh', s, w3) + b3
        logits = jnp.einsum('bsh,he->bse', x, gate_w) + gate_b
        topv, topi = jax.lax.top_k(logits, TOPK)
        probs = jax.nn.softmax(topv, axis=-1)
        out = jnp.zeros_like(x)
        for e in range(E):
            we = jnp.sum(probs * (topi == e), axis=-1)
            y = _expert_ffn(x, w1[e], b1[e], w2[e], b2[e], wg[e], bg[e], w3[e], b3[e])
            out = out + we[..., None] * y
        return out
    x = L0_attn_x
    xn = _layernorm(x, axis=-1)
    x = x + _L0_attn_ref(xn, L0_attn_Wq, L0_attn_Wk, L0_attn_Wv) + _L0_ffn_ref(xn, L0_ffn_gate_w, L0_ffn_gate_b, L0_ffn_w1, L0_ffn_b1, L0_ffn_w2, L0_ffn_b2)
    xn = _layernorm(x, axis=-1)
    x = x + _L1_attn_ref(xn, L1_attn_Wq, L1_attn_Wk, L1_attn_Wphi, L1_attn_Wy_w, L1_attn_Wy_b, L1_attn_We_w, L1_attn_We_b) + _L1_ffn_ref(xn, L1_ffn_gate_w, L1_ffn_gate_b, L1_ffn_w1, L1_ffn_b1, L1_ffn_w2, L1_ffn_b2, L1_ffn_wg, L1_ffn_bg, L1_ffn_w3, L1_ffn_b3)
    return x

_drawn_inputs = setup_inputs


def setup_inputs(seed=0):
    import zlib

    import numpy as np

    out = dict(_drawn_inputs(seed))
    spreads = {'L0_ffn_gate_b': (0.0, 0.798),
     'L0_ffn_b1': (0.0, 0.8),
     'L0_ffn_b2': (0.0, 0.8),
     'L1_ffn_gate_b': (0.0, 0.267),
     'L1_ffn_b1': (0.0, 0.8),
     'L1_ffn_b2': (0.0, 0.8),
     'L1_ffn_bg': (0.0, 0.8),
     'L1_ffn_b3': (0.0, 0.8)}
    factors = {'L0_attn_Wq': 8.0,
     'L0_attn_Wk': 8.0,
     'L0_attn_Wv': 8.0,
     'L0_ffn_gate_w': 5.604,
     'L0_ffn_w1': 8.0,
     'L0_ffn_w2': 8.0,
     'L1_ffn_w1': 8.0,
     'L1_ffn_w2': 8.0,
     'L1_ffn_wg': 8.0,
     'L1_ffn_w3': 5.878,
     'L1_attn_Wk': 7.741,
     'L1_attn_Wphi': 8.0,
     'L1_attn_Wy_w': 5.062,
     'L1_attn_Wy_b': 5.221,
     'L1_attn_We_b': 4.089}
    for name, (base, spread) in spreads.items():
        noise = np.random.default_rng([zlib.crc32(name.encode()), seed]).standard_normal(out[name].shape)
        drawn = base * np.exp(spread * noise) if base else spread * noise
        out[name] = jnp.asarray(drawn.astype(out[name].dtype))
    for name, factor in factors.items():
        out[name] = (out[name] * factor).astype(out[name].dtype)
    return out
```

```python
from contextlib import ExitStack
import math

import concourse.bass as bass
from concourse import mybir

F32 = mybir.dt.float32
BF16 = mybir.dt.bfloat16
F16 = mybir.dt.float16
U32 = mybir.dt.uint32
ALU = mybir.AluOpType
ACT = mybir.ActivationFunctionType
AX = mybir.AxisListType

P = 128
B, N, D = 4, 512, 128
TOK = B * N
NT = TOK // P
TB = N // P
H, R = 8, 64
E = 8
CAP = 80
SLOTS = E * CAP
ST = SLOTS // P
F0 = 512
FT = F0 // P
DFF = 256
GT = DFF // P
A = 64
BLK = 64
PAIRS = BLK // 2
QUADS = 4
GROUPS = PAIRS // QUADS
LN_EPS = 1e-5
EPS_RHO = 1e-8
EPS_DEN = 1e-9
EX_LIFT = 15
DROPPED = 4096


class Memory:
    pass


class Chain:

    def __init__(self, eng, sem, base=0):
        self.eng, self.sem, self.base, self.n = eng, sem, base, 0

    def step(self, ins):
        self.n += 1
        ins.then_inc(self.sem, 1)
        return self.n

    def done(self, n=None):
        self.eng.wait_ge(self.sem, self.base + (self.n if n is None else n))

    def link(self, ins):
        self.step(ins)
        self.done()


def per_tile(ap, n):
    return ap.unsqueeze(2).to_broadcast([P, ap.shape[1], n])


def first_max(dve, chain, values, desc, top, tie, rank, mask):
    chain.link(dve.reduce_max(top, values, axis=AX.X))
    chain.link(dve.tensor_tensor(tie, values, per_tile(top, E), ALU.is_equal))
    chain.link(dve.tensor_tensor(tie, tie, desc, ALU.mult))
    chain.link(dve.reduce_max(rank, tie, axis=AX.X))
    chain.link(dve.tensor_tensor(mask, desc, per_tile(rank, E), ALU.is_equal))


def norm_scale(dve, chain, x, stats, mv, std, rstd, var_ready, std_ready):
    for t in range(NT):
        chain.step(dve.bn_stats(stats[:, t, :], x[:, t, :]))
    chain.done()
    for t in range(NT):
        chain.step(dve.bn_aggr(mv[:, t, :], stats[:, t, :]))
    chain.done()
    dve.tensor_scalar(std, mv[:, :, 1], LN_EPS, None, ALU.add).then_inc(var_ready, 1)
    dve.wait_ge(std_ready, 1)
    chain.link(dve.reciprocal(rstd, std))


def layers_kernel(nc, x, wqk, wv, gate0_w, gate0_b, w1, b1, w2, b2,
                  a_wq, a_wk, a_phi, a_wy, a_wyb, a_we, a_web,
                  gate1_w, gate1_b, e_w1, e_b1, e_w2, e_b2, e_wg, e_bg, e_w3, e_b3, out):
    g = Memory()
    g.gate0_w, g.gate0_b, g.gate1_w, g.gate1_b = gate0_w, gate0_b, gate1_w, gate1_b
    g.wqk, g.wv, g.w1, g.b1, g.w2, g.b2 = wqk, wv, w1, b1, w2, b2
    g.a_wq, g.a_wk, g.a_phi, g.a_wy, g.a_wyb, g.a_we, g.a_web = a_wq, a_wk, a_phi, a_wy, a_wyb, a_we, a_web
    g.e_w1, g.e_b1, g.e_w2, g.e_b2, g.e_wg, g.e_bg, g.e_w3, g.e_b3 = e_w1, e_b1, e_w2, e_b2, e_wg, e_bg, e_w3, e_b3
    with ExitStack() as ctx:
        def sb(name, shape, dt=F32):
            return ctx.enter_context(nc.sbuf_tensor(name, shape, dt))

        g.x1 = sb("x1", [P, NT, D])
        g.xnT = sb("xnT", [P, TOK])
        g.ident = sb("ident", [P, P])
        g.desc = sb("desc", [P, NT, E])
        g.lg = sb("lg", [P, NT, E])
        g.tie = sb("tie", [P, NT, E])
        g.mask1 = sb("mask1", [P, NT, E])
        g.mask2 = sb("mask2", [P, NT, E])
        g.top = sb("top", [P, NT])
        g.rank = sb("rank", [P, NT])
        g.stats = sb("stats", [P, NT, 6])
        g.mv = sb("mv", [P, NT, 2])
        g.std = sb("std", [P, NT])
        g.rstd = sb("rstd", [P, NT])
        g.coef = sb("coef", [P, NT])
        g.gather_at = sb("gather_at", [P, NT], U32)
        g.gateb = sb("gateb", [P, E])
        g.share = sb("share", [P, NT, E])
        g.arena = sb("arena", [P, 2 * PAIRS * N])
        g.taken = 0

        def take(*shape, dt=F32):
            n = math.prod(shape) * (4 if dt in (F32, U32) else 2) // 4
            v = g.arena[:, g.taken:g.taken + n]
            g.taken += n
            assert g.taken <= 2 * PAIRS * N
            if dt != F32:
                v = v.bitcast(dt)
            if len(shape) == 2:
                v = v.rearrange("p (a b) -> p a b", a=shape[0])
            elif len(shape) == 3:
                v = v.rearrange("p (a b c) -> p a b c", a=shape[0], b=shape[1])
            return v

        g.disp = nc.dram_tensor("disp", (SLOTS, D), F32, kind="Internal").ap()
        g.eout = nc.dram_tensor("eout", (SLOTS, D), F32, kind="Internal").ap()
        g.x_tiles = x.rearrange("b (t p) d -> p (b t) d", p=P)
        g.out_tiles = out.rearrange("b (t p) d -> p (b t) d", p=P)

        g.xn = take(NT, D)
        g.wqk_sb = take(H, P)
        g.wv_sb = take(H * D)
        g.w1_sb = take(E, F0)
        g.w2_sb = take(E, FT, D)
        g.b1_sb = take(E, FT)
        g.b2_sb = take(E, D)
        g.gathered = take(NT, D)

        normalise_and_route(nc, g)
        first_layer(nc, g, take)
        g.taken = 0
        second_route(nc, g, take)
        g.taken = 0
        second_experts(nc, g, take)
        second_attention(nc, g, sb)


def normalise_and_route(nc, g):
    with ExitStack() as ctx:
        def sb(name, shape, dt=F32):
            return ctx.enter_context(nc.sbuf_tensor(name, shape, dt))

        def sem(name):
            return ctx.enter_context(nc.semaphore(name))

        tri = sb("tri", [P, P], BF16)
        ones = sb("ones", [P, P], BF16)
        place0 = sb("place0", [P, NT, E])
        past = sb("past", [P, NT])
        maskb = sb("maskb", [P, NT, E], BF16)
        ex = sb("ex", [P, NT, E])
        esum = sb("esum", [P, NT])
        pre = sb("pre", [P, 2, NT, E])
        queue = sb("queue", [P, NT, E])
        own = sb("own", [P, NT])
        keep = sb("keep", [P, NT])
        slot = sb("slot", [P, NT])
        scatter_at = sb("scatter_at", [P, NT], U32)
        zeros = sb("zeros", [P, ST * D])
        gw = sb("gw", [P, E])
        psX = ctx.enter_context(nc.psum_tensor("psX", [P, 4, 512], F32))
        psL = ctx.enter_context(nc.psum_tensor("psL", [P, NT, E], F32))
        psC = ctx.enter_context(nc.psum_tensor("psC", [P, 2, NT, E], F32))

        x_in, gate_in, w_in = sem("x_in"), sem("gate_in"), sem("w_in")
        pool_made, consts = sem("pool_made"), sem("consts")
        dve_steps, var_ready, std_ready = sem("dve_steps"), sem("var_ready"), sem("std_ready")
        xn_ready, xT_done, xT_kept = sem("xn_ready"), sem("xT_done"), sem("xT_kept")
        logits_done, shifted, exp_done = sem("logits_done"), sem("shifted"), sem("exp_done")
        mask_ready, counts_done, places = sem("mask_ready"), sem("counts_done"), sem("places")
        zero_ready, zero_out, scattered = sem("zero_ready"), sem("zero_out"), sem("scattered")
        block = ctx.enter_context(nc.Block())

        @block.sync
        def _(sp):
            sp.dma_start(g.x1[:], g.x_tiles).then_inc(x_in, 16)
            sp.dma_start(gw[:], g.gate0_w).then_inc(gate_in, 16)
            sp.dma_start(g.gateb[:], g.gate0_b.partition_broadcast(P)).then_inc(gate_in, 16)
            sp.wait_ge(zero_ready, 1)
            sp.dma_start(g.disp.rearrange("(t p) d -> p t d", p=P),
                         zeros[:].rearrange("p (t d) -> p t d", t=ST)).then_inc(zero_out, 16)
            sp.dma_start(g.wqk_sb, g.wqk).then_inc(w_in, 16)
            sp.dma_start(g.wv_sb, g.wv).then_inc(w_in, 16)
            sp.dma_start(g.w1_sb, g.w1.rearrange("e d f -> d e f")).then_inc(w_in, 16)
            sp.dma_start(g.w2_sb.rearrange("p e t d -> p (e t) d"),
                         g.w2.rearrange("e (t p) d -> p (e t) d", p=P)).then_inc(w_in, 16)
            sp.dma_start(g.b1_sb, g.b1).then_inc(w_in, 16)
            sp.dma_start(g.b2_sb[0:1, :, :], g.b2.rearrange("(o e) d -> o e d", o=1)).then_inc(w_in, 16)
            sp.wait_ge(w_in, 96)

        @block.gpsimd
        def _(pool):
            pool.memset(g.ident[:], 0.0).then_inc(pool_made, 1)
            pool.memset(tri[:], 1.0).then_inc(pool_made, 1)
            pool.memset(ones[:], 1.0).then_inc(consts, 1)
            pool.memset(zeros[:], 0.0).then_inc(zero_ready, 1)
            pool.wait_ge(pool_made, 2)
            pool.affine_select(out=g.ident[:], in_=g.ident[:], compare_op=ALU.not_equal, fill=1.0,
                               base=0, pattern=[[-1, P]], channel_multiplier=1).then_inc(consts, 1)
            pool.affine_select(out=tri[:], in_=tri[:], compare_op=ALU.is_ge, fill=0.0,
                               base=0, pattern=[[1, P]], channel_multiplier=-1).then_inc(consts, 1)
            pool.iota(g.desc[:], pattern=[[0, NT], [-1, E]], base=E, channel_multiplier=0,
                      allow_small_or_imprecise_dtypes=True).then_inc(consts, 1)
            pool.iota(place0[:], pattern=[[0, NT], [CAP, E]], base=-1, channel_multiplier=0,
                      allow_small_or_imprecise_dtypes=True).then_inc(consts, 1)
            pool.iota(past[:], pattern=[[P, NT]], base=DROPPED, channel_multiplier=1,
                      allow_small_or_imprecise_dtypes=True).then_inc(consts, 1)
            pool.wait_ge(places, 2)
            pool.wait_ge(zero_out, 16)
            pool.wait_ge(xn_ready, NT)
            for t in range(NT):
                pool.indirect_dma_start(
                    g.disp, bass.IndirectOffsetOnAxis(ap=scatter_at[:, t:t + 1], axis=0),
                    g.xn[:, t, :], None, bounds_check=SLOTS - 1, oob_is_err=False).then_inc(scattered, 16)
            pool.wait_ge(scattered, 16 * NT)

        @block.scalar
        def _(act):
            act.wait_ge(var_ready, 1)
            act.activation(g.std[:], g.std[:], ACT.Sqrt).then_inc(std_ready, 1)
            for c in range(4):
                act.wait_ge(xT_done, c + 1)
                act.activation(g.xnT[:, c * 512:(c + 1) * 512], psX[:, c, :], ACT.Copy).then_inc(xT_kept, 1)
            act.wait_ge(shifted, 1)
            act.activation(ex[:], ex[:], ACT.Exp).then_inc(exp_done, 1)

        @block.vector
        def _(dve):
            chain = Chain(dve, dve_steps)
            dve.wait_ge(x_in, 16)
            norm_scale(dve, chain, g.x1, g.stats, g.mv, g.std[:], g.rstd[:], var_ready, std_ready)
            for t in range(NT):
                dve.tensor_scalar(g.xn[:, t, :], g.x1[:, t, :], g.mv[:, t, 0:1], g.rstd[:, t:t + 1],
                                  ALU.subtract, ALU.mult).then_inc(xn_ready, 1)
            dve.wait_ge(logits_done, 1)
            dve.wait_ge(gate_in, 32)
            dve.wait_ge(consts, 6)
            chain.link(dve.tensor_tensor(g.lg[:], psL[:], g.gateb[:].unsqueeze(1).to_broadcast([P, NT, E]), ALU.add))
            first_max(dve, chain, g.lg[:], g.desc[:], g.top[:], g.tie[:], g.rank[:], g.mask1[:])
            dve.tensor_copy(maskb[:], g.mask1[:]).then_inc(mask_ready, 1)
            dve.tensor_tensor(ex[:], g.lg[:], per_tile(g.top[:], E), ALU.subtract).then_inc(shifted, 1)
            dve.wait_ge(counts_done, 1)
            chain.link(dve.tensor_copy(pre[:, 0], psC[:, 1]))
            at = 0
            for k in (1, 2, 4, 8):
                chain.link(dve.tensor_copy(pre[:, 1 - at, 0:k], pre[:, at, 0:k]))
                chain.link(dve.tensor_tensor(pre[:, 1 - at, k:NT], pre[:, at, k:NT], pre[:, at, 0:NT - k], ALU.add))
                at = 1 - at
            chain.link(dve.tensor_tensor(queue[:], pre[:, at], psC[:, 1], ALU.subtract))
            chain.link(dve.tensor_tensor(queue[:], queue[:], psC[:, 0], ALU.add))
            chain.link(dve.tensor_tensor(g.tie[:], queue[:], g.mask1[:], ALU.mult))
            chain.link(dve.reduce_sum(own[:], g.tie[:], axis=AX.X))
            chain.link(dve.tensor_scalar(keep[:], own[:], float(CAP), None, ALU.is_le))
            chain.link(dve.tensor_tensor(queue[:], queue[:], place0[:], ALU.add))
            chain.link(dve.tensor_tensor(queue[:], queue[:], g.mask1[:], ALU.mult))
            chain.link(dve.reduce_sum(slot[:], queue[:], axis=AX.X))
            chain.link(dve.tensor_tensor(own[:], slot[:], keep[:], ALU.mult))
            dve.tensor_copy(g.gather_at[:], own[:]).then_inc(places, 1)
            chain.link(dve.tensor_tensor(slot[:], slot[:], past[:], ALU.subtract))
            chain.link(dve.tensor_tensor(slot[:], slot[:], keep[:], ALU.mult))
            chain.link(dve.tensor_tensor(slot[:], slot[:], past[:], ALU.add))
            dve.tensor_copy(scatter_at[:], slot[:]).then_inc(places, 1)
            dve.wait_ge(exp_done, 1)
            chain.link(dve.reduce_sum(esum[:], ex[:], axis=AX.X))
            chain.link(dve.reciprocal(esum[:], esum[:]))
            chain.link(dve.tensor_tensor(g.coef[:], esum[:], keep[:], ALU.mult))

        @block.tensor
        def _(pe):
            pe.wait_ge(consts, 6)
            for t in range(NT):
                pe.wait_ge(xn_ready, t + 1)
                ins = pe.transpose(psX[:, t // TB, (t % TB) * P:(t % TB + 1) * P], g.xn[:, t, :], g.ident[:])
                if t % TB == TB - 1:
                    ins.then_inc(xT_done, 1)
            pe.wait_ge(gate_in, 32)
            for t in range(NT):
                if t % TB == 0:
                    pe.wait_ge(xT_kept, t // TB + 1)
                ins = pe.matmul(psL[:, t, :], g.xnT[:, t * P:(t + 1) * P], gw[:], start=True, stop=True)
            ins.then_inc(logits_done, 1)
            pe.wait_ge(mask_ready, 1)
            pe.matmul(psC[:, 0].rearrange("p t e -> p (t e)"), tri[:], maskb[:].rearrange("p t e -> p (t e)"),
                      start=True, stop=True)
            pe.matmul(psC[:, 1].rearrange("p t e -> p (t e)"), ones[:], maskb[:].rearrange("p t e -> p (t e)"),
                      start=True, stop=True).then_inc(counts_done, 1)


def first_layer(nc, g, take):
    STEPS = H * TB
    with ExitStack() as ctx:
        def sem(name):
            return ctx.enter_context(nc.semaphore(name))

        xTb = take(N)
        V = take(TB, H * D)
        qT = take(2, N)
        kT = take(2, N)
        ex = take(3, N)
        pT = take(2, TB, N)
        rows = take(ST, D)
        rowsT = take(SLOTS)
        hT = take(2, FT, CAP)
        eo = take(E, D)
        oT = take(N)
        one_row = take(P)
        nmax = take(4)
        den = take(4)
        rden = take(4)
        ps = ctx.enter_context(nc.psum_tensor("ps0", [P, 8, 512], F32))
        SB, TBK, PJ, AV = (0, 1, 2), (3, 4), 5, 6

        rows_in, prep, zeroed = sem("rows_in"), sem("prep"), sem("zeroed")
        rowsT_done, rowsT_kept = sem("rowsT_done"), sem("rowsT_kept")
        h_done, h_kept, eo_done, eo_kept = sem("h_done"), sem("h_kept"), sem("eo_done"), sem("eo_kept")
        eo_out, gathered_in = sem("eo_out"), sem("gathered_in")
        row_staged, v_done, v_kept = sem("row_staged"), sem("v_done"), sem("v_kept")
        qk_done, qk_kept = sem("qk_done"), sem("qk_kept")
        s_done, nmax_ready, exp_ready = sem("s_done"), sem("nmax_ready"), sem("exp_ready")
        rden_ready, p_ready = sem("rden_ready"), sem("p_ready")
        pT_done, pT_kept, av_done = sem("pT_done"), sem("pT_kept"), sem("av_done")
        oT_kept, o_done, o_added = sem("oT_kept"), sem("o_done"), sem("o_added")
        block = ctx.enter_context(nc.Block())

        @block.sync
        def _(sp):
            sp.dma_start(rows, g.disp.rearrange("(t p) d -> p t d", p=P)).then_inc(rows_in, 16)
            sp.wait_ge(eo_kept, E)
            sp.dma_start(g.eout.rearrange("(e c) d -> c e d", c=CAP), eo[0:CAP, :, :]).then_inc(eo_out, 16)
            sp.wait_ge(eo_out, 16)

        @block.gpsimd
        def _(pool):
            pool.memset(one_row[0:1, :], 1.0).then_inc(prep, 1)
            pool.memset(qT[R:P, :, :], 0.0).then_inc(zeroed, 1)
            pool.memset(kT[R:P, :, :], 0.0).then_inc(zeroed, 1)
            pool.wait_ge(eo_out, 16)
            for t in range(NT):
                pool.indirect_dma_start(
                    g.gathered[:, t, :], None, g.eout,
                    bass.IndirectOffsetOnAxis(ap=g.gather_at[:, t:t + 1], axis=0)).then_inc(gathered_in, 16)
            pool.wait_ge(gathered_in, 16 * NT)

        @block.scalar
        def _(act):
            act.wait_ge(rowsT_done, 1)
            act.activation(rowsT[:, 0:512], ps[:, 0, :], ACT.Copy).then_inc(rowsT_kept, 1)
            act.activation(rowsT[:, 512:SLOTS], ps[:, 1, 0:SLOTS - 512], ACT.Copy).then_inc(rowsT_kept, 1)
            for e in range(E):
                act.wait_ge(h_done, e + 1)
                if e >= 2:
                    act.wait_ge(eo_done, e - 1)
                for f in range(FT):
                    act.activation(hT[:, e % 2, f, :], ps[:, 2 + e % 2, f * CAP:(f + 1) * CAP],
                                   ACT.Gelu_apprx_tanh, bias=g.b1_sb[:, e, f:f + 1]).then_inc(h_kept, 1)
            with act.Fori(0, B) as b:
                for j in range(2 * TB):
                    act.wait_ge(v_done, b * 2 * TB + j + 1)
                    if j % 2 == 0:
                        act.activation(V[:, j // 2, 0:512], ps[:, TBK[0], :], ACT.Copy).then_inc(v_kept, 1)
                    else:
                        act.activation(V[:, j // 2, 512:1024], ps[:, TBK[1], :], ACT.Copy).then_inc(v_kept, 1)

                def exp_step(s):
                    act.wait_ge(nmax_ready, b * STEPS + s + 1)
                    if s >= 3:
                        act.wait_ge(pT_done, b * STEPS + s - 2)
                    act.activation(ex[:, s % 3, :], ps[:, SB[s % 3], :], ACT.Exp, bias=nmax[:, s % 4:s % 4 + 1],
                                   accum_out=den[:, s % 4:s % 4 + 1]).then_inc(exp_ready, 1)

                def keep_pT(s):
                    h, t = s // TB, s % TB
                    act.wait_ge(pT_done, b * STEPS + s + 1)
                    if h >= 2 and t == 0:
                        act.wait_ge(av_done, b * H + h - 1)
                    act.activation(pT[:, h % 2, :, t * P:(t + 1) * P],
                                   ps[:, TBK[s % 2], :].rearrange("p (m n) -> p m n", m=TB),
                                   ACT.Copy).then_inc(pT_kept, 1)

                for s in range(STEPS):
                    exp_step(s)
                    if s >= 2:
                        keep_pT(s - 2)
                keep_pT(STEPS - 2)
                keep_pT(STEPS - 1)

        @block.vector
        def _(dve):
            for e in range(E):
                dve.wait_ge(eo_done, e + 1)
                dve.tensor_copy(eo[0:CAP, e, :], ps[0:CAP, 4 + e % 2, 0:D]).then_inc(eo_kept, 1)
            dve.sem_inc(o_added, 1)
            with dve.Fori(0, B) as b:
                dve.wait_ge(o_done, b + 1)
                dve.tensor_copy(xTb, g.xnT[:, bass.ds(b * N, N)]).then_inc(row_staged, 1)

                def keep_qk(h):
                    dve.wait_ge(qk_done, b * H + h + 1)
                    if h >= 2:
                        dve.wait_ge(s_done, b * STEPS + (h - 1) * TB)
                    dve.tensor_copy(qT[0:R, h % 2, :], ps[0:R, PJ, :]).then_inc(qk_kept, 1)
                    dve.tensor_copy(kT[0:R, h % 2, :], ps[R:P, PJ, :]).then_inc(qk_kept, 1)

                def max_step(s):
                    dve.wait_ge(s_done, b * STEPS + s + 1)
                    if s >= 4:
                        dve.wait_ge(exp_ready, b * STEPS + s - 3)
                    dve.reduce_max(nmax[:, s % 4:s % 4 + 1], ps[:, SB[s % 3], :], axis=AX.X,
                                   negate=True).then_inc(nmax_ready, 1)

                def norm_step(s):
                    dve.wait_ge(exp_ready, b * STEPS + s + 1)
                    dve.reciprocal(rden[:, s % 4:s % 4 + 1], den[:, s % 4:s % 4 + 1]).then_inc(rden_ready, 1)
                    dve.wait_ge(rden_ready, b * STEPS + s + 1)
                    dve.tensor_scalar(ex[:, s % 3, :], ex[:, s % 3, :], rden[:, s % 4:s % 4 + 1], None,
                                      ALU.mult).then_inc(p_ready, 1)

                keep_qk(0)
                for s in range(STEPS):
                    if s % TB == 1 and s // TB + 1 < H:
                        keep_qk(s // TB + 1)
                    max_step(s)
                    if s >= 1:
                        norm_step(s - 1)
                norm_step(STEPS - 1)
                dve.wait_ge(av_done, (b + 1) * H)
                dve.tensor_copy(oT, ps[:, AV, :]).then_inc(oT_kept, 1)
                dve.wait_ge(o_done, b + 2)
                xr = g.x1[:, bass.ds(b * TB, TB), :]
                dve.tensor_tensor(xr, xr, ps[:, TBK[0], :].rearrange("p (t d) -> p t d", t=TB),
                                  ALU.add).then_inc(o_added, 1)

        @block.tensor
        def _(pe):
            pe.wait_ge(rows_in, 16)
            for t in range(ST):
                ins = pe.transpose(ps[:, t // 4, (t % 4) * P:(t % 4 + 1) * P], rows[:, t, :], g.ident[:])
            ins.then_inc(rowsT_done, 1)
            pe.wait_ge(rowsT_kept, 2)
            pe.wait_ge(prep, 1)

            def up(e):
                if e >= 2:
                    pe.wait_ge(h_kept, FT * (e - 1))
                for f in range(FT):
                    ins = pe.matmul(ps[:, 2 + e % 2, f * CAP:(f + 1) * CAP], g.w1_sb[:, e, f * P:(f + 1) * P],
                                    rowsT[:, e * CAP:(e + 1) * CAP], start=True, stop=True)
                ins.then_inc(h_done, 1)

            def down(e):
                pe.wait_ge(h_kept, FT * (e + 1))
                if e >= 2:
                    pe.wait_ge(eo_kept, e - 1)
                pe.matmul(ps[0:CAP, 4 + e % 2, 0:D], one_row[0:1, 0:CAP], g.b2_sb[0:1, e, :], start=True, stop=False)
                for f in range(FT):
                    ins = pe.matmul(ps[0:CAP, 4 + e % 2, 0:D], hT[:, e % 2, f, :], g.w2_sb[:, e, f, :],
                                    start=False, stop=(f == FT - 1))
                ins.then_inc(eo_done, 1)

            up(0)
            for e in range(E):
                if e + 1 < E:
                    up(e + 1)
                down(e)
            pe.wait_ge(eo_kept, E)
            pe.wait_ge(zeroed, 2)
            pe.sem_inc(o_done, 1)
            with pe.Fori(0, B) as b:
                pe.wait_ge(row_staged, b + 1)
                pe.wait_ge(o_added, b + 1)
                for j in range(2 * TB):
                    if j >= 2:
                        pe.wait_ge(v_kept, b * 2 * TB + j - 1)
                    pe.matmul(ps[:, TBK[j % 2], :], xTb[:, (j // 2) * P:(j // 2 + 1) * P],
                              g.wv_sb[:, (j % 2) * 512:(j % 2 + 1) * 512], start=True, stop=True).then_inc(v_done, 1)

                def project(h):
                    if h >= 1:
                        pe.wait_ge(qk_kept, b * 2 * H + 2 * h)
                    pe.matmul(ps[:, PJ, :], g.wqk_sb[:, h, :], xTb, start=True, stop=True).then_inc(qk_done, 1)

                def scores(s):
                    h, t = s // TB, s % TB
                    if t == 0:
                        pe.wait_ge(qk_kept, b * 2 * H + 2 * (h + 1))
                    if s >= 3:
                        pe.wait_ge(exp_ready, b * STEPS + s - 2)
                    pe.matmul(ps[:, SB[s % 3], :], qT[:, h % 2, t * P:(t + 1) * P], kT[:, h % 2, :],
                              start=True, stop=True).then_inc(s_done, 1)

                def transpose_p(s):
                    pe.wait_ge(p_ready, b * STEPS + s + 1)
                    if s >= 2:
                        pe.wait_ge(pT_kept, b * STEPS + s - 1)
                    for m in range(TB):
                        ins = pe.transpose(ps[:, TBK[s % 2], m * P:(m + 1) * P], ex[:, s % 3, m * P:(m + 1) * P],
                                           g.ident[:])
                    ins.then_inc(pT_done, 1)

                def weigh(h):
                    pe.wait_ge(pT_kept, b * STEPS + (h + 1) * TB)
                    for m in range(TB):
                        ins = pe.matmul(ps[:, AV, :], V[:, m, h * D:(h + 1) * D], pT[:, h % 2, m, :],
                                        start=(h == 0 and m == 0), stop=(h == H - 1 and m == TB - 1))
                    ins.then_inc(av_done, 1)

                project(0)
                pe.wait_ge(v_kept, (b + 1) * 2 * TB)
                for s in range(STEPS):
                    scores(s)
                    if s % TB == 0 and s // TB + 1 < H:
                        project(s // TB + 1)
                    if s >= 2:
                        transpose_p(s - 2)
                        if s >= TB + 2 and (s - 3) % TB == TB - 1:
                            weigh((s - 3) // TB)
                transpose_p(STEPS - 2)
                transpose_p(STEPS - 1)
                weigh(H - 1)
                pe.wait_ge(oT_kept, b + 1)
                for t in range(TB):
                    ins = pe.transpose(ps[:, TBK[0], t * P:(t + 1) * P], oT[:, t * P:(t + 1) * P], g.ident[:])
                ins.then_inc(o_done, 1)


def second_route(nc, g, take):
    with ExitStack() as ctx:
        def sb(name, shape, dt=F32):
            return ctx.enter_context(nc.sbuf_tensor(name, shape, dt))

        def sem(name):
            return ctx.enter_context(nc.semaphore(name))

        xn = take(NT, D)
        shareT = take(TOK)
        gw = take(E)
        b3 = take(D)
        p1 = take(NT)
        p2 = take(NT)
        top2 = take(NT)
        term = take(NT, E)
        psX = ctx.enter_context(nc.psum_tensor("psX1", [P, 4, 512], F32))
        psL = ctx.enter_context(nc.psum_tensor("psL1", [P, NT, E], F32))
        gate_in, r_steps = sem("gate1_in"), sem("r_steps")
        var_ready, std_ready = sem("var1_ready"), sem("std1_ready")
        xn_ready, xT_done, xT_kept = sem("xn1_ready"), sem("xT1_done"), sem("xT1_kept")
        logits_done, gap_ready, exp_done = sem("logits1_done"), sem("gap_ready"), sem("exp1_done")
        share_ready, shareT_done, shareT_kept = sem("share_ready"), sem("shareT_done"), sem("shareT_kept")
        b3_done, b3_added = sem("b3_done"), sem("b3_added")
        block = ctx.enter_context(nc.Block())

        @block.sync
        def _(sp):
            sp.dma_start(gw, g.gate1_w).then_inc(gate_in, 16)
            sp.dma_start(g.gateb[:], g.gate1_b.partition_broadcast(P)).then_inc(gate_in, 16)
            sp.dma_start(b3[0:E, :], g.e_b3).then_inc(gate_in, 16)

        @block.scalar
        def _(act):
            act.wait_ge(var_ready, 1)
            act.activation(g.std[:], g.std[:], ACT.Sqrt).then_inc(std_ready, 1)
            for c in range(4):
                act.wait_ge(xT_done, c + 1)
                act.activation(g.xnT[:, c * 512:(c + 1) * 512], psX[:, c, :], ACT.Copy).then_inc(xT_kept, 1)
            act.wait_ge(gap_ready, 1)
            act.activation(p2, p2, ACT.Exp).then_inc(exp_done, 1)
            act.wait_ge(shareT_done, 1)
            act.activation(shareT[0:E, :].rearrange("p (c n) -> p c n", c=4), psX[0:E, :, :],
                           ACT.Copy).then_inc(shareT_kept, 1)

        @block.vector
        def _(dve):
            chain = Chain(dve, r_steps)
            for t in range(NT):
                chain.step(dve.scalar_tensor_tensor(g.x1[:, t, :], g.gathered[:, t, :], g.coef[:, t:t + 1],
                                                    g.x1[:, t, :], ALU.mult, ALU.add))
            chain.done()
            norm_scale(dve, chain, g.x1, g.stats, g.mv, g.std[:], g.rstd[:], var_ready, std_ready)
            for t in range(NT):
                dve.tensor_scalar(xn[:, t, :], g.x1[:, t, :], g.mv[:, t, 0:1], g.rstd[:, t:t + 1],
                                  ALU.subtract, ALU.mult).then_inc(xn_ready, 1)
            dve.wait_ge(logits_done, 1)
            chain.link(dve.tensor_tensor(g.lg[:], psL[:], g.gateb[:].unsqueeze(1).to_broadcast([P, NT, E]), ALU.add))
            first_max(dve, chain, g.lg[:], g.desc[:], g.top[:], g.tie[:], g.rank[:], g.mask1[:])
            chain.link(dve.scalar_tensor_tensor(g.lg[:], g.mask1[:], -1e30, g.lg[:], ALU.mult, ALU.add))
            first_max(dve, chain, g.lg[:], g.desc[:], top2, g.tie[:], g.rank[:], g.mask2[:])
            dve.tensor_tensor(p2, top2, g.top[:], ALU.subtract).then_inc(gap_ready, 1)
            dve.wait_ge(exp_done, 1)
            chain.link(dve.tensor_scalar(p1, p2, 1.0, None, ALU.add))
            chain.link(dve.reciprocal(p1, p1))
            chain.link(dve.tensor_tensor(p2, p2, p1, ALU.mult))
            chain.link(dve.tensor_tensor(term, g.mask1[:], per_tile(p1, E), ALU.mult))
            chain.link(dve.tensor_tensor(g.mask2[:], g.mask2[:], per_tile(p2, E), ALU.mult))
            dve.tensor_tensor(g.share[:], term, g.mask2[:], ALU.add).then_inc(share_ready, 1)
            for c in range(4):
                dve.wait_ge(b3_done, c + 1)
                xr = g.x1[:, c * TB:(c + 1) * TB, :]
                dve.tensor_tensor(xr, xr, psX[:, c, :].rearrange("p (t d) -> p t d", t=TB), ALU.add).then_inc(b3_added, 1)

        @block.tensor
        def _(pe):
            for t in range(NT):
                pe.wait_ge(xn_ready, t + 1)
                ins = pe.transpose(psX[:, t // TB, (t % TB) * P:(t % TB + 1) * P], xn[:, t, :], g.ident[:])
                if t % TB == TB - 1:
                    ins.then_inc(xT_done, 1)
            pe.wait_ge(gate_in, 48)
            for t in range(NT):
                if t % TB == 0:
                    pe.wait_ge(xT_kept, t // TB + 1)
                ins = pe.matmul(psL[:, t, :], g.xnT[:, t * P:(t + 1) * P], gw, start=True, stop=True)
            ins.then_inc(logits_done, 1)
            pe.wait_ge(share_ready, 1)
            for t in range(NT):
                ins = pe.transpose(psX[0:E, t // TB, (t % TB) * P:(t % TB + 1) * P], g.share[:, t, :], g.ident[:])
            ins.then_inc(shareT_done, 1)
            pe.wait_ge(shareT_kept, 1)
            for t in range(NT):
                ins = pe.matmul(psX[:, t // TB, (t % TB) * P:(t % TB + 1) * P], shareT[0:E, t * P:(t + 1) * P],
                                b3[0:E, :], start=True, stop=True)
                if t % TB == TB - 1:
                    ins.then_inc(b3_done, 1)


def second_experts(nc, g, take):
    C = TOK // N
    UNITS = 2 * C
    with ExitStack() as ctx:
        def sem(name):
            return ctx.enter_context(nc.semaphore(name))

        w1 = take(2, DFF)
        w2 = take(2, DFF)
        wg = take(2, GT * DFF)
        w3 = take(2, GT * D)
        b1, b2, bg = take(E, GT), take(E, GT), take(E, GT)
        left = take(GT, N)
        z = take(2 * GT, N)
        s = take(2 * GT, N)
        ps = ctx.enter_context(nc.psum_tensor("ps1", [P, 8, 512], F32))
        LEFT, RIGHT, GATE, OUT = 0, 2, 4, 6
        b_in, w_in = sem("b_in"), [sem("w_in0"), sem("w_in1")]
        up_done, left_kept, z_ready = sem("up_done"), sem("left_kept"), sem("z_ready")
        gate_done, s_ready, y_done, y_added = sem("gate_done"), sem("s_ready"), sem("y_done"), sem("y_added")
        act_passed = sem("act_passed1")
        block = ctx.enter_context(nc.Block())

        @block.sync
        def _(sp):
            for v, src in ((b1, g.e_b1), (b2, g.e_b2), (bg, g.e_bg)):
                sp.dma_start(v, src).then_inc(b_in, 16)
            with sp.Fori(0, E // 2) as ep:
                for j in range(2):
                    sp.wait_ge(y_done, ep * UNITS + 1)
                    e = ep * 2 + j
                    sp.dma_start(w1[:, j, :], g.e_w1[bass.ds(e, 1), :, :].rearrange("e d f -> (e d) f")).then_inc(w_in[j], 16)
                    sp.dma_start(w2[:, j, :], g.e_w2[bass.ds(e, 1), :, :].rearrange("e d f -> (e d) f")).then_inc(w_in[j], 16)
                    sp.dma_start(wg[:, j, :].rearrange("p (t n) -> p t n", t=GT),
                                 g.e_wg[bass.ds(e, 1), :, :].rearrange("e (t p) n -> p (e t) n", p=P)).then_inc(w_in[j], 16)
                    sp.dma_start(w3[:, j, :].rearrange("p (t n) -> p t n", t=GT),
                                 g.e_w3[bass.ds(e, 1), :, :].rearrange("e (t p) n -> p (e t) n", p=P)).then_inc(w_in[j], 16)

        @block.scalar
        def _(act):
            act.wait_ge(b_in, 48)
            with act.Fori(0, E // 2) as ep:
                def keep_left(u):
                    act.wait_ge(up_done, ep * UNITS + u + 1)
                    if u >= 1:
                        act.wait_ge(z_ready, (ep * UNITS + u) * GT)
                    act.sem_inc(act_passed, 1)
                    for f in range(GT):
                        act.activation(left[:, f, :], ps[:, LEFT + f, :], ACT.Identity,
                                       bias=b1[:, bass.ds(ep * 2 + u // C, 1), f]).then_inc(left_kept, 1)

                def silu(u):
                    act.wait_ge(gate_done, ep * UNITS + u + 1)
                    if u >= 2:
                        act.wait_ge(y_done, ep * UNITS + u)
                    act.sem_inc(act_passed, 1)
                    for f in range(GT):
                        act.activation(s[:, (u % 2) * GT + f, :], ps[:, GATE + f, :], ACT.Silu,
                                       bias=bg[:, bass.ds(ep * 2 + u // C, 1), f]).then_inc(s_ready, 1)

                keep_left(0)
                for u in range(UNITS):
                    if u + 1 < UNITS:
                        keep_left(u + 1)
                    silu(u)

        @block.vector
        def _(dve):
            dve.wait_ge(b_in, 48)
            with dve.Fori(0, E // 2) as ep:
                def product(u):
                    if u >= 2:
                        dve.wait_ge(gate_done, ep * UNITS + u - 1)
                    for f in range(GT):
                        dve.wait_ge(left_kept, (ep * UNITS + u) * GT + f + 1)
                        dve.scalar_tensor_tensor(z[:, (u % 2) * GT + f, :], ps[:, RIGHT + f, :],
                                                 b2[:, bass.ds(ep * 2 + u // C, 1), f], left[:, f, :],
                                                 ALU.add, ALU.mult).then_inc(z_ready, 1)

                def add(u):
                    dve.wait_ge(y_done, ep * UNITS + u + 2)
                    if u >= C:
                        dve.wait_ge(y_added, (ep * UNITS + u - C + 1) * TB)
                    for i in range(TB):
                        t = (u % C) * TB + i
                        dve.scalar_tensor_tensor(g.x1[:, t, :], ps[:, OUT + u % 2, i * D:(i + 1) * D],
                                                 g.share[:, t, bass.ds(ep * 2 + u // C, 1)], g.x1[:, t, :],
                                                 ALU.mult, ALU.add).then_inc(y_added, 1)

                product(0)
                for u in range(UNITS):
                    if u + 1 < UNITS:
                        product(u + 1)
                    add(u)
                dve.wait_ge(y_added, (ep + 1) * UNITS * TB)

        @block.tensor
        def _(pe):
            pe.sem_inc(y_done, 1)
            with pe.Fori(0, E // 2) as ep:
                def up(u):
                    j = u // C
                    if u % C == 0:
                        pe.wait_ge(w_in[j], (ep + 1) * 64)
                    if u >= 1:
                        pe.wait_ge(z_ready, (ep * UNITS + u) * GT)
                    for w, bank in ((w1, LEFT), (w2, RIGHT)):
                        for f in range(GT):
                            ins = pe.matmul(ps[:, bank + f, :], w[:, j, f * P:(f + 1) * P],
                                            g.xnT[:, (u % C) * N:(u % C + 1) * N], start=True, stop=True)
                    ins.then_inc(up_done, 1)

                def gate(u):
                    j = u // C
                    pe.wait_ge(z_ready, (ep * UNITS + u + 1) * GT)
                    if u >= 1:
                        pe.wait_ge(s_ready, (ep * UNITS + u) * GT)
                    for m in range(GT):
                        for f in range(GT):
                            ins = pe.matmul(ps[:, GATE + m, :], wg[:, j, f * DFF + m * P:f * DFF + (m + 1) * P],
                                            z[:, (u % 2) * GT + f, :], start=(f == 0), stop=(f == GT - 1))
                    ins.then_inc(gate_done, 1)

                def down(u):
                    j = u // C
                    pe.wait_ge(s_ready, (ep * UNITS + u + 1) * GT)
                    if u >= 2:
                        pe.wait_ge(y_added, (ep * UNITS + u - 1) * TB)
                    for i in range(TB):
                        for f in range(GT):
                            ins = pe.matmul(ps[:, OUT + u % 2, i * D:(i + 1) * D],
                                            s[:, (u % 2) * GT + f, i * P:(i + 1) * P],
                                            w3[:, j, f * D:(f + 1) * D], start=(f == 0), stop=(f == GT - 1))
                    ins.then_inc(y_done, 1)

                up(0)
                for u in range(UNITS):
                    if u + 1 < UNITS:
                        up(u + 1)
                    gate(u)
                    down(u)
                pe.wait_ge(y_added, (ep + 1) * UNITS * TB)


def second_attention(nc, g, sb):
    x1, xnT, ident = g.x1, g.xnT, g.ident
    MB = TOK // BLK
    BB = N // BLK
    ON_ACT = 1
    ON_DVE = QUADS - ON_ACT
    DV = D + 1
    with ExitStack() as ctx:
        def sem(name):
            return ctx.enter_context(nc.semaphore(name))

        feat = g.arena[:].rearrange("p (s k n) -> p s k n", s=2, k=PAIRS)
        kT = sb("kT2", [P, TOK])
        q2 = sb("q2", [P, TOK // 2])
        V = sb("V2", [P, NT, DV])
        phi_cols = sb("phi_cols", [P, GROUPS, 32])
        sel = sb("sel", [P, GROUPS, QUADS, P], F16)
        weT = sb("weT", [P, DV])
        bias_out = sb("bias_out", [P, D])
        split_by = sb("split_by", [P, 1])
        eps = sb("eps", [P, 1])
        ex = sb("ex2", [P, 2, N])
        exh = sb("exh", [P, N], F16)
        part = sb("part", [P, N], F16)
        spread = sb("spread", [P, 2, N], F16)
        exT = sb("exT", [P, 2, TB, P])
        nmax = sb("nmax2", [P, 2])
        shift = sb("shift", [P, 2])
        sums = sb("sums", [P, 2, GROUPS, QUADS])
        sumsT = sb("sumsT", [P, 2, P])
        den = sb("den2", [P, 2])
        res = sb("res", [P, 2, D])
        rot = sb("rot", [P, 2, D])

        psS = ctx.enter_context(nc.psum_tensor("psS", [P, 2, 512], F32))
        psB = ctx.enter_context(nc.psum_tensor("psB", [P, QUADS, 512], F32))
        psT = ctx.enter_context(nc.psum_tensor("psT", [P, 512], F32))
        psO = ctx.enter_context(nc.psum_tensor("psO", [P, 512], F32))

        wq, wk = feat[:, 1, 0, 0:P], feat[:, 1, 0, P:2 * P]
        wy, wyb = feat[:, 1, 0, 2 * P:3 * P], feat[:, 1, 0, 3 * P:4 * P]
        web, phi = feat[:, 1, 1, 0:D], feat[:, 1, 1, D:D + 1]
        rho = feat[:, 1, 2, 0:P]
        mask_c = feat[:, 1, 3, 0:QUADS]

        w2_in, c2_made, c2_ready, prep = sem("w2_in"), sem("c2_made"), sem("c2_ready"), sem("prep2")
        pq_done, pq_kept = sem("pq_done"), sem("pq_kept")
        feat_ready, act_feat, e_ready = sem("feat_ready"), sem("act_feat"), sem("e_ready")
        s_done, max_ready, shift_ready = sem("s2_done"), sem("max_ready"), sem("shift_ready")
        ex_ready, exh_ready, split_step, spread_ready = sem("ex_ready"), sem("exh_ready"), sem("split_step"), sem("spread_ready")
        bc_done, reduced, placed = sem("bc_done"), sem("reduced"), sem("placed")
        exT_done, exT_kept = sem("exT_done"), sem("exT_kept")
        o_done, fin_steps, fin_ready, out_done = sem("o2_done"), sem("fin_steps"), sem("fin_ready"), sem("out_done")
        act_passed, pool_passed = sem("act_passed"), sem("pool_passed")

        with nc.Block() as block:
            @block.sync
            def _(sp):
                sp.dma_start(wq, g.a_wq).then_inc(w2_in, 16)
                sp.dma_start(wk, g.a_wk).then_inc(w2_in, 16)
                sp.dma_start(wy, g.a_wy).then_inc(w2_in, 16)
                sp.dma_start(wyb, g.a_wyb.partition_broadcast(P)).then_inc(w2_in, 16)
                sp.dma_start(web, g.a_web.partition_broadcast(P)).then_inc(w2_in, 16)
                sp.dma_start(phi, g.a_phi).then_inc(w2_in, 16)
                sp.dma_start(weT[:, 0:D], g.a_we).then_inc(w2_in, 16)

            @block.gpsimd
            def _(pool):
                pool.memset(sel[:], 0.0).then_inc(c2_made, 1)
                pool.memset(mask_c, 1.0).then_inc(c2_made, 1)
                pool.memset(phi_cols[:], 0.0).then_inc(c2_ready, 1)
                pool.memset(weT[:, D:DV], 0.0).then_inc(c2_ready, 1)
                pool.memset(V[:, :, D:DV], 1.0).then_inc(c2_ready, 1)
                pool.memset(sumsT[:], 0.0).then_inc(c2_ready, 1)
                pool.memset(exT[:], 0.0).then_inc(c2_ready, 1)
                pool.memset(eps[:], EPS_RHO).then_inc(c2_ready, 1)
                pool.memset(rho, -math.sqrt(EPS_RHO)).then_inc(c2_ready, 1)
                pool.wait_ge(c2_made, 2)
                v = sel[:].rearrange("p g c (h a) -> p g c h a", h=2)
                for gg in range(GROUPS):
                    for half in range(2):
                        if half:
                            pool.wait_ge(prep, gg + 1)
                        ins = pool.affine_select(out=v[:, gg], in_=v[:, gg], compare_op=ALU.not_equal, fill=1.0,
                                                 base=-2 * gg - 16 * half, pattern=[[-32, QUADS], [-1, 2], [0, A]],
                                                 channel_multiplier=1)
                        ins.then_inc(c2_ready if half else prep, 1)
                pool.affine_select(out=mask_c, in_=mask_c, compare_op=ALU.is_ge, fill=0.0, base=-16,
                                   pattern=[[-32, QUADS]], channel_multiplier=1).then_inc(c2_made, 1)
                pool.wait_ge(c2_made, 3)
                pool.affine_select(out=mask_c, in_=mask_c, compare_op=ALU.is_ge, fill=0.0, base=31,
                                   pattern=[[32, QUADS]], channel_multiplier=-1).then_inc(c2_ready, 1)

            CONSTS = 7 + GROUPS + 1

            @block.vector
            def _(dve):
                dve.wait_ge(w2_in, 7 * 16)
                dve.wait_ge(c2_ready, CONSTS)
                flat = phi_cols[:].rearrange("p g n -> p (g n)")
                for h in range(2):
                    for d in range(2):
                        at = 16 * d + h
                        col = flat[h * A:(h + 1) * A, at:at + 34 * (GROUPS - 1) + 1:34]
                        dve.tensor_copy(col, phi[h * A:(h + 1) * A, :].to_broadcast([A, GROUPS])).then_inc(pq_kept, 1)
                dve.tensor_reduce(split_by[:], mask_c, axis=AX.X, op=ALU.add, negate=True).then_inc(pq_kept, 1)
                n = 0
                for c in range(B):
                    dve.wait_ge(pq_done, 3 * c + 1)
                    qv = psS[:, 0, :].rearrange("p (n h) -> p n h", h=2)
                    for h in range(2):
                        dve.tensor_copy(q2[h * A:(h + 1) * A, c * N // 2:(c + 1) * N // 2],
                                        qv[h * A:(h + 1) * A, :, h]).then_inc(pq_kept, 1)
                    dve.wait_ge(pq_done, 3 * c + 2)
                    dve.tensor_copy(kT[:, c * N:(c + 1) * N], psS[:, 1, :]).then_inc(pq_kept, 1)
                    dve.wait_ge(pq_done, 3 * c + 3)
                    dve.tensor_tensor(V[:, c * TB:(c + 1) * TB, 0:D], psB[:, c, :].rearrange("p (t d) -> p t d", t=TB),
                                      wyb.unsqueeze(1).to_broadcast([P, TB, D]), ALU.add).then_inc(pq_kept, 1)
                dve.wait_ge(pq_done, 3 * B + 1)
                dve.tensor_tensor(bias_out[:], psT[:, 0:D], web, ALU.add).then_inc(pq_kept, 1)

            @block.tensor
            def _(pe):
                pe.wait_ge(w2_in, 7 * 16)
                pe.wait_ge(c2_ready, CONSTS)
                for c in range(B):
                    if c:
                        pe.wait_ge(pq_kept, 5 + 4 * c)
                    xc = xnT[:, c * N:(c + 1) * N]
                    pe.matmul(psS[:, 0, :], wq, xc, start=True, stop=True).then_inc(pq_done, 1)
                    pe.matmul(psS[:, 1, :], wk, xc, start=True, stop=True).then_inc(pq_done, 1)
                    for i in range(TB):
                        t = c * TB + i
                        ins = pe.matmul(psB[:, c, i * D:(i + 1) * D], xnT[:, t * P:(t + 1) * P], wy,
                                        start=True, stop=True)
                    ins.then_inc(pq_done, 1)
                pe.matmul(psT[:, 0:D], rho[0:A, :], weT[0:A, 0:D], start=True, stop=True).then_inc(pq_done, 1)

        FEATURE_LAG, SCORE_LAG = 1, 3

        def behind(m, j, gg, lag):
            if gg >= lag:
                return m + 2, j, gg - lag, 2
            return m + 1, 1 - j, gg - lag + GROUPS, 1

        def makes(late, first, last):
            return not last or (late[1] == 1 and late[3] == 1)

        def slot_parts(m):
            return m // BB, m * PAIRS

        with nc.Block() as block:
            @block.vector
            def _(dve):
                def features(m, j, gg):
                    b, pair0 = slot_parts(m)
                    for c in range(ON_DVE):
                        dve.tensor_scalar(feat[:, j, QUADS * gg + c, :], kT[:, bass.ds(b * N, N)],
                                          q2[:, bass.ds(pair0 + GROUPS * c + gg, 1)], 0.0,
                                          ALU.add, ALU.max).then_inc(feat_ready, 1)

                def largest(m, j):
                    dve.wait_ge(s_done, m + 1)
                    dve.reduce_max(nmax[:, j:j + 1], psS[:, j, :], axis=AX.X, negate=True).then_inc(max_ready, 1)
                    dve.wait_ge(max_ready, m + 1)
                    dve.tensor_scalar(shift[:, j:j + 1], nmax[:, j:j + 1], EX_LIFT * math.log(2.0), None,
                                      ALU.add).then_inc(shift_ready, 1)

                def reduce_pairs(m, j, gg):
                    for c in range(QUADS):
                        k = QUADS * gg + c
                        dve.wait_ge(bc_done, m * PAIRS + k + 1)
                        dve.scalar_tensor_tensor(feat[:, j, k, :], feat[:, j, k, :], 1.0, psB[:, c, :],
                                                 ALU.mult, ALU.mult,
                                                 accum_out=sums[:, j, gg, c:c + 1]).then_inc(reduced, 1)

                def finish(t, r):
                    n0 = t * 4
                    dve.wait_ge(o_done, 2 * (t + 1))
                    dve.wait_ge(out_done, t * 16 + 16)
                    dve.tensor_scalar(den[:, 0:1], psO[:, D:DV], EPS_DEN * 2.0 ** EX_LIFT, None,
                                      ALU.add).then_inc(fin_steps, 1)
                    dve.wait_ge(fin_steps, n0 + 1)
                    dve.reciprocal(den[:, 0:1], den[:, 0:1]).then_inc(fin_steps, 1)
                    dve.wait_ge(fin_steps, n0 + 2)
                    dve.tensor_tensor(den[:, 1:2], den[:, 0:1], psO[:, D:DV], ALU.mult).then_inc(fin_steps, 1)
                    dve.wait_ge(fin_steps, n0 + 3)
                    dve.scalar_tensor_tensor(rot[:, 0, :], bias_out[:], den[:, 1:2], x1[:, bass.ds(t, 1), :].rearrange("p t d -> p (t d)"),
                                             ALU.mult, ALU.add).then_inc(fin_steps, 1)
                    dve.wait_ge(fin_steps, n0 + 4)
                    dve.scalar_tensor_tensor(res[:, 0, :], psO[:, 0:D], den[:, 0:1], rot[:, 0, :],
                                             ALU.mult, ALU.add).then_inc(fin_ready, 1)

                def tile(t, first=False, last=False):
                    for j in range(2):
                        m = t * 2 + j
                        for gg in range(GROUPS):
                            reduce_pairs(m, j, gg)
                            late = behind(m, j, gg, FEATURE_LAG)
                            if makes(late, first, last):
                                if not (first and late[3] == 1):
                                    dve.wait_ge(reduced, (late[0] - 2) * PAIRS + QUADS * (late[2] + 1))
                                features(*late[0:3])
                            if gg == SCORE_LAG and not (last and j == 1):
                                largest(m + 1, 1 - j)
                            if j == 0 and gg == 5 and not first:
                                finish(t - 1, 0)

                for n in range(2 * GROUPS - FEATURE_LAG):
                    features(n // GROUPS, n // GROUPS, n % GROUPS)
                    if n == GROUPS + SCORE_LAG:
                        largest(0, 0)
                tile(0, first=True)
                with dve.Fori(1, NT - 1) as t:
                    tile(t)
                tile(NT - 1, last=True)
                finish(NT - 1, 0)

            @block.scalar
            def _(act):
                def roots(m, j, gg, before=True):
                    b, pair0 = slot_parts(m)
                    n = m * GROUPS + gg
                    if before:
                        act.wait_ge(reduced, m * PAIRS - 2 * PAIRS + QUADS * (gg + 1))
                    act.sem_inc(act_passed, 1)
                    for c in range(ON_DVE, QUADS):
                        act.activation(feat[:, j, QUADS * gg + c, :], kT[:, bass.ds(b * N, N)], ACT.Relu,
                                       bias=q2[:, bass.ds(pair0 + GROUPS * c + gg, 1)]).then_inc(act_feat, 1)
                    act.wait_ge(feat_ready, (n + 1) * ON_DVE)
                    act.wait_ge(act_feat, (n + 1) * ON_ACT)
                    grp = feat[:, j, QUADS * gg:QUADS * (gg + 1), :].rearrange("p k n -> p (k n)")
                    act.activation(grp, grp, ACT.Sqrt, bias=eps[:]).then_inc(e_ready, 1)

                def exponentials(m, j, before=2):
                    act.wait_ge(shift_ready, m + 1)
                    if before == 2:
                        act.wait_ge(exT_done, m - 1)
                        act.wait_ge(spread_ready, m - 1)
                    act.activation(ex[:, j, :], psS[:, j, :], ACT.Exp, bias=shift[:, j:j + 1]).then_inc(ex_ready, 1)
                    if before:
                        act.wait_ge(split_step, m)
                    act.activation(exh[:], psS[:, j, :], ACT.Exp, bias=shift[:, j:j + 1]).then_inc(exh_ready, 1)

                def keep_exT(m, j, warm=True):
                    act.wait_ge(exT_done, m + 1)
                    if warm:
                        act.wait_ge(o_done, m - 1)
                    act.activation(exT[:, j, :, j * BLK:(j + 1) * BLK].rearrange("p t (c r) -> p t c r", c=QUADS),
                                   psT[:, :].rearrange("p (t c r) -> p t c r", t=TB, c=QUADS)[:, :, :, 0:16],
                                   ACT.Copy).then_inc(exT_kept, 1)

                def tile(t, first=False, last=False):
                    for j in range(2):
                        m = t * 2 + j
                        for gg in range(GROUPS):
                            late = behind(m, j, gg, FEATURE_LAG)
                            if makes(late, first, last):
                                roots(*late[0:3], before=not (first and late[3] == 1))
                            if gg == SCORE_LAG and not (last and j == 1):
                                exponentials(m + 1, 1 - j, before=1 if first and j == 0 else 2)
                            if gg == GROUPS - 1 and not (last and j == 1):
                                keep_exT(m + 1, 1 - j, warm=not (first and j == 0))

                for n in range(2 * GROUPS - FEATURE_LAG):
                    roots(n // GROUPS, n // GROUPS, n % GROUPS, before=False)
                    if n == GROUPS + SCORE_LAG:
                        exponentials(0, 0, before=0)
                keep_exT(0, 0, warm=False)
                tile(0, first=True)
                with act.Fori(1, NT - 1) as t:
                    tile(t)
                tile(NT - 1, last=True)

            @block.gpsimd
            def _(pool):
                def split(m, j, before=2):
                    pool.wait_ge(exh_ready, m + 1)
                    if before:
                        pool.wait_ge(spread_ready, m)
                    if before == 2:
                        pool.wait_ge(placed, 2 * (m - 1))
                    if before == 2:
                        pool.wait_ge(bc_done, (m - 1) * PAIRS)
                    pool.sem_inc(pool_passed, 1)
                    pool.tensor_scalar(part[:], exh[:], split_by[:], None, ALU.mult).then_inc(split_step, 1)
                    pool.wait_ge(split_step, m + 1)
                    pool.tensor_tensor(spread[:, j, :], part[:], ex[:, j, :], ALU.add).then_inc(spread_ready, 1)

                def place(m, j, last_split, warm=True):
                    pool.wait_ge(reduced, (m + 1) * PAIRS)
                    if warm:
                        pool.wait_ge(o_done, m - 1)
                    v = sumsT[:, j, j * BLK:(j + 1) * BLK].rearrange("p (c g h) -> p g c h", c=QUADS, h=2)
                    for h in range(2):
                        if h:
                            pool.wait_ge(placed, 2 * m + 1)
                        else:
                            pool.wait_ge(spread_ready, last_split)
                        pool.sem_inc(pool_passed, 1)
                        pool.tensor_copy(v[h * A:(h + 1) * A, :, :, h], sums[h * A:(h + 1) * A, j]).then_inc(placed, 1)

                def tile(t, first=False, last=False):
                    for j in range(2):
                        m = t * 2 + j
                        if not (last and j == 1):
                            split(m + 1, 1 - j, before=1 if first and j == 0 else 2)
                        place(m, j, m + 1 if last and j == 1 else m + 2, warm=not first)

                split(0, 0, before=0)
                tile(0, first=True)
                with pool.Fori(1, NT - 1) as t:
                    tile(t)
                tile(NT - 1, last=True)

            @block.tensor
            def _(pe):
                def scores(m, j, gg):
                    pe.wait_ge(e_ready, m * GROUPS + gg + 1)
                    for c in range(QUADS):
                        ins = pe.matmul(psS[32 * c:32 * (c + 1), j, :], phi_cols[:, gg, :],
                                        feat[:, j, QUADS * gg + c, :], start=(gg == 0), stop=(gg == GROUPS - 1))
                    if gg == GROUPS - 1:
                        ins.then_inc(s_done, 1)

                def broadcast(m, j, gg, warm=True):
                    for c in range(QUADS):
                        k = QUADS * gg + c
                        if warm or k >= QUADS:
                            pe.wait_ge(reduced, m * PAIRS + k - QUADS + 1)
                        pe.matmul(psB[:, c, :], sel[:, gg, c, :], spread[:, j, :], start=True, stop=True).then_inc(bc_done, 1)

                def transpose_ex(m, j, warm=True):
                    pe.wait_ge(ex_ready, m + 1)
                    if warm:
                        pe.wait_ge(exT_kept, m)
                    for i in range(TB):
                        ins = pe.transpose(psT[:, i * P:(i + 1) * P], ex[:, j, i * P:(i + 1) * P], ident[:])
                    ins.then_inc(exT_done, 1)

                def combine(m, j, warm=True):
                    b = m // BB
                    pe.wait_ge(placed, 2 * (m + 1))
                    pe.wait_ge(exT_kept, m + 1)
                    if warm and j == 0:
                        pe.wait_ge(fin_ready, m // 2)
                    o = psO[:, 0:DV]
                    for i in range(TB):
                        pe.matmul(o, exT[:, j, i, :], V[:, bass.ds(b * TB + i, 1), :].rearrange("p t d -> p (t d)"),
                                  start=(i == 0 and j == 0), stop=False)
                    pe.matmul(o, sumsT[:, j, :], weT[:], start=False, stop=(j == 1)).then_inc(o_done, 1)

                def tile(t, first=False, last=False):
                    for j in range(2):
                        m = t * 2 + j
                        pe.wait_ge(spread_ready, m + 1)
                        for gg in range(GROUPS):
                            broadcast(m, j, gg, warm=not (first and j == 0))
                            late = behind(m, j, gg, SCORE_LAG)
                            if makes(late, first, last):
                                scores(*late[0:3])
                            if gg == SCORE_LAG and not (first and j == 0):
                                combine(m - 1, 1 - j, warm=not first)
                            if gg == GROUPS - 2 and not (last and j == 1):
                                transpose_ex(m + 1, 1 - j)

                for n in range(2 * GROUPS - SCORE_LAG):
                    scores(n // GROUPS, n // GROUPS, n % GROUPS)
                transpose_ex(0, 0, warm=False)
                tile(0, first=True)
                with pe.Fori(1, NT - 1) as t:
                    tile(t)
                tile(NT - 1, last=True)
                combine(MB - 1, 1)

            @block.sync
            def _(sp):
                sp.sem_inc(out_done, 16)
                with sp.Fori(0, NT) as t:
                    sp.wait_ge(fin_ready, t + 1)
                    sp.dma_start(g.out_tiles[:, bass.ds(t, 1), :].rearrange("p t d -> p (t d)"),
                                 res[:, 0, :]).then_inc(out_done, 16)
                sp.wait_ge(out_done, 16 * NT + 16)


def _layout(inputs):
    import numpy as np

    def heads(w, width):
        return np.asarray(w).reshape(8, width, 128).transpose(2, 0, 1)

    def columns(b):
        b = np.asarray(b)
        return b.reshape(b.shape[0], -1, 128).transpose(2, 0, 1)

    def twice(w):
        return np.concatenate([w, w], axis=1)

    i = {k: np.asarray(v) for k, v in inputs.items()}
    return {
        "x": i["L0_attn_x"],
        "wqk": np.concatenate([heads(i["L0_attn_Wq"], 64), heads(i["L0_attn_Wk"], 64)], axis=2),
        "wv": i["L0_attn_Wv"].T,
        "gate0_w": i["L0_ffn_gate_w"], "gate0_b": i["L0_ffn_gate_b"],
        "w1": i["L0_ffn_w1"], "b1": columns(i["L0_ffn_b1"]), "w2": i["L0_ffn_w2"], "b2": i["L0_ffn_b2"],
        "a_wq": twice(i["L1_attn_Wq"].T), "a_wk": twice(i["L1_attn_Wk"].T),
        "a_phi": np.concatenate([i["L1_attn_Wphi"], i["L1_attn_Wphi"]]).reshape(128, 1),
        "a_wy": i["L1_attn_Wy_w"].T, "a_wyb": i["L1_attn_Wy_b"],
        "a_we": np.concatenate([i["L1_attn_We_w"].T, i["L1_attn_We_w"].T], axis=0), "a_web": i["L1_attn_We_b"],
        "gate1_w": i["L1_ffn_gate_w"], "gate1_b": i["L1_ffn_gate_b"],
        "e_w1": i["L1_ffn_w1"], "e_b1": columns(i["L1_ffn_b1"]),
        "e_w2": i["L1_ffn_w2"], "e_b2": columns(i["L1_ffn_b2"]),
        "e_wg": i["L1_ffn_wg"], "e_bg": columns(i["L1_ffn_bg"]),
        "e_w3": i["L1_ffn_w3"], "e_b3": i["L1_ffn_b3"],
    }


def kernel(**inputs):
    import numpy as np
    import concourse.bacc as bacc
    from concourse.bass_utils import run_bass_kernel_spmd

    nc = bacc.Bacc("TRN2", target_bir_lowering=False, num_devices=1)
    arrays, args = {}, {}
    for name, a in _layout(inputs).items():
        a = np.ascontiguousarray(a)
        arrays[f"in_{name}"] = a
        args[name] = nc.dram_tensor(f"in_{name}", a.shape, mybir.dt.from_np(a.dtype), kind="ExternalInput").ap()
    out = nc.dram_tensor("out_0", (B, N, D), F32, kind="ExternalOutput").ap()
    layers_kernel(nc, out=out, **args)
    r = run_bass_kernel_spmd(nc, [arrays], core_ids=[0])
    return r.results[0]["out_0"]
```

```python
from contextlib import ExitStack
import math

import concourse.bass as bass
from concourse import mybir

F32 = mybir.dt.float32
BF16 = mybir.dt.bfloat16
F16 = mybir.dt.float16
U32 = mybir.dt.uint32
ALU = mybir.AluOpType
ACT = mybir.ActivationFunctionType
AX = mybir.AxisListType

P = 128
B, N, D = 4, 512, 128
TOK = B * N
NT = TOK // P
TB = N // P
H, R = 8, 64
E = 8
CAP = 80
SLOTS = E * CAP
ST = SLOTS // P
F0 = 512
FT = F0 // P
DFF = 256
GT = DFF // P
A = 64
BLK = 64
PAIRS = BLK // 2
QUADS = 4
GROUPS = PAIRS // QUADS
LN_EPS = 1e-5
EPS_RHO = 1e-8
EPS_DEN = 1e-9
EX_LIFT = 15
DROPPED = 4096


class Memory:
    pass


class Chain:

    def __init__(self, eng, sem, base=0):
        self.eng, self.sem, self.base, self.n = eng, sem, base, 0

    def step(self, ins):
        self.n += 1
        ins.then_inc(self.sem, 1)
        return self.n

    def done(self, n=None):
        self.eng.wait_ge(self.sem, self.base + (self.n if n is None else n))

    def link(self, ins):
        self.step(ins)
        self.done()


def per_tile(ap, n):
    return ap.unsqueeze(2).to_broadcast([P, ap.shape[1], n])


def first_max(dve, chain, values, desc, top, tie, rank, mask):
    chain.link(dve.reduce_max(top, values, axis=AX.X))
    chain.link(dve.tensor_tensor(tie, values, per_tile(top, E), ALU.is_equal))
    chain.link(dve.tensor_tensor(tie, tie, desc, ALU.mult))
    chain.link(dve.reduce_max(rank, tie, axis=AX.X))
    chain.link(dve.tensor_tensor(mask, desc, per_tile(rank, E), ALU.is_equal))


def norm_scale(dve, chain, x, stats, mv, std, rstd, var_ready, std_ready):
    for t in range(NT):
        chain.step(dve.bn_stats(stats[:, t, :], x[:, t, :]))
    chain.done()
    for t in range(NT):
        chain.step(dve.bn_aggr(mv[:, t, :], stats[:, t, :]))
    chain.done()
    dve.tensor_scalar(std, mv[:, :, 1], LN_EPS, None, ALU.add).then_inc(var_ready, 1)
    dve.wait_ge(std_ready, 1)
    chain.link(dve.reciprocal(rstd, std))


def layers_kernel(nc, x, wqk, wv, gate0_w, gate0_b, w1, b1, w2, b2,
                  a_wq, a_wk, a_phi, a_wy, a_wyb, a_we, a_web,
                  gate1_w, gate1_b, e_w1, e_b1, e_w2, e_b2, e_wg, e_bg, e_w3, e_b3, out):
    g = Memory()
    g.gate0_w, g.gate0_b, g.gate1_w, g.gate1_b = gate0_w, gate0_b, gate1_w, gate1_b
    g.wqk, g.wv, g.w1, g.b1, g.w2, g.b2 = wqk, wv, w1, b1, w2, b2
    g.a_wq, g.a_wk, g.a_phi, g.a_wy, g.a_wyb, g.a_we, g.a_web = a_wq, a_wk, a_phi, a_wy, a_wyb, a_we, a_web
    g.e_w1, g.e_b1, g.e_w2, g.e_b2, g.e_wg, g.e_bg, g.e_w3, g.e_b3 = e_w1, e_b1, e_w2, e_b2, e_wg, e_bg, e_w3, e_b3
    with ExitStack() as ctx:
        def sb(name, shape, dt=F32):
            return ctx.enter_context(nc.sbuf_tensor(name, shape, dt))

        g.x1 = sb("x1", [P, NT, D])
        g.xnT = sb("xnT", [P, TOK])
        g.ident = sb("ident", [P, P])
        g.share = sb("share", [P, NT, E])
        g.arena = sb("arena", [P, 2 * PAIRS * N])
        g.taken = 0

        def take(*shape, dt=F32):
            n = math.prod(shape) * (4 if dt in (F32, U32) else 2) // 4
            v = g.arena[:, g.taken:g.taken + n]
            g.taken += n
            assert g.taken <= 2 * PAIRS * N
            if dt != F32:
                v = v.bitcast(dt)
            if len(shape) == 2:
                v = v.rearrange("p (a b) -> p a b", a=shape[0])
            elif len(shape) == 3:
                v = v.rearrange("p (a b c) -> p a b c", a=shape[0], b=shape[1])
            return v

        g.disp = nc.dram_tensor("disp", (SLOTS, D), F32, kind="Internal").ap()
        g.eout = nc.dram_tensor("eout", (SLOTS, D), F32, kind="Internal").ap()
        g.x_tiles = x.rearrange("b (t p) d -> p (b t) d", p=P)
        g.out_tiles = out.rearrange("b (t p) d -> p (b t) d", p=P)

        g.xn = take(NT, D)
        g.wqk_sb = take(H, P)
        g.wv_sb = take(H * D)
        g.w1_sb = take(E, F0)
        g.w2_sb = take(E, FT, D)
        g.b1_sb = take(E, FT)
        g.b2_sb = take(E, D)
        g.gathered = take(NT, D)

        with ExitStack() as routing:
            def scratch(name, shape, dt=F32):
                return routing.enter_context(nc.sbuf_tensor(name, shape, dt))

            g.desc = scratch("desc", [P, NT, E])
            g.lg = scratch("lg", [P, NT, E])
            g.tie = scratch("tie", [P, NT, E])
            g.mask1 = scratch("mask1", [P, NT, E])
            g.mask2 = scratch("mask2", [P, NT, E])
            g.top = scratch("top", [P, NT])
            g.rank = scratch("rank", [P, NT])
            g.stats = scratch("stats", [P, NT, 6])
            g.mv = scratch("mv", [P, NT, 2])
            g.std = scratch("std", [P, NT])
            g.rstd = scratch("rstd", [P, NT])
            g.coef = scratch("coef", [P, NT])
            g.gather_at = scratch("gather_at", [P, NT], U32)
            g.gateb = scratch("gateb", [P, E])

            normalise_and_route(nc, g)
            first_layer(nc, g, take)
            g.taken = 0
            second_route(nc, g, take)
        second_layer(nc, g, sb)


def normalise_and_route(nc, g):
    with ExitStack() as ctx:
        def sb(name, shape, dt=F32):
            return ctx.enter_context(nc.sbuf_tensor(name, shape, dt))

        def sem(name):
            return ctx.enter_context(nc.semaphore(name))

        tri = sb("tri", [P, P], BF16)
        ones = sb("ones", [P, P], BF16)
        place0 = sb("place0", [P, NT, E])
        past = sb("past", [P, NT])
        maskb = sb("maskb", [P, NT, E], BF16)
        ex = sb("ex", [P, NT, E])
        esum = sb("esum", [P, NT])
        pre = sb("pre", [P, 2, NT, E])
        queue = sb("queue", [P, NT, E])
        own = sb("own", [P, NT])
        keep = sb("keep", [P, NT])
        slot = sb("slot", [P, NT])
        scatter_at = sb("scatter_at", [P, NT], U32)
        zeros = sb("zeros", [P, ST * D])
        gw = sb("gw", [P, E])
        psX = ctx.enter_context(nc.psum_tensor("psX", [P, 4, 512], F32))
        psL = ctx.enter_context(nc.psum_tensor("psL", [P, NT, E], F32))
        psC = ctx.enter_context(nc.psum_tensor("psC", [P, 2, NT, E], F32))

        x_in, gate_in, w_in = sem("x_in"), sem("gate_in"), sem("w_in")
        pool_made, consts = sem("pool_made"), sem("consts")
        dve_steps, var_ready, std_ready = sem("dve_steps"), sem("var_ready"), sem("std_ready")
        xn_ready, xT_done, xT_kept = sem("xn_ready"), sem("xT_done"), sem("xT_kept")
        logits_done, shifted, exp_done = sem("logits_done"), sem("shifted"), sem("exp_done")
        mask_ready, counts_done, places = sem("mask_ready"), sem("counts_done"), sem("places")
        zero_ready, zero_out, scattered = sem("zero_ready"), sem("zero_out"), sem("scattered")
        block = ctx.enter_context(nc.Block())

        @block.sync
        def _(sp):
            sp.dma_start(g.x1[:], g.x_tiles).then_inc(x_in, 16)
            sp.dma_start(gw[:], g.gate0_w).then_inc(gate_in, 16)
            sp.dma_start(g.gateb[:], g.gate0_b.partition_broadcast(P)).then_inc(gate_in, 16)
            sp.wait_ge(zero_ready, 1)
            sp.dma_start(g.disp.rearrange("(t p) d -> p t d", p=P),
                         zeros[:].rearrange("p (t d) -> p t d", t=ST)).then_inc(zero_out, 16)
            sp.dma_start(g.wqk_sb, g.wqk).then_inc(w_in, 16)
            sp.dma_start(g.wv_sb, g.wv).then_inc(w_in, 16)
            sp.dma_start(g.w1_sb, g.w1.rearrange("e d f -> d e f")).then_inc(w_in, 16)
            sp.dma_start(g.w2_sb.rearrange("p e t d -> p (e t) d"),
                         g.w2.rearrange("e (t p) d -> p (e t) d", p=P)).then_inc(w_in, 16)
            sp.dma_start(g.b1_sb, g.b1).then_inc(w_in, 16)
            sp.dma_start(g.b2_sb[0:1, :, :], g.b2.rearrange("(o e) d -> o e d", o=1)).then_inc(w_in, 16)
            sp.wait_ge(w_in, 96)

        @block.gpsimd
        def _(pool):
            pool.memset(g.ident[:], 0.0).then_inc(pool_made, 1)
            pool.memset(tri[:], 1.0).then_inc(pool_made, 1)
            pool.memset(ones[:], 1.0).then_inc(consts, 1)
            pool.memset(zeros[:], 0.0).then_inc(zero_ready, 1)
            pool.wait_ge(pool_made, 2)
            pool.affine_select(out=g.ident[:], in_=g.ident[:], compare_op=ALU.not_equal, fill=1.0,
                               base=0, pattern=[[-1, P]], channel_multiplier=1).then_inc(consts, 1)
            pool.affine_select(out=tri[:], in_=tri[:], compare_op=ALU.is_ge, fill=0.0,
                               base=0, pattern=[[1, P]], channel_multiplier=-1).then_inc(consts, 1)
            pool.iota(g.desc[:], pattern=[[0, NT], [-1, E]], base=E, channel_multiplier=0,
                      allow_small_or_imprecise_dtypes=True).then_inc(consts, 1)
            pool.iota(place0[:], pattern=[[0, NT], [CAP, E]], base=-1, channel_multiplier=0,
                      allow_small_or_imprecise_dtypes=True).then_inc(consts, 1)
            pool.iota(past[:], pattern=[[P, NT]], base=DROPPED, channel_multiplier=1,
                      allow_small_or_imprecise_dtypes=True).then_inc(consts, 1)
            pool.wait_ge(places, 2)
            pool.wait_ge(zero_out, 16)
            pool.wait_ge(xn_ready, NT)
            for t in range(NT):
                pool.indirect_dma_start(
                    g.disp, bass.IndirectOffsetOnAxis(ap=scatter_at[:, t:t + 1], axis=0),
                    g.xn[:, t, :], None, bounds_check=SLOTS - 1, oob_is_err=False).then_inc(scattered, 16)
            pool.wait_ge(scattered, 16 * NT)

        @block.scalar
        def _(act):
            act.wait_ge(var_ready, 1)
            act.activation(g.std[:], g.std[:], ACT.Sqrt).then_inc(std_ready, 1)
            for c in range(4):
                act.wait_ge(xT_done, c + 1)
                act.activation(g.xnT[:, c * 512:(c + 1) * 512], psX[:, c, :], ACT.Copy).then_inc(xT_kept, 1)
            act.wait_ge(shifted, 1)
            act.activation(ex[:], ex[:], ACT.Exp).then_inc(exp_done, 1)

        @block.vector
        def _(dve):
            chain = Chain(dve, dve_steps)
            dve.wait_ge(x_in, 16)
            norm_scale(dve, chain, g.x1, g.stats, g.mv, g.std[:], g.rstd[:], var_ready, std_ready)
            for t in range(NT):
                dve.tensor_scalar(g.xn[:, t, :], g.x1[:, t, :], g.mv[:, t, 0:1], g.rstd[:, t:t + 1],
                                  ALU.subtract, ALU.mult).then_inc(xn_ready, 1)
            dve.wait_ge(logits_done, 1)
            dve.wait_ge(gate_in, 32)
            dve.wait_ge(consts, 6)
            chain.link(dve.tensor_tensor(g.lg[:], psL[:], g.gateb[:].unsqueeze(1).to_broadcast([P, NT, E]), ALU.add))
            first_max(dve, chain, g.lg[:], g.desc[:], g.top[:], g.tie[:], g.rank[:], g.mask1[:])
            dve.tensor_copy(maskb[:], g.mask1[:]).then_inc(mask_ready, 1)
            dve.tensor_tensor(ex[:], g.lg[:], per_tile(g.top[:], E), ALU.subtract).then_inc(shifted, 1)
            dve.wait_ge(counts_done, 1)
            chain.link(dve.tensor_copy(pre[:, 0], psC[:, 1]))
            at = 0
            for k in (1, 2, 4, 8):
                chain.link(dve.tensor_copy(pre[:, 1 - at, 0:k], pre[:, at, 0:k]))
                chain.link(dve.tensor_tensor(pre[:, 1 - at, k:NT], pre[:, at, k:NT], pre[:, at, 0:NT - k], ALU.add))
                at = 1 - at
            chain.link(dve.tensor_tensor(queue[:], pre[:, at], psC[:, 1], ALU.subtract))
            chain.link(dve.tensor_tensor(queue[:], queue[:], psC[:, 0], ALU.add))
            chain.link(dve.tensor_tensor(g.tie[:], queue[:], g.mask1[:], ALU.mult))
            chain.link(dve.reduce_sum(own[:], g.tie[:], axis=AX.X))
            chain.link(dve.tensor_scalar(keep[:], own[:], float(CAP), None, ALU.is_le))
            chain.link(dve.tensor_tensor(queue[:], queue[:], place0[:], ALU.add))
            chain.link(dve.tensor_tensor(queue[:], queue[:], g.mask1[:], ALU.mult))
            chain.link(dve.reduce_sum(slot[:], queue[:], axis=AX.X))
            chain.link(dve.tensor_tensor(own[:], slot[:], keep[:], ALU.mult))
            dve.tensor_copy(g.gather_at[:], own[:]).then_inc(places, 1)
            chain.link(dve.tensor_tensor(slot[:], slot[:], past[:], ALU.subtract))
            chain.link(dve.tensor_tensor(slot[:], slot[:], keep[:], ALU.mult))
            chain.link(dve.tensor_tensor(slot[:], slot[:], past[:], ALU.add))
            dve.tensor_copy(scatter_at[:], slot[:]).then_inc(places, 1)
            dve.wait_ge(exp_done, 1)
            chain.link(dve.reduce_sum(esum[:], ex[:], axis=AX.X))
            chain.link(dve.reciprocal(esum[:], esum[:]))
            chain.link(dve.tensor_tensor(g.coef[:], esum[:], keep[:], ALU.mult))

        @block.tensor
        def _(pe):
            pe.wait_ge(consts, 6)
            for t in range(NT):
                pe.wait_ge(xn_ready, t + 1)
                ins = pe.transpose(psX[:, t // TB, (t % TB) * P:(t % TB + 1) * P], g.xn[:, t, :], g.ident[:])
                if t % TB == TB - 1:
                    ins.then_inc(xT_done, 1)
            pe.wait_ge(gate_in, 32)
            for t in range(NT):
                if t % TB == 0:
                    pe.wait_ge(xT_kept, t // TB + 1)
                ins = pe.matmul(psL[:, t, :], g.xnT[:, t * P:(t + 1) * P], gw[:], start=True, stop=True)
            ins.then_inc(logits_done, 1)
            pe.wait_ge(mask_ready, 1)
            pe.matmul(psC[:, 0].rearrange("p t e -> p (t e)"), tri[:], maskb[:].rearrange("p t e -> p (t e)"),
                      start=True, stop=True)
            pe.matmul(psC[:, 1].rearrange("p t e -> p (t e)"), ones[:], maskb[:].rearrange("p t e -> p (t e)"),
                      start=True, stop=True).then_inc(counts_done, 1)


def first_layer(nc, g, take):
    STEPS = H * TB
    with ExitStack() as ctx:
        def sem(name):
            return ctx.enter_context(nc.semaphore(name))

        xTb = take(N)
        V = take(TB, H * D)
        qT = take(2, N)
        kT = take(2, N)
        ex = take(3, N)
        pT = take(2, TB, N)
        rows = take(ST, D)
        rowsT = take(SLOTS)
        hT = take(2, FT, CAP)
        eo = take(E, D)
        oT = take(N)
        one_row = take(P)
        nmax = take(4)
        den = take(4)
        rden = take(4)
        ps = ctx.enter_context(nc.psum_tensor("ps0", [P, 8, 512], F32))
        SB, TBK, PJ, AV = (0, 1, 2), (3, 4), 5, 6

        rows_in, prep, zeroed = sem("rows_in"), sem("prep"), sem("zeroed")
        rowsT_done, rowsT_kept = sem("rowsT_done"), sem("rowsT_kept")
        h_done, h_kept, eo_done, eo_kept = sem("h_done"), sem("h_kept"), sem("eo_done"), sem("eo_kept")
        eo_out, gathered_in = sem("eo_out"), sem("gathered_in")
        row_staged, v_done, v_kept = sem("row_staged"), sem("v_done"), sem("v_kept")
        qk_done, qk_kept = sem("qk_done"), sem("qk_kept")
        s_done, nmax_ready, exp_ready = sem("s_done"), sem("nmax_ready"), sem("exp_ready")
        rden_ready, p_ready = sem("rden_ready"), sem("p_ready")
        pT_done, pT_kept, av_done = sem("pT_done"), sem("pT_kept"), sem("av_done")
        oT_kept, o_done, o_added = sem("oT_kept"), sem("o_done"), sem("o_added")
        block = ctx.enter_context(nc.Block())

        @block.sync
        def _(sp):
            sp.dma_start(rows, g.disp.rearrange("(t p) d -> p t d", p=P)).then_inc(rows_in, 16)
            sp.wait_ge(eo_kept, E)
            sp.dma_start(g.eout.rearrange("(e c) d -> c e d", c=CAP), eo[0:CAP, :, :]).then_inc(eo_out, 16)
            sp.wait_ge(eo_out, 16)

        @block.gpsimd
        def _(pool):
            pool.memset(one_row[0:1, :], 1.0).then_inc(prep, 1)
            pool.memset(qT[R:P, :, :], 0.0).then_inc(zeroed, 1)
            pool.memset(kT[R:P, :, :], 0.0).then_inc(zeroed, 1)
            pool.wait_ge(eo_out, 16)
            for t in range(NT):
                pool.indirect_dma_start(
                    g.gathered[:, t, :], None, g.eout,
                    bass.IndirectOffsetOnAxis(ap=g.gather_at[:, t:t + 1], axis=0)).then_inc(gathered_in, 16)
            pool.wait_ge(gathered_in, 16 * NT)

        @block.scalar
        def _(act):
            act.wait_ge(rowsT_done, 1)
            act.activation(rowsT[:, 0:512], ps[:, 0, :], ACT.Copy).then_inc(rowsT_kept, 1)
            act.activation(rowsT[:, 512:SLOTS], ps[:, 1, 0:SLOTS - 512], ACT.Copy).then_inc(rowsT_kept, 1)
            for e in range(E):
                act.wait_ge(h_done, e + 1)
                if e >= 2:
                    act.wait_ge(eo_done, e - 1)
                for f in range(FT):
                    act.activation(hT[:, e % 2, f, :], ps[:, 2 + e % 2, f * CAP:(f + 1) * CAP],
                                   ACT.Gelu_apprx_tanh, bias=g.b1_sb[:, e, f:f + 1]).then_inc(h_kept, 1)
            with act.Fori(0, B) as b:
                for j in range(2 * TB):
                    act.wait_ge(v_done, b * 2 * TB + j + 1)
                    if j % 2 == 0:
                        act.activation(V[:, j // 2, 0:512], ps[:, TBK[0], :], ACT.Copy).then_inc(v_kept, 1)
                    else:
                        act.activation(V[:, j // 2, 512:1024], ps[:, TBK[1], :], ACT.Copy).then_inc(v_kept, 1)

                def exp_step(s):
                    act.wait_ge(nmax_ready, b * STEPS + s + 1)
                    if s >= 3:
                        act.wait_ge(pT_done, b * STEPS + s - 2)
                    act.activation(ex[:, s % 3, :], ps[:, SB[s % 3], :], ACT.Exp, bias=nmax[:, s % 4:s % 4 + 1],
                                   accum_out=den[:, s % 4:s % 4 + 1]).then_inc(exp_ready, 1)

                def keep_pT(s):
                    h, t = s // TB, s % TB
                    act.wait_ge(pT_done, b * STEPS + s + 1)
                    if h >= 2 and t == 0:
                        act.wait_ge(av_done, b * H + h - 1)
                    act.activation(pT[:, h % 2, :, t * P:(t + 1) * P],
                                   ps[:, TBK[s % 2], :].rearrange("p (m n) -> p m n", m=TB),
                                   ACT.Copy).then_inc(pT_kept, 1)

                for s in range(STEPS):
                    exp_step(s)
                    if s >= 2:
                        keep_pT(s - 2)
                keep_pT(STEPS - 2)
                keep_pT(STEPS - 1)

        @block.vector
        def _(dve):
            for e in range(E):
                dve.wait_ge(eo_done, e + 1)
                dve.tensor_copy(eo[0:CAP, e, :], ps[0:CAP, 4 + e % 2, 0:D]).then_inc(eo_kept, 1)
            dve.sem_inc(o_added, 1)
            with dve.Fori(0, B) as b:
                dve.wait_ge(o_done, b + 1)
                dve.tensor_copy(xTb, g.xnT[:, bass.ds(b * N, N)]).then_inc(row_staged, 1)

                def keep_qk(h):
                    dve.wait_ge(qk_done, b * H + h + 1)
                    if h >= 2:
                        dve.wait_ge(s_done, b * STEPS + (h - 1) * TB)
                    dve.tensor_copy(qT[0:R, h % 2, :], ps[0:R, PJ, :]).then_inc(qk_kept, 1)
                    dve.tensor_copy(kT[0:R, h % 2, :], ps[R:P, PJ, :]).then_inc(qk_kept, 1)

                def max_step(s):
                    dve.wait_ge(s_done, b * STEPS + s + 1)
                    if s >= 4:
                        dve.wait_ge(exp_ready, b * STEPS + s - 3)
                    dve.reduce_max(nmax[:, s % 4:s % 4 + 1], ps[:, SB[s % 3], :], axis=AX.X,
                                   negate=True).then_inc(nmax_ready, 1)

                def norm_step(s):
                    dve.wait_ge(exp_ready, b * STEPS + s + 1)
                    dve.reciprocal(rden[:, s % 4:s % 4 + 1], den[:, s % 4:s % 4 + 1]).then_inc(rden_ready, 1)
                    dve.wait_ge(rden_ready, b * STEPS + s + 1)
                    dve.tensor_scalar(ex[:, s % 3, :], ex[:, s % 3, :], rden[:, s % 4:s % 4 + 1], None,
                                      ALU.mult).then_inc(p_ready, 1)

                keep_qk(0)
                for s in range(STEPS):
                    if s % TB == 1 and s // TB + 1 < H:
                        keep_qk(s // TB + 1)
                    max_step(s)
                    if s >= 1:
                        norm_step(s - 1)
                norm_step(STEPS - 1)
                dve.wait_ge(av_done, (b + 1) * H)
                dve.tensor_copy(oT, ps[:, AV, :]).then_inc(oT_kept, 1)
                dve.wait_ge(o_done, b + 2)
                xr = g.x1[:, bass.ds(b * TB, TB), :]
                dve.tensor_tensor(xr, xr, ps[:, TBK[0], :].rearrange("p (t d) -> p t d", t=TB),
                                  ALU.add).then_inc(o_added, 1)

        @block.tensor
        def _(pe):
            pe.wait_ge(rows_in, 16)
            for t in range(ST):
                ins = pe.transpose(ps[:, t // 4, (t % 4) * P:(t % 4 + 1) * P], rows[:, t, :], g.ident[:])
            ins.then_inc(rowsT_done, 1)
            pe.wait_ge(rowsT_kept, 2)
            pe.wait_ge(prep, 1)

            def up(e):
                if e >= 2:
                    pe.wait_ge(h_kept, FT * (e - 1))
                for f in range(FT):
                    ins = pe.matmul(ps[:, 2 + e % 2, f * CAP:(f + 1) * CAP], g.w1_sb[:, e, f * P:(f + 1) * P],
                                    rowsT[:, e * CAP:(e + 1) * CAP], start=True, stop=True)
                ins.then_inc(h_done, 1)

            def down(e):
                pe.wait_ge(h_kept, FT * (e + 1))
                if e >= 2:
                    pe.wait_ge(eo_kept, e - 1)
                pe.matmul(ps[0:CAP, 4 + e % 2, 0:D], one_row[0:1, 0:CAP], g.b2_sb[0:1, e, :], start=True, stop=False)
                for f in range(FT):
                    ins = pe.matmul(ps[0:CAP, 4 + e % 2, 0:D], hT[:, e % 2, f, :], g.w2_sb[:, e, f, :],
                                    start=False, stop=(f == FT - 1))
                ins.then_inc(eo_done, 1)

            up(0)
            for e in range(E):
                if e + 1 < E:
                    up(e + 1)
                down(e)
            pe.wait_ge(eo_kept, E)
            pe.wait_ge(zeroed, 2)
            pe.sem_inc(o_done, 1)
            with pe.Fori(0, B) as b:
                pe.wait_ge(row_staged, b + 1)
                pe.wait_ge(o_added, b + 1)
                for j in range(2 * TB):
                    if j >= 2:
                        pe.wait_ge(v_kept, b * 2 * TB + j - 1)
                    pe.matmul(ps[:, TBK[j % 2], :], xTb[:, (j // 2) * P:(j // 2 + 1) * P],
                              g.wv_sb[:, (j % 2) * 512:(j % 2 + 1) * 512], start=True, stop=True).then_inc(v_done, 1)

                def project(h):
                    if h >= 1:
                        pe.wait_ge(qk_kept, b * 2 * H + 2 * h)
                    pe.matmul(ps[:, PJ, :], g.wqk_sb[:, h, :], xTb, start=True, stop=True).then_inc(qk_done, 1)

                def scores(s):
                    h, t = s // TB, s % TB
                    if t == 0:
                        pe.wait_ge(qk_kept, b * 2 * H + 2 * (h + 1))
                    if s >= 3:
                        pe.wait_ge(exp_ready, b * STEPS + s - 2)
                    pe.matmul(ps[:, SB[s % 3], :], qT[:, h % 2, t * P:(t + 1) * P], kT[:, h % 2, :],
                              start=True, stop=True).then_inc(s_done, 1)

                def transpose_p(s):
                    pe.wait_ge(p_ready, b * STEPS + s + 1)
                    if s >= 2:
                        pe.wait_ge(pT_kept, b * STEPS + s - 1)
                    for m in range(TB):
                        ins = pe.transpose(ps[:, TBK[s % 2], m * P:(m + 1) * P], ex[:, s % 3, m * P:(m + 1) * P],
                                           g.ident[:])
                    ins.then_inc(pT_done, 1)

                def weigh(h):
                    pe.wait_ge(pT_kept, b * STEPS + (h + 1) * TB)
                    for m in range(TB):
                        ins = pe.matmul(ps[:, AV, :], V[:, m, h * D:(h + 1) * D], pT[:, h % 2, m, :],
                                        start=(h == 0 and m == 0), stop=(h == H - 1 and m == TB - 1))
                    ins.then_inc(av_done, 1)

                project(0)
                pe.wait_ge(v_kept, (b + 1) * 2 * TB)
                for s in range(STEPS):
                    scores(s)
                    if s % TB == 0 and s // TB + 1 < H:
                        project(s // TB + 1)
                    if s >= 2:
                        transpose_p(s - 2)
                        if s >= TB + 2 and (s - 3) % TB == TB - 1:
                            weigh((s - 3) // TB)
                transpose_p(STEPS - 2)
                transpose_p(STEPS - 1)
                weigh(H - 1)
                pe.wait_ge(oT_kept, b + 1)
                for t in range(TB):
                    ins = pe.transpose(ps[:, TBK[0], t * P:(t + 1) * P], oT[:, t * P:(t + 1) * P], g.ident[:])
                ins.then_inc(o_done, 1)


def second_route(nc, g, take):
    with ExitStack() as ctx:
        def sb(name, shape, dt=F32):
            return ctx.enter_context(nc.sbuf_tensor(name, shape, dt))

        def sem(name):
            return ctx.enter_context(nc.semaphore(name))

        xn = take(NT, D)
        shareT = take(TOK)
        gw = take(E)
        b3 = take(D)
        p1 = take(NT)
        p2 = take(NT)
        top2 = take(NT)
        term = take(NT, E)
        psX = ctx.enter_context(nc.psum_tensor("psX1", [P, 4, 512], F32))
        psL = ctx.enter_context(nc.psum_tensor("psL1", [P, NT, E], F32))
        gate_in, r_steps = sem("gate1_in"), sem("r_steps")
        var_ready, std_ready = sem("var1_ready"), sem("std1_ready")
        xn_ready, xT_done, xT_kept = sem("xn1_ready"), sem("xT1_done"), sem("xT1_kept")
        logits_done, gap_ready, exp_done = sem("logits1_done"), sem("gap_ready"), sem("exp1_done")
        share_ready, shareT_done, shareT_kept = sem("share_ready"), sem("shareT_done"), sem("shareT_kept")
        b3_done, b3_added = sem("b3_done"), sem("b3_added")
        block = ctx.enter_context(nc.Block())

        @block.sync
        def _(sp):
            sp.dma_start(gw, g.gate1_w).then_inc(gate_in, 16)
            sp.dma_start(g.gateb[:], g.gate1_b.partition_broadcast(P)).then_inc(gate_in, 16)
            sp.dma_start(b3[0:E, :], g.e_b3).then_inc(gate_in, 16)

        @block.scalar
        def _(act):
            act.wait_ge(var_ready, 1)
            act.activation(g.std[:], g.std[:], ACT.Sqrt).then_inc(std_ready, 1)
            for c in range(4):
                act.wait_ge(xT_done, c + 1)
                act.activation(g.xnT[:, c * 512:(c + 1) * 512], psX[:, c, :], ACT.Copy).then_inc(xT_kept, 1)
            act.wait_ge(gap_ready, 1)
            act.activation(p2, p2, ACT.Exp).then_inc(exp_done, 1)
            act.wait_ge(shareT_done, 1)
            act.activation(shareT[0:E, :].rearrange("p (c n) -> p c n", c=4), psX[0:E, :, :],
                           ACT.Copy).then_inc(shareT_kept, 1)

        @block.vector
        def _(dve):
            chain = Chain(dve, r_steps)
            for t in range(NT):
                chain.step(dve.scalar_tensor_tensor(g.x1[:, t, :], g.gathered[:, t, :], g.coef[:, t:t + 1],
                                                    g.x1[:, t, :], ALU.mult, ALU.add))
            chain.done()
            norm_scale(dve, chain, g.x1, g.stats, g.mv, g.std[:], g.rstd[:], var_ready, std_ready)
            for t in range(NT):
                dve.tensor_scalar(xn[:, t, :], g.x1[:, t, :], g.mv[:, t, 0:1], g.rstd[:, t:t + 1],
                                  ALU.subtract, ALU.mult).then_inc(xn_ready, 1)
            dve.wait_ge(logits_done, 1)
            chain.link(dve.tensor_tensor(g.lg[:], psL[:], g.gateb[:].unsqueeze(1).to_broadcast([P, NT, E]), ALU.add))
            first_max(dve, chain, g.lg[:], g.desc[:], g.top[:], g.tie[:], g.rank[:], g.mask1[:])
            chain.link(dve.scalar_tensor_tensor(g.lg[:], g.mask1[:], -1e30, g.lg[:], ALU.mult, ALU.add))
            first_max(dve, chain, g.lg[:], g.desc[:], top2, g.tie[:], g.rank[:], g.mask2[:])
            dve.tensor_tensor(p2, top2, g.top[:], ALU.subtract).then_inc(gap_ready, 1)
            dve.wait_ge(exp_done, 1)
            chain.link(dve.tensor_scalar(p1, p2, 1.0, None, ALU.add))
            chain.link(dve.reciprocal(p1, p1))
            chain.link(dve.tensor_tensor(p2, p2, p1, ALU.mult))
            chain.link(dve.tensor_tensor(term, g.mask1[:], per_tile(p1, E), ALU.mult))
            chain.link(dve.tensor_tensor(g.mask2[:], g.mask2[:], per_tile(p2, E), ALU.mult))
            dve.tensor_tensor(g.share[:], term, g.mask2[:], ALU.add).then_inc(share_ready, 1)
            for c in range(4):
                dve.wait_ge(b3_done, c + 1)
                xr = g.x1[:, c * TB:(c + 1) * TB, :]
                dve.tensor_tensor(xr, xr, psX[:, c, :].rearrange("p (t d) -> p t d", t=TB), ALU.add).then_inc(b3_added, 1)

        @block.tensor
        def _(pe):
            for t in range(NT):
                pe.wait_ge(xn_ready, t + 1)
                ins = pe.transpose(psX[:, t // TB, (t % TB) * P:(t % TB + 1) * P], xn[:, t, :], g.ident[:])
                if t % TB == TB - 1:
                    ins.then_inc(xT_done, 1)
            pe.wait_ge(gate_in, 48)
            for t in range(NT):
                if t % TB == 0:
                    pe.wait_ge(xT_kept, t // TB + 1)
                ins = pe.matmul(psL[:, t, :], g.xnT[:, t * P:(t + 1) * P], gw, start=True, stop=True)
            ins.then_inc(logits_done, 1)
            pe.wait_ge(share_ready, 1)
            for t in range(NT):
                ins = pe.transpose(psX[0:E, t // TB, (t % TB) * P:(t % TB + 1) * P], g.share[:, t, :], g.ident[:])
            ins.then_inc(shareT_done, 1)
            pe.wait_ge(shareT_kept, 1)
            for t in range(NT):
                ins = pe.matmul(psX[:, t // TB, (t % TB) * P:(t % TB + 1) * P], shareT[0:E, t * P:(t + 1) * P],
                                b3[0:E, :], start=True, stop=True)
                if t % TB == TB - 1:
                    ins.then_inc(b3_done, 1)


def second_layer(nc, g, sb):
    x1, xnT, ident = g.x1, g.xnT, g.ident
    share = g.share[:].rearrange("p t e -> p (t e)")
    MB = TOK // BLK
    BB = N // BLK
    ON_ACT = [2, 2, 2, 2, 1, 1, 2, 1]
    ON_DVE = [QUADS - n for n in ON_ACT]
    BANKS = 3
    DV = D + 1
    with ExitStack() as ctx:
        def sem(name):
            return ctx.enter_context(nc.semaphore(name))

        feat = g.arena[:].rearrange("p (s k n) -> p s k n", s=2, k=PAIRS)
        kT = sb("kT2", [P, TOK])
        q2 = sb("q2", [P, TOK // 2])
        V = sb("V2", [P, NT, DV])
        phi_cols = sb("phi_cols", [P, GROUPS, 32])
        sel = sb("sel", [P, GROUPS, QUADS, P], F16)
        weT = sb("weT", [P, DV])
        bias_out = sb("bias_out", [P, D])
        split_by = sb("split_by", [P, 1])
        eps = sb("eps", [P, 1])
        ex = sb("ex2", [P, 2, N])
        exh = sb("exh", [P, N], F16)
        part = sb("part", [P, N], F16)
        spread = sb("spread", [P, 2, N], F16)
        exT = sb("exT", [P, 2, TB, P])
        nmax = sb("nmax2", [P, 2])
        shift = sb("shift", [P, 2])
        sums = sb("sums", [P, 2, GROUPS, QUADS])
        sumsT = sb("sumsT", [P, 2, P])
        den = sb("den2", [P, 2])
        b1, b2, bg = sb("b1e", [P, GT, E]), sb("b2e", [P, GT, E]), sb("bge", [P, GT, E])
        w1 = sb("w1e", [P, DFF])
        w2 = sb("w2e", [P, DFF])
        wg = sb("wge", [P, GT * DFF])
        w3 = sb("w3e", [P, GT * D])
        left = sb("left", [P, GT, N])
        z = sb("z", [P, GT, N])
        s = sb("s", [P, GT, N])

        ps = ctx.enter_context(nc.psum_tensor("ps2", [P, 8, 512], F32))
        psS, psB = ps[:, 0, :], ps[:, 2:5, :]
        psT = psO = ps[:, 5, :]
        psX, psY, psZ = ps[:, 6, :], ps[:, 7, :], ps[:, 1, :]

        wq, wk = feat[:, 1, 0, 0:P], feat[:, 1, 0, P:2 * P]
        wy, wyb = feat[:, 1, 0, 2 * P:3 * P], feat[:, 1, 0, 3 * P:4 * P]
        web, phi = feat[:, 1, 1, 0:D], feat[:, 1, 1, D:D + 1]
        rho = feat[:, 1, 2, 0:P]
        mask_c = feat[:, 1, 3, 0:QUADS]

        w2_in, c2_made, c2_ready, prep = sem("w2_in"), sem("c2_made"), sem("c2_ready"), sem("prep2")
        pq_done, pq_kept = sem("pq_done"), sem("pq_kept")
        feat_ready, act_feat, e_ready = sem("feat_ready"), sem("act_feat"), sem("e_ready")
        s_done, max_ready, shift_ready = sem("s2_done"), sem("max_ready"), sem("shift_ready")
        ex_ready, exh_ready, split_step, spread_ready = sem("ex_ready"), sem("exh_ready"), sem("split_step"), sem("spread_ready")
        bc_done, reduced, placed = sem("bc_done"), sem("reduced"), sem("placed")
        exT_done, exT_kept = sem("exT_done"), sem("exT_kept")
        o_done, fin_steps, fin_ready, out_done = sem("o2_done"), sem("fin_steps"), sem("fin_ready"), sem("out_done")
        w12_in, wg_in, w3_in = sem("w12_in"), sem("wg_in"), sem("w3_in")
        left_done, right_done, left_kept, z_ready = sem("left_done"), sem("right_done"), sem("left_kept"), sem("z_ready")
        gate_done, s_ready, y_done, y_added = sem("gate_done"), sem("s_ready"), sem("y_done"), sem("y_added")
        act_passed, pool_passed = sem("act_passed"), sem("pool_passed")

        with nc.Block() as block:
            @block.sync
            def _(sp):
                sp.dma_start(wq, g.a_wq).then_inc(w2_in, 16)
                sp.dma_start(wk, g.a_wk).then_inc(w2_in, 16)
                sp.dma_start(wy, g.a_wy).then_inc(w2_in, 16)
                sp.dma_start(wyb, g.a_wyb.partition_broadcast(P)).then_inc(w2_in, 16)
                sp.dma_start(web, g.a_web.partition_broadcast(P)).then_inc(w2_in, 16)
                sp.dma_start(phi, g.a_phi).then_inc(w2_in, 16)
                sp.dma_start(weT[:, 0:D], g.a_we).then_inc(w2_in, 16)
                for v, src in ((b1, g.e_b1), (b2, g.e_b2), (bg, g.e_bg)):
                    sp.dma_start(v[:], src).then_inc(w2_in, 16)
                sp.wait_ge(w2_in, 10 * 16)

            @block.gpsimd
            def _(pool):
                pool.memset(sel[:], 0.0).then_inc(c2_made, 1)
                pool.memset(mask_c, 1.0).then_inc(c2_made, 1)
                pool.memset(phi_cols[:], 0.0).then_inc(c2_ready, 1)
                pool.memset(weT[:, D:DV], 0.0).then_inc(c2_ready, 1)
                pool.memset(V[:, :, D:DV], 1.0).then_inc(c2_ready, 1)
                pool.memset(sumsT[:], 0.0).then_inc(c2_ready, 1)
                pool.memset(exT[:], 0.0).then_inc(c2_ready, 1)
                pool.memset(eps[:], EPS_RHO).then_inc(c2_ready, 1)
                pool.memset(rho, -math.sqrt(EPS_RHO)).then_inc(c2_ready, 1)
                pool.wait_ge(c2_made, 2)
                v = sel[:].rearrange("p g c (h a) -> p g c h a", h=2)
                for gg in range(GROUPS):
                    for half in range(2):
                        if half:
                            pool.wait_ge(prep, gg + 1)
                        ins = pool.affine_select(out=v[:, gg], in_=v[:, gg], compare_op=ALU.not_equal, fill=1.0,
                                                 base=-2 * gg - 16 * half, pattern=[[-32, QUADS], [-1, 2], [0, A]],
                                                 channel_multiplier=1)
                        ins.then_inc(c2_ready if half else prep, 1)
                pool.affine_select(out=mask_c, in_=mask_c, compare_op=ALU.is_ge, fill=0.0, base=-16,
                                   pattern=[[-32, QUADS]], channel_multiplier=1).then_inc(c2_made, 1)
                pool.wait_ge(c2_made, 3)
                pool.affine_select(out=mask_c, in_=mask_c, compare_op=ALU.is_ge, fill=0.0, base=31,
                                   pattern=[[32, QUADS]], channel_multiplier=-1).then_inc(c2_ready, 1)

            CONSTS = 7 + GROUPS + 1

            @block.vector
            def _(dve):
                dve.wait_ge(w2_in, 10 * 16)
                dve.wait_ge(c2_ready, CONSTS)
                flat = phi_cols[:].rearrange("p g n -> p (g n)")
                for h in range(2):
                    for d in range(2):
                        at = 16 * d + h
                        col = flat[h * A:(h + 1) * A, at:at + 34 * (GROUPS - 1) + 1:34]
                        dve.tensor_copy(col, phi[h * A:(h + 1) * A, :].to_broadcast([A, GROUPS])).then_inc(pq_kept, 1)
                dve.tensor_reduce(split_by[:], mask_c, axis=AX.X, op=ALU.add, negate=True).then_inc(pq_kept, 1)
                n = 0
                for c in range(B):
                    dve.wait_ge(pq_done, 3 * c + 1)
                    qv = ps[:, 0, :].rearrange("p (n h) -> p n h", h=2)
                    for h in range(2):
                        dve.tensor_copy(q2[h * A:(h + 1) * A, c * N // 2:(c + 1) * N // 2],
                                        qv[h * A:(h + 1) * A, :, h]).then_inc(pq_kept, 1)
                    dve.wait_ge(pq_done, 3 * c + 2)
                    dve.tensor_copy(kT[:, c * N:(c + 1) * N], ps[:, 1, :]).then_inc(pq_kept, 1)
                    dve.wait_ge(pq_done, 3 * c + 3)
                    dve.tensor_tensor(V[:, c * TB:(c + 1) * TB, 0:D], ps[:, 2 + c, :].rearrange("p (t d) -> p t d", t=TB),
                                      wyb.unsqueeze(1).to_broadcast([P, TB, D]), ALU.add).then_inc(pq_kept, 1)
                dve.wait_ge(pq_done, 3 * B + 1)
                dve.tensor_tensor(bias_out[:], ps[:, 6, 0:D], web, ALU.add).then_inc(pq_kept, 1)

            @block.tensor
            def _(pe):
                pe.wait_ge(w2_in, 10 * 16)
                pe.wait_ge(c2_ready, CONSTS)
                for c in range(B):
                    if c:
                        pe.wait_ge(pq_kept, 5 + 4 * c)
                    xc = xnT[:, c * N:(c + 1) * N]
                    pe.matmul(ps[:, 0, :], wq, xc, start=True, stop=True).then_inc(pq_done, 1)
                    pe.matmul(ps[:, 1, :], wk, xc, start=True, stop=True).then_inc(pq_done, 1)
                    for i in range(TB):
                        t = c * TB + i
                        ins = pe.matmul(ps[:, 2 + c, i * D:(i + 1) * D], xnT[:, t * P:(t + 1) * P], wy,
                                        start=True, stop=True)
                    ins.then_inc(pq_done, 1)
                pe.matmul(ps[:, 6, 0:D], rho[0:A, :], weT[0:A, 0:D], start=True, stop=True).then_inc(pq_done, 1)

        FEATURE_LAG = 1
        SCORES_AT = {(6, 2): 0, (7, 0): 1, (7, 2): 2, (0, 0): 3, (0, 2): 4, (1, 0): 5, (2, 2): 6, (3, 2): 7}

        LEFT_AT, EXT_AT = (7, 1), 7

        def behind(m, j, gg, lag):
            if gg >= lag:
                return m + 2, j, gg - lag, 2
            return m + 1, 1 - j, gg - lag + GROUPS, 1

        def makes(late, first, last):
            return not last or (late[1] == 1 and late[3] == 1)

        def slot_parts(m):
            return m // BB, m * PAIRS

        with nc.Block() as block:
            @block.vector
            def _(dve):
                def feature(m, j, gg, c):
                    if c < ON_DVE[gg]:
                        b, pair0 = slot_parts(m)
                        dve.tensor_scalar(feat[:, j, QUADS * gg + c, :], kT[:, bass.ds(b * N, N)],
                                          q2[:, bass.ds(pair0 + GROUPS * c + gg, 1)], 0.0,
                                          ALU.add, ALU.max).then_inc(feat_ready, 1)

                def largest(m, j):
                    dve.wait_ge(s_done, m + 1)
                    dve.reduce_max(nmax[:, j:j + 1], psS, axis=AX.X, negate=True).then_inc(max_ready, 1)
                    dve.wait_ge(max_ready, m + 1)
                    dve.tensor_scalar(shift[:, j:j + 1], nmax[:, j:j + 1], EX_LIFT * math.log(2.0), None,
                                      ALU.add).then_inc(shift_ready, 1)

                def reduce_pair(m, j, gg, c):
                    k = QUADS * gg + c
                    dve.wait_ge(bc_done, m * PAIRS + k + 1)
                    dve.scalar_tensor_tensor(feat[:, j, k, :], feat[:, j, k, :], 1.0, psB[:, k % BANKS, :],
                                             ALU.mult, ALU.mult,
                                             accum_out=sums[:, j, gg, c:c + 1]).then_inc(reduced, 1)

                def finish(m, part):
                    row = x1[:, bass.ds(m // 2, 1), :].rearrange("p t d -> p (t d)")
                    if part == 0:
                        dve.wait_ge(o_done, m + 1)
                    else:
                        dve.wait_ge(fin_steps, m * 4 + part)
                    if part == 0:
                        dve.tensor_scalar(den[:, 0:1], psO[:, D:DV], EPS_DEN * 2.0 ** EX_LIFT, None,
                                          ALU.add).then_inc(fin_steps, 1)
                    elif part == 1:
                        dve.reciprocal(den[:, 0:1], den[:, 0:1]).then_inc(fin_steps, 1)
                    elif part == 2:
                        dve.tensor_tensor(den[:, 1:2], den[:, 0:1], psO[:, D:DV], ALU.mult).then_inc(fin_steps, 1)
                    elif part == 3:
                        dve.scalar_tensor_tensor(row, bias_out[:], den[:, 1:2], row, ALU.mult, ALU.add).then_inc(fin_steps, 1)
                    else:
                        dve.scalar_tensor_tensor(row, psO[:, 0:D], den[:, 0:1], row, ALU.mult, ALU.add).then_inc(fin_ready, 1)

                def product(m, f, first=False):
                    dve.wait_ge(right_done, m * GT + f + 1)
                    dve.wait_ge(left_kept, m * GT + f + 1)
                    if not first:
                        dve.wait_ge(gate_done, m * GT)
                    dve.scalar_tensor_tensor(z[:, f, :], psX, b2[:, f, bass.ds(m % E, 1)], left[:, f, :],
                                             ALU.add, ALU.mult).then_inc(z_ready, 1)

                def add_experts(m, i, first=False):
                    if i == 0:
                        if not first:
                            dve.wait_ge(y_added, m * TB)
                        dve.wait_ge(y_done, m + 1)
                        dve.wait_ge(fin_ready, m + 1)
                    row = x1[:, bass.ds(m // E * TB + i, 1), :].rearrange("p t d -> p (t d)")
                    dve.scalar_tensor_tensor(row, psY[:, i * D:(i + 1) * D],
                                             share[:, bass.ds(m // E * (TB * E) + i * E + m % E, 1)], row,
                                             ALU.mult, ALU.add).then_inc(y_added, 1)

                def tile(t, first=False, last=False):
                    for j in range(2):
                        m = t * 2 + j
                        none, final = first and j == 0, last and j == 1
                        work = {
                            (1, 2): lambda: product(m, 0, none),
                            (3, 0): lambda: product(m, 1, none),
                            (2, 0): lambda: none or finish(m - 1, 0),
                            (2, 1): lambda: none or finish(m - 1, 1),
                            (2, 2): lambda: none or finish(m - 1, 2),
                            (2, 3): lambda: none or finish(m - 1, 3),
                            (3, 1): lambda: none or finish(m - 1, 4),
                            (4, 0): lambda: none or add_experts(m - 1, 0, first),
                            (4, 3): lambda: final or largest(m + 1, 1 - j),
                            (5, 0): lambda: none or add_experts(m - 1, 1),
                            (5, 2): lambda: none or add_experts(m - 1, 2),
                            (5, 3): lambda: none or add_experts(m - 1, 3),
                        }
                        for gg in range(GROUPS):
                            late = behind(m, j, gg, FEATURE_LAG)
                            for c in range(QUADS):
                                reduce_pair(m, j, gg, c)
                                if (gg, c) in work:
                                    work[gg, c]()
                                if makes(late, first, last):
                                    if c == 0 and not (none and late[3] == 1):
                                        dve.wait_ge(reduced, (late[0] - 2) * PAIRS + QUADS * (late[2] + 1))
                                    feature(*late[0:3], c)

                for n in range(2 * GROUPS - FEATURE_LAG):
                    for c in range(QUADS):
                        feature(n // GROUPS, n // GROUPS, n % GROUPS, c)
                    if n == GROUPS + 3:
                        largest(0, 0)
                tile(0, first=True)
                with dve.Fori(1, NT - 1) as t:
                    tile(t)
                tile(NT - 1, last=True)
                for part in range(5):
                    finish(MB - 1, part)
                for i in range(TB):
                    add_experts(MB - 1, i)

            @block.scalar
            def _(act):
                def roots(m, j, gg, before=True):
                    b, pair0 = slot_parts(m)
                    if before:
                        act.wait_ge(reduced, m * PAIRS - 2 * PAIRS + QUADS * (gg + 1))
                    if ON_ACT[gg]:
                        act.sem_inc(act_passed, 1)
                    for c in range(ON_DVE[gg], QUADS):
                        act.activation(feat[:, j, QUADS * gg + c, :], kT[:, bass.ds(b * N, N)], ACT.Relu,
                                       bias=q2[:, bass.ds(pair0 + GROUPS * c + gg, 1)]).then_inc(act_feat, 1)
                    act.wait_ge(feat_ready, m * sum(ON_DVE) + sum(ON_DVE[:gg + 1]))
                    if sum(ON_ACT):
                        act.wait_ge(act_feat, m * sum(ON_ACT) + sum(ON_ACT[:gg + 1]))
                    grp = feat[:, j, QUADS * gg:QUADS * (gg + 1), :].rearrange("p k n -> p (k n)")
                    act.activation(grp, grp, ACT.Sqrt, bias=eps[:]).then_inc(e_ready, 1)

                def exponentials(m, j, before=2):
                    act.wait_ge(shift_ready, m + 1)
                    if before == 2:
                        act.wait_ge(exT_done, m - 1)
                        act.wait_ge(spread_ready, m - 1)
                    act.activation(ex[:, j, :], psS, ACT.Exp, bias=shift[:, j:j + 1]).then_inc(ex_ready, 1)
                    if before:
                        act.wait_ge(split_step, m)
                    act.activation(exh[:], psS, ACT.Exp, bias=shift[:, j:j + 1]).then_inc(exh_ready, 1)

                def keep_exT(m, j, warm=True):
                    act.wait_ge(exT_done, m + 1)
                    if warm:
                        act.wait_ge(o_done, m - 1)
                    act.activation(exT[:, j, :, j * BLK:(j + 1) * BLK].rearrange("p t (c r) -> p t c r", c=QUADS),
                                   psT.rearrange("p (t c r) -> p t c r", t=TB, c=QUADS)[:, :, :, 0:16],
                                   ACT.Copy).then_inc(exT_kept, 1)

                def keep_left(m, f, first=False):
                    act.wait_ge(left_done, m * GT + f + 1)
                    if not first:
                        act.wait_ge(z_ready, m * GT - GT + f + 1)
                    act.sem_inc(act_passed, 1)
                    act.activation(left[:, f, :], psY, ACT.Identity, bias=b1[:, f, bass.ds(m % E, 1)]).then_inc(left_kept, 1)

                def silu(m, first=False):
                    if not first:
                        act.wait_ge(y_done, m)
                    for f in range(GT):
                        act.wait_ge(gate_done, m * GT + f + 1)
                        act.sem_inc(act_passed, 1)
                        act.activation(s[:, f, :], (psZ, psX)[f], ACT.Silu,
                                       bias=bg[:, f, bass.ds(m % E, 1)]).then_inc(s_ready, 1)

                def tile(t, first=False, last=False):
                    for j in range(2):
                        m = t * 2 + j
                        none = first and j == 0
                        for gg in range(GROUPS):
                            if gg == LEFT_AT[0] and not (last and j == 1):
                                keep_left(m + 1, 0)
                            if gg == LEFT_AT[1]:
                                keep_left(m, 1, none)
                            if gg == EXT_AT:
                                keep_exT(m, j, warm=not first)
                            if gg == 5 and not (last and j == 1):
                                exponentials(m + 1, 1 - j, before=1 if none else 2)
                            if gg == 5:
                                silu(m, none)
                            late = behind(m, j, gg, FEATURE_LAG)
                            if makes(late, first, last):
                                roots(*late[0:3], before=not (none and late[3] == 1))

                for n in range(2 * GROUPS - FEATURE_LAG):
                    roots(n // GROUPS, n // GROUPS, n % GROUPS, before=False)
                    if n == GROUPS + 3:
                        exponentials(0, 0, before=0)
                keep_left(0, 0, first=True)
                tile(0, first=True)
                with act.Fori(1, NT - 1) as t:
                    tile(t)
                tile(NT - 1, last=True)

            @block.gpsimd
            def _(pool):
                def split(m, j, before=2):
                    pool.wait_ge(exh_ready, m + 1)
                    if before:
                        pool.wait_ge(spread_ready, m)
                    if before == 2:
                        pool.wait_ge(placed, 2 * (m - 1))
                    if before == 2:
                        pool.wait_ge(bc_done, (m - 1) * PAIRS)
                    pool.sem_inc(pool_passed, 1)
                    pool.tensor_scalar(part[:], exh[:], split_by[:], None, ALU.mult).then_inc(split_step, 1)
                    pool.wait_ge(split_step, m + 1)
                    pool.tensor_tensor(spread[:, j, :], part[:], ex[:, j, :], ALU.add).then_inc(spread_ready, 1)

                def place(m, j, last_split, warm=True):
                    pool.wait_ge(reduced, (m + 1) * PAIRS)
                    if warm:
                        pool.wait_ge(o_done, m - 1)
                    v = sumsT[:, j, j * BLK:(j + 1) * BLK].rearrange("p (c g h) -> p g c h", c=QUADS, h=2)
                    for h in range(2):
                        if h:
                            pool.wait_ge(placed, 2 * m + 1)
                        else:
                            pool.wait_ge(spread_ready, last_split)
                        pool.sem_inc(pool_passed, 1)
                        pool.tensor_copy(v[h * A:(h + 1) * A, :, :, h], sums[h * A:(h + 1) * A, j]).then_inc(placed, 1)

                def tile(t, first=False, last=False):
                    for j in range(2):
                        m = t * 2 + j
                        if not (last and j == 1):
                            split(m + 1, 1 - j, before=1 if first and j == 0 else 2)
                        place(m, j, m + 1 if last and j == 1 else m + 2, warm=not first)

                split(0, 0, before=0)
                tile(0, first=True)
                with pool.Fori(1, NT - 1) as t:
                    tile(t)
                tile(NT - 1, last=True)

            @block.tensor
            def _(pe):
                def scores(m, j, gg, first=False):
                    pe.wait_ge(e_ready, m * GROUPS + gg + 1)
                    if gg == 0 and not first:
                        pe.wait_ge(exh_ready, m)
                    for c in range(QUADS):
                        ins = pe.matmul(psS[32 * c:32 * (c + 1), :], phi_cols[:, gg, :],
                                        feat[:, j, QUADS * gg + c, :], start=(gg == 0), stop=(gg == GROUPS - 1))
                    if gg == GROUPS - 1:
                        ins.then_inc(s_done, 1)

                def broadcast(m, j, gg, c, warm=True):
                    k = QUADS * gg + c
                    if warm or k >= BANKS:
                        before = k - BANKS if k >= BANKS else k + PAIRS // BANKS * BANKS - PAIRS
                        before = before - BANKS if before >= 0 and k < BANKS else before
                        pe.wait_ge(reduced, m * PAIRS + before + 1)
                    pe.matmul(psB[:, k % BANKS, :], sel[:, gg, c, :], spread[:, j, :], start=True,
                              stop=True).then_inc(bc_done, 1)

                def transpose_ex(m, j, first=False):
                    pe.wait_ge(ex_ready, m + 1)
                    if not first:
                        pe.wait_ge(fin_ready, m)
                    for i in range(TB):
                        ins = pe.transpose(psT[:, i * P:(i + 1) * P], ex[:, j, i * P:(i + 1) * P], ident[:])
                    ins.then_inc(exT_done, 1)

                def combine(m, j, half):
                    b = m // BB
                    if half == 0:
                        pe.wait_ge(placed, 2 * (m + 1))
                        pe.wait_ge(exT_kept, m + 1)
                    for i in (2 * half, 2 * half + 1):
                        pe.matmul(psO[:, 0:DV], exT[:, j, i, :],
                                  V[:, bass.ds(b * TB + i, 1), :].rearrange("p t d -> p (t d)"),
                                  start=(i == 0), stop=False)
                    if half:
                        pe.matmul(psO[:, 0:DV], sumsT[:, j, :], weT[:], start=False, stop=True).then_inc(o_done, 1)

                def left_product(m, f, first=0):
                    if f == 0:
                        pe.wait_ge(w12_in, (m + 1) * 32)
                        if first < 2:
                            pe.wait_ge(left_kept, m * GT)
                        if first < 1:
                            pe.wait_ge(y_added, (m - 1) * TB)
                    else:
                        pe.wait_ge(left_kept, m * GT + 1)
                    pe.matmul(psY, w1[:, f * P:(f + 1) * P], xnT[:, bass.ds(m // E * N, N)], start=True,
                              stop=True).then_inc(left_done, 1)

                def right_product(m, f, first=0):
                    if f:
                        pe.wait_ge(z_ready, m * GT + 1)
                    elif first < 2:
                        pe.wait_ge(s_ready, m * GT)
                    pe.matmul(psX, w2[:, f * P:(f + 1) * P], xnT[:, bass.ds(m // E * N, N)], start=True,
                              stop=True).then_inc(right_done, 1)

                def gate(m, f, half):
                    if half == 0 and f == 0:
                        pe.wait_ge(z_ready, (m + 1) * GT)
                        pe.wait_ge(wg_in, (m + 1) * 16)
                    ins = pe.matmul((psZ, psX)[f], wg[:, half * DFF + f * P:half * DFF + (f + 1) * P], z[:, half, :],
                                    start=(half == 0), stop=(half == 1))
                    if half:
                        ins.then_inc(gate_done, 1)

                def down(m, half, last=False):
                    if half == 0:
                        pe.wait_ge(s_ready, (m + 1) * GT)
                        pe.wait_ge(w3_in, (m + 1) * 16)
                        if not last:
                            pe.wait_ge(left_kept, (m + 2) * GT)
                    for i in (2 * half, 2 * half + 1):
                        for f in range(GT):
                            ins = pe.matmul(psY[:, i * D:(i + 1) * D], s[:, f, i * P:(i + 1) * P],
                                            w3[:, f * D:(f + 1) * D], start=(f == 0), stop=(f == GT - 1))
                    if half:
                        ins.then_inc(y_done, 1)

                def tile(t, first=False, last=False):
                    for j in range(2):
                        m = t * 2 + j
                        none, final = first and j == 0, last and j == 1
                        work = {
                            (0, 3): lambda: left_product(m, 1),
                            (1, 1): lambda: none or combine(m - 1, 1 - j, 0),
                            (1, 3): lambda: none or combine(m - 1, 1 - j, 1),
                            (2, 1): lambda: right_product(m, 1),
                            (2, 3): lambda: none or down(m - 1, 0),
                            (3, 1): lambda: none or down(m - 1, 1),
                            (3, 3): lambda: gate(m, 0, 0),
                            (4, 1): lambda: gate(m, 0, 1),
                            (4, 3): lambda: gate(m, 1, 0),
                            (5, 1): lambda: gate(m, 1, 1),
                            (6, 1): lambda: transpose_ex(m, j, none),
                            (6, 3): lambda: final or left_product(m + 1, 0, first=1 if none else 0),
                            (7, 1): lambda: final or right_product(m + 1, 0),
                        }
                        pe.wait_ge(spread_ready, m + 1)
                        for gg in range(GROUPS):
                            for c in range(QUADS):
                                broadcast(m, j, gg, c, warm=not none)
                                if (gg, c) in work:
                                    work[gg, c]()
                                if (gg, c) in SCORES_AT:
                                    k = SCORES_AT[gg, c]
                                    if gg >= 6 and not last:
                                        scores(m + 2, j, k)
                                    elif gg < 6 and not final:
                                        scores(m + 1, 1 - j, k)

                for gg in range(GROUPS):
                    scores(0, 0, gg, first=True)
                left_product(0, 0, first=2)
                right_product(0, 0, first=2)
                for (gg, c), k in SCORES_AT.items():
                    if gg >= 6:
                        scores(1, 1, k)
                tile(0, first=True)
                with pe.Fori(1, NT - 1) as t:
                    tile(t)
                tile(NT - 1, last=True)
                down(MB - 1, 0, last=True)
                down(MB - 1, 1)
                combine(MB - 1, 1, 0)
                combine(MB - 1, 1, 1)

            @block.sync
            def _(sp):
                def load_up(e):
                    sp.dma_start(w1[:], g.e_w1[bass.ds(e, 1), :, :].rearrange("e d f -> (e d) f")).then_inc(w12_in, 16)
                    sp.dma_start(w2[:], g.e_w2[bass.ds(e, 1), :, :].rearrange("e d f -> (e d) f")).then_inc(w12_in, 16)

                def load_gate(e):
                    sp.dma_start(wg[:].rearrange("p (t n) -> p t n", t=GT),
                                 g.e_wg[bass.ds(e, 1), :, :].rearrange("e (t p) n -> p (e t) n", p=P)).then_inc(wg_in, 16)

                def load_down(e):
                    sp.dma_start(w3[:].rearrange("p (t n) -> p t n", t=GT),
                                 g.e_w3[bass.ds(e, 1), :, :].rearrange("e (t p) n -> p (e t) n", p=P)).then_inc(w3_in, 16)

                load_up(0)
                load_gate(0)
                load_down(0)
                with sp.Fori(1, MB) as u:
                    sp.wait_ge(right_done, u * GT)
                    load_up(u % E)
                    sp.wait_ge(gate_done, u * GT)
                    load_gate(u % E)
                    sp.wait_ge(y_done, u)
                    load_down(u % E)
                for b in range(B):
                    sp.wait_ge(fin_ready, (b + 1) * BB)
                    sp.wait_ge(y_added, (b + 1) * BB * TB)
                    sp.dma_start(g.out_tiles[:, b * TB:(b + 1) * TB, :], x1[:, b * TB:(b + 1) * TB, :]).then_inc(out_done, 16)
                sp.wait_ge(out_done, 16 * B)


def _layout(inputs):
    import numpy as np

    def heads(w, width):
        return np.asarray(w).reshape(8, width, 128).transpose(2, 0, 1)

    def columns(b):
        b = np.asarray(b)
        return b.reshape(b.shape[0], -1, 128).transpose(2, 1, 0)

    def twice(w):
        return np.concatenate([w, w], axis=1)

    i = {k: np.asarray(v) for k, v in inputs.items()}
    return {
        "x": i["L0_attn_x"],
        "wqk": np.concatenate([heads(i["L0_attn_Wq"], 64), heads(i["L0_attn_Wk"], 64)], axis=2),
        "wv": i["L0_attn_Wv"].T,
        "gate0_w": i["L0_ffn_gate_w"], "gate0_b": i["L0_ffn_gate_b"],
        "w1": i["L0_ffn_w1"], "b1": columns(i["L0_ffn_b1"]).transpose(0, 2, 1), "w2": i["L0_ffn_w2"], "b2": i["L0_ffn_b2"],
        "a_wq": twice(i["L1_attn_Wq"].T), "a_wk": twice(i["L1_attn_Wk"].T),
        "a_phi": np.concatenate([i["L1_attn_Wphi"], i["L1_attn_Wphi"]]).reshape(128, 1),
        "a_wy": i["L1_attn_Wy_w"].T, "a_wyb": i["L1_attn_Wy_b"],
        "a_we": np.concatenate([i["L1_attn_We_w"].T, i["L1_attn_We_w"].T], axis=0), "a_web": i["L1_attn_We_b"],
        "gate1_w": i["L1_ffn_gate_w"], "gate1_b": i["L1_ffn_gate_b"],
        "e_w1": i["L1_ffn_w1"], "e_b1": columns(i["L1_ffn_b1"]),
        "e_w2": i["L1_ffn_w2"], "e_b2": columns(i["L1_ffn_b2"]),
        "e_wg": i["L1_ffn_wg"], "e_bg": columns(i["L1_ffn_bg"]),
        "e_w3": i["L1_ffn_w3"], "e_b3": i["L1_ffn_b3"],
    }


def kernel(**inputs):
    import numpy as np
    import concourse.bacc as bacc
    from concourse.bass_utils import run_bass_kernel_spmd

    nc = bacc.Bacc("TRN2", target_bir_lowering=False, num_devices=1)
    arrays, args = {}, {}
    for name, a in _layout(inputs).items():
        a = np.ascontiguousarray(a)
        arrays[f"in_{name}"] = a
        args[name] = nc.dram_tensor(f"in_{name}", a.shape, mybir.dt.from_np(a.dtype), kind="ExternalInput").ap()
    out = nc.dram_tensor("out_0", (B, N, D), F32, kind="ExternalOutput").ap()
    layers_kernel(nc, out=out, **args)
    r = run_bass_kernel_spmd(nc, [arrays], core_ids=[0])
    return r.results[0]["out_0"]
```

```python
from contextlib import ExitStack
import math

import concourse.bass as bass
from concourse import mybir

F32 = mybir.dt.float32
BF16 = mybir.dt.bfloat16
F16 = mybir.dt.float16
F32R = mybir.dt.float32r
U32 = mybir.dt.uint32
ALU = mybir.AluOpType
ACT = mybir.ActivationFunctionType
AX = mybir.AxisListType

P = 128
B, N, D = 4, 512, 128
TOK = B * N
NT = TOK // P
TB = N // P
H, R = 8, 64
E = 8
CAP = 80
SLOTS = E * CAP
ST = SLOTS // P
F0 = 512
FT = F0 // P
DFF = 256
GT = DFF // P
A = 64
BLK = 64
PAIRS = BLK // 2
QUADS = 4
GROUPS = PAIRS // QUADS
LN_EPS = 1e-5
EPS_RHO = 1e-8
EPS_DEN = 1e-9
DV = D + 1
EX_LIFT = 15
REGION = 16704
DROPPED = 4096


class Memory:
    pass


class Chain:

    def __init__(self, eng, sem, base=0):
        self.eng, self.sem, self.base, self.n = eng, sem, base, 0

    def step(self, ins):
        self.n += 1
        ins.then_inc(self.sem, 1)
        return self.n

    def done(self, n=None):
        self.eng.wait_ge(self.sem, self.base + (self.n if n is None else n))

    def link(self, ins):
        self.step(ins)
        self.done()


def per_tile(ap, n):
    return ap.unsqueeze(2).to_broadcast([P, ap.shape[1], n])


def first_max(dve, chain, values, desc, top, tie, rank, mask):
    chain.link(dve.reduce_max(top, values, axis=AX.X))
    chain.link(dve.tensor_tensor(tie, values, per_tile(top, E), ALU.is_equal))
    chain.link(dve.tensor_tensor(tie, tie, desc, ALU.mult))
    chain.link(dve.reduce_max(rank, tie, axis=AX.X))
    chain.link(dve.tensor_tensor(mask, desc, per_tile(rank, E), ALU.is_equal))


def norm_scale(dve, chain, x, stats, mv, std, rstd, var_ready, std_ready):
    for t in range(NT):
        chain.step(dve.bn_stats(stats[:, t, :], x[:, t, :]))
    chain.done()
    for t in range(NT):
        chain.step(dve.bn_aggr(mv[:, t, :], stats[:, t, :]))
    chain.done()
    dve.tensor_scalar(std, mv[:, :, 1], LN_EPS, None, ALU.add).then_inc(var_ready, 1)
    dve.wait_ge(std_ready, 1)
    chain.link(dve.reciprocal(rstd, std))


def layers_kernel(nc, x, wqk, wv, gate0_w, gate0_b, w1, b1, w2, b2,
                  a_wq, a_wk, a_phi, a_wy, a_wyb, a_we, a_web,
                  gate1_w, gate1_b, e_w1, e_b1, e_w2, e_b2, e_wg, e_bg, e_w3, e_b3, out):
    g = Memory()
    g.gate0_w, g.gate0_b, g.gate1_w, g.gate1_b = gate0_w, gate0_b, gate1_w, gate1_b
    g.wqk, g.wv, g.w1, g.b1, g.w2, g.b2 = wqk, wv, w1, b1, w2, b2
    g.a_wq, g.a_wk, g.a_phi, g.a_wy, g.a_wyb, g.a_we, g.a_web = a_wq, a_wk, a_phi, a_wy, a_wyb, a_we, a_web
    g.e_w1, g.e_b1, g.e_w2, g.e_b2, g.e_wg, g.e_bg, g.e_w3, g.e_b3 = e_w1, e_b1, e_w2, e_b2, e_wg, e_bg, e_w3, e_b3
    with ExitStack() as ctx:
        def sb(name, shape, dt=F32):
            return ctx.enter_context(nc.sbuf_tensor(name, shape, dt))

        g.x1 = sb("x1", [P, NT, D])
        g.xnT = sb("xnT", [P, TOK])
        g.ident = sb("ident", [P, P])
        g.share = sb("share", [P, NT, E])
        g.kT2 = sb("kT2", [P, TOK])
        g.q2 = sb("q2", [P, TOK // 2])
        g.V2 = sb("V2", [P, NT, DV])
        g.phi_cols = sb("phi_cols", [P, GROUPS, 32])
        g.sel = sb("sel", [P, GROUPS, QUADS, P], F16)
        g.weT = sb("weT", [P, DV])
        g.value_bias = sb("value_bias", [P, D])
        g.split_by = sb("split_by", [P, 1])
        g.eps = sb("eps", [P, 1])
        g.exT = sb("exT", [P, 2, TB, P])
        g.sumsT = sb("sumsT", [P, 2, P])
        g.b1e, g.b2e = sb("b1e", [P, GT, E]), sb("b2e", [P, GT, E])
        g.bge, g.ones = sb("bge", [1, DFF]), sb("ones_row", [1, N])
        g.w1e, g.w2e = sb("w1e", [P, DFF]), sb("w2e", [P, DFF])
        g.wge, g.w3e = sb("wge", [P, GT * DFF]), sb("w3e", [P, GT * D])
        g.wq, g.wk, g.wy, g.wyb = (g.wge[:, i * P:(i + 1) * P] for i in range(4))
        g.web, g.rho = g.w3e[:, 0:P], g.w3e[:, P:2 * P]
        g.phi, g.mask_c = sb("phi", [P, 1])[:], sb("mask_c", [P, QUADS])[:]

        g.disp = nc.dram_tensor("disp", (SLOTS, D), F32, kind="Internal").ap()
        g.eout = nc.dram_tensor("eout", (SLOTS, D), F32, kind="Internal").ap()
        g.x_tiles = x.rearrange("b (t p) d -> p (b t) d", p=P)
        g.out_tiles = out.rearrange("b (t p) d -> p (b t) d", p=P)

        with ExitStack() as first:
            def scratch(name, shape, dt=F32):
                return first.enter_context(nc.sbuf_tensor(name, shape, dt))

            region = scratch("region", [P, REGION])
            g.taken = 0

            def take(*shape):
                n = math.prod(shape)
                v = region[:, g.taken:g.taken + n]
                g.taken += n
                assert g.taken <= REGION
                if len(shape) == 2:
                    v = v.rearrange("p (a b) -> p a b", a=shape[0])
                elif len(shape) == 3:
                    v = v.rearrange("p (a b c) -> p a b c", a=shape[0], b=shape[1])
                return v

            g.xn = take(NT, D)
            g.wqk_sb = take(H, P)
            g.wv_sb = take(H * D)
            g.w1_sb = take(E, F0)
            g.w2_sb = take(E, FT, D)
            g.b1_sb = take(E, FT)
            g.b2_sb = take(E, D)
            g.gathered = take(NT, D)

            g.desc = scratch("desc", [P, NT, E])
            g.lg = scratch("lg", [P, NT, E])
            g.tie = scratch("tie", [P, NT, E])
            g.mask1 = scratch("mask1", [P, NT, E])
            g.mask2 = scratch("mask2", [P, NT, E])
            g.top = scratch("top", [P, NT])
            g.rank = scratch("rank", [P, NT])
            g.stats = scratch("stats", [P, NT, 6])
            g.mv = scratch("mv", [P, NT, 2])
            g.std = scratch("std", [P, NT])
            g.rstd = scratch("rstd", [P, NT])
            g.coef = scratch("coef", [P, NT])
            g.gather_at = scratch("gather_at", [P, NT], U32)
            g.gateb = scratch("gateb", [P, E])

            normalise_and_route(nc, g)
            first_layer(nc, g, take)
            g.taken = 0
            second_route(nc, g, take)
        g.arena = sb("arena", [P, 2 * PAIRS * N])
        second_layer(nc, g, sb)


def normalise_and_route(nc, g):
    with ExitStack() as ctx:
        def sb(name, shape, dt=F32):
            return ctx.enter_context(nc.sbuf_tensor(name, shape, dt))

        def sem(name):
            return ctx.enter_context(nc.semaphore(name))

        tri = sb("tri", [P, P], BF16)
        ones = sb("ones", [P, P], BF16)
        place0 = sb("place0", [P, NT, E])
        past = sb("past", [P, NT])
        maskb = sb("maskb", [P, NT, E], BF16)
        ex = sb("ex", [P, NT, E])
        esum = sb("esum", [P, NT])
        pre = sb("pre", [P, 2, NT, E])
        queue = sb("queue", [P, NT, E])
        own = sb("own", [P, NT])
        keep = sb("keep", [P, NT])
        slot = sb("slot", [P, NT])
        scatter_at = sb("scatter_at", [P, NT], U32)
        zeros = sb("zeros", [P, ST * D])
        gw = sb("gw", [P, E])
        psX = ctx.enter_context(nc.psum_tensor("psX", [P, 4, 512], F32))
        psL = ctx.enter_context(nc.psum_tensor("psL", [P, NT, E], F32))
        psC = ctx.enter_context(nc.psum_tensor("psC", [P, 2, NT, E], F32))

        x_in, gate_in, w_in = sem("x_in"), sem("gate_in"), sem("w_in")
        pool_made, consts = sem("pool_made"), sem("consts")
        dve_steps, var_ready, std_ready = sem("dve_steps"), sem("var_ready"), sem("std_ready")
        xn_ready, xT_done, xT_kept = sem("xn_ready"), sem("xT_done"), sem("xT_kept")
        logits_done, shifted, exp_done = sem("logits_done"), sem("shifted"), sem("exp_done")
        mask_ready, counts_done, places = sem("mask_ready"), sem("counts_done"), sem("places")
        zero_ready, zero_out, scattered = sem("zero_ready"), sem("zero_out"), sem("scattered")
        block = ctx.enter_context(nc.Block())

        @block.sync
        def _(sp):
            sp.dma_start(g.x1[:], g.x_tiles).then_inc(x_in, 16)
            sp.dma_start(gw[:], g.gate0_w).then_inc(gate_in, 16)
            sp.dma_start(g.gateb[:], g.gate0_b.partition_broadcast(P)).then_inc(gate_in, 16)
            sp.wait_ge(zero_ready, 1)
            sp.dma_start(g.disp.rearrange("(t p) d -> p t d", p=P),
                         zeros[:].rearrange("p (t d) -> p t d", t=ST)).then_inc(zero_out, 16)
            sp.dma_start(g.wqk_sb, g.wqk).then_inc(w_in, 16)
            sp.dma_start(g.wv_sb, g.wv).then_inc(w_in, 16)
            sp.dma_start(g.w1_sb, g.w1.rearrange("e d f -> d e f")).then_inc(w_in, 16)
            sp.dma_start(g.w2_sb.rearrange("p e t d -> p (e t) d"),
                         g.w2.rearrange("e (t p) d -> p (e t) d", p=P)).then_inc(w_in, 16)
            sp.dma_start(g.b1_sb, g.b1).then_inc(w_in, 16)
            sp.dma_start(g.b2_sb[0:1, :, :], g.b2.rearrange("(o e) d -> o e d", o=1)).then_inc(w_in, 16)
            sp.wait_ge(w_in, 96)

        @block.gpsimd
        def _(pool):
            pool.memset(g.ident[:], 0.0).then_inc(pool_made, 1)
            pool.memset(tri[:], 1.0).then_inc(pool_made, 1)
            pool.memset(ones[:], 1.0).then_inc(consts, 1)
            pool.memset(zeros[:], 0.0).then_inc(zero_ready, 1)
            pool.wait_ge(pool_made, 2)
            pool.affine_select(out=g.ident[:], in_=g.ident[:], compare_op=ALU.not_equal, fill=1.0,
                               base=0, pattern=[[-1, P]], channel_multiplier=1).then_inc(consts, 1)
            pool.affine_select(out=tri[:], in_=tri[:], compare_op=ALU.is_ge, fill=0.0,
                               base=0, pattern=[[1, P]], channel_multiplier=-1).then_inc(consts, 1)
            pool.iota(g.desc[:], pattern=[[0, NT], [-1, E]], base=E, channel_multiplier=0,
                      allow_small_or_imprecise_dtypes=True).then_inc(consts, 1)
            pool.iota(place0[:], pattern=[[0, NT], [CAP, E]], base=-1, channel_multiplier=0,
                      allow_small_or_imprecise_dtypes=True).then_inc(consts, 1)
            pool.iota(past[:], pattern=[[P, NT]], base=DROPPED, channel_multiplier=1,
                      allow_small_or_imprecise_dtypes=True).then_inc(consts, 1)
            pool.wait_ge(places, 2)
            pool.wait_ge(zero_out, 16)
            pool.wait_ge(xn_ready, NT)
            for t in range(NT):
                pool.indirect_dma_start(
                    g.disp, bass.IndirectOffsetOnAxis(ap=scatter_at[:, t:t + 1], axis=0),
                    g.xn[:, t, :], None, bounds_check=SLOTS - 1, oob_is_err=False).then_inc(scattered, 16)
            pool.wait_ge(scattered, 16 * NT)

        @block.scalar
        def _(act):
            act.wait_ge(var_ready, 1)
            act.activation(g.std[:], g.std[:], ACT.Sqrt).then_inc(std_ready, 1)
            for c in range(4):
                act.wait_ge(xT_done, c + 1)
                act.activation(g.xnT[:, c * 512:(c + 1) * 512], psX[:, c, :], ACT.Copy).then_inc(xT_kept, 1)
            act.wait_ge(shifted, 1)
            act.activation(ex[:], ex[:], ACT.Exp).then_inc(exp_done, 1)

        @block.vector
        def _(dve):
            chain = Chain(dve, dve_steps)
            dve.wait_ge(x_in, 16)
            norm_scale(dve, chain, g.x1, g.stats, g.mv, g.std[:], g.rstd[:], var_ready, std_ready)
            for t in range(NT):
                dve.tensor_scalar(g.xn[:, t, :], g.x1[:, t, :], g.mv[:, t, 0:1], g.rstd[:, t:t + 1],
                                  ALU.subtract, ALU.mult).then_inc(xn_ready, 1)
            dve.wait_ge(logits_done, 1)
            dve.wait_ge(gate_in, 32)
            dve.wait_ge(consts, 6)
            chain.link(dve.tensor_tensor(g.lg[:], psL[:], g.gateb[:].unsqueeze(1).to_broadcast([P, NT, E]), ALU.add))
            first_max(dve, chain, g.lg[:], g.desc[:], g.top[:], g.tie[:], g.rank[:], g.mask1[:])
            dve.tensor_copy(maskb[:], g.mask1[:]).then_inc(mask_ready, 1)
            dve.tensor_tensor(ex[:], g.lg[:], per_tile(g.top[:], E), ALU.subtract).then_inc(shifted, 1)
            dve.wait_ge(counts_done, 1)
            chain.link(dve.tensor_copy(pre[:, 0], psC[:, 1]))
            at = 0
            for k in (1, 2, 4, 8):
                chain.link(dve.tensor_copy(pre[:, 1 - at, 0:k], pre[:, at, 0:k]))
                chain.link(dve.tensor_tensor(pre[:, 1 - at, k:NT], pre[:, at, k:NT], pre[:, at, 0:NT - k], ALU.add))
                at = 1 - at
            chain.link(dve.tensor_tensor(queue[:], pre[:, at], psC[:, 1], ALU.subtract))
            chain.link(dve.tensor_tensor(queue[:], queue[:], psC[:, 0], ALU.add))
            chain.link(dve.tensor_tensor(g.tie[:], queue[:], g.mask1[:], ALU.mult))
            chain.link(dve.reduce_sum(own[:], g.tie[:], axis=AX.X))
            chain.link(dve.tensor_scalar(keep[:], own[:], float(CAP), None, ALU.is_le))
            chain.link(dve.tensor_tensor(queue[:], queue[:], place0[:], ALU.add))
            chain.link(dve.tensor_tensor(queue[:], queue[:], g.mask1[:], ALU.mult))
            chain.link(dve.reduce_sum(slot[:], queue[:], axis=AX.X))
            chain.link(dve.tensor_tensor(own[:], slot[:], keep[:], ALU.mult))
            dve.tensor_copy(g.gather_at[:], own[:]).then_inc(places, 1)
            chain.link(dve.tensor_tensor(slot[:], slot[:], past[:], ALU.subtract))
            chain.link(dve.tensor_tensor(slot[:], slot[:], keep[:], ALU.mult))
            chain.link(dve.tensor_tensor(slot[:], slot[:], past[:], ALU.add))
            dve.tensor_copy(scatter_at[:], slot[:]).then_inc(places, 1)
            dve.wait_ge(exp_done, 1)
            chain.link(dve.reduce_sum(esum[:], ex[:], axis=AX.X))
            chain.link(dve.reciprocal(esum[:], esum[:]))
            chain.link(dve.tensor_tensor(g.coef[:], esum[:], keep[:], ALU.mult))

        @block.tensor
        def _(pe):
            pe.wait_ge(consts, 6)
            for t in range(NT):
                pe.wait_ge(xn_ready, t + 1)
                ins = pe.transpose(psX[:, t // TB, (t % TB) * P:(t % TB + 1) * P], g.xn[:, t, :], g.ident[:])
                if t % TB == TB - 1:
                    ins.then_inc(xT_done, 1)
            pe.wait_ge(gate_in, 32)
            for t in range(NT):
                if t % TB == 0:
                    pe.wait_ge(xT_kept, t // TB + 1)
                ins = pe.matmul(psL[:, t, :], g.xnT[:, t * P:(t + 1) * P], gw[:], start=True, stop=True)
            ins.then_inc(logits_done, 1)
            pe.wait_ge(mask_ready, 1)
            pe.matmul(psC[:, 0].rearrange("p t e -> p (t e)"), tri[:], maskb[:].rearrange("p t e -> p (t e)"),
                      start=True, stop=True)
            pe.matmul(psC[:, 1].rearrange("p t e -> p (t e)"), ones[:], maskb[:].rearrange("p t e -> p (t e)"),
                      start=True, stop=True).then_inc(counts_done, 1)


def first_layer(nc, g, take):
    STEPS = H * TB
    with ExitStack() as ctx:
        def sem(name):
            return ctx.enter_context(nc.semaphore(name))

        def rounded(name, *shape):
            return ctx.enter_context(nc.sbuf_tensor(name, [P] + list(shape), F32R))

        V_hi, V_lo = rounded("V_hi", TB, H * D), rounded("V_lo", TB, H * D)
        q_parts = rounded("q_parts", 2, N)
        k_hi = rounded("k_hi", 2, N)
        k_lo = rounded("k_lo", 2, N)
        pT_hi, pT_lo = rounded("pT_hi", 2, TB, N), rounded("pT_lo", 2, TB, N)
        free = g.w1_sb.rearrange("p e f -> p (e f)")
        xTb, oT = free[:, 0:N], free[:, N:2 * N]
        ex = free[:, 2 * N:6 * N].rearrange("p (s n) -> p s n", s=4)
        free = g.xn.rearrange("p t d -> p (t d)")
        rows = free[:, 0:ST * D].rearrange("p (t d) -> p t d", t=ST)
        rowsT = free[:, ST * D:ST * D + SLOTS]
        hT = free[:, ST * D + SLOTS:ST * D + SLOTS + 2 * FT * CAP].rearrange("p (a f c) -> p a f c", a=2, f=FT)
        eo = take(E, D)
        one_row = take(P)
        zero = take(1)
        nmax = take(4)
        den = take(4)
        rden = take(4)
        ps = ctx.enter_context(nc.psum_tensor("ps0", [P, 8, 512], F32))
        SB, TBK, PJ, AV, VB = (0, 1), (2, 3), 4, 5, (6, 7)
        VALUES_AT = {1: 0, 3: 2, 5: 4, 6: 6, 9: 1, 11: 3, 13: 5, 15: 7}
        VALUES = list(VALUES_AT.values())
        ON_ACT = (2,)
        QK_AT, QK_HI, QK_LO = 1, 2, 3
        LAG_T, LAG_LO, LAG_W = 2, 3, 4

        rows_in, prep, zeroed = sem("rows_in"), sem("prep"), sem("zeroed")
        rowsT_done, rowsT_kept = sem("rowsT_done"), sem("rowsT_kept")
        h_done, h_kept, eo_done, eo_kept = sem("h_done"), sem("h_kept"), sem("eo_done"), sem("eo_kept")
        eo_out, gathered_in = sem("eo_out"), sem("gathered_in")
        small_in, c2_made, c2_prep = sem("small_in"), sem("c2_made"), sem("c2_prep")
        row_staged, v_done, v_kept = sem("row_staged"), sem("v_done"), sem("v_kept")
        qk_done, qk_kept = sem("qk_done"), sem("qk_kept")
        k_lo_filled, act_p_ready = sem("k_lo_filled"), sem("act_p_ready")
        q_hi_kept, k_hi_kept, v_hi_kept, lo_kept = (sem("q_hi_kept"), sem("k_hi_kept"), sem("v_hi_kept"),
                                                    sem("lo_kept"))
        s_done, nmax_ready, exp_ready = sem("s_done"), sem("nmax_ready"), sem("exp_ready")
        rden_ready, p_ready = sem("rden_ready"), sem("p_ready")
        pT_done, pT_kept, av_done = sem("pT_done"), sem("pT_kept"), sem("av_done")
        oT_kept, o_done, o_added = sem("oT_kept"), sem("o_done"), sem("o_added")
        OUT_AT = 5
        DRAIN = OUT_AT + 3

        def runs(late, first, drain):
            return late < 0 if drain else late >= 0 or not first

        block = ctx.enter_context(nc.Block())

        @block.sync
        def _(sp):
            sp.dma_start(rows, g.disp.rearrange("(t p) d -> p t d", p=P)).then_inc(rows_in, 16)
            sp.wait_ge(eo_kept, E)
            sp.dma_start(g.eout.rearrange("(e c) d -> c e d", c=CAP), eo[0:CAP, :, :]).then_inc(eo_out, 16)
            small = ((g.wq, g.a_wq), (g.wk, g.a_wk), (g.wy, g.a_wy), (g.wyb, g.a_wyb.partition_broadcast(P)),
                     (g.web, g.a_web.partition_broadcast(P)), (g.phi, g.a_phi), (g.weT[:, 0:D], g.a_we),
                     (g.b1e[:], g.e_b1), (g.b2e[:], g.e_b2))
            for v, src in small:
                sp.dma_start(v, src).then_inc(small_in, 16)
            sp.wait_ge(small_in, 16 * len(small))
            sp.wait_ge(eo_out, 16)

        @block.gpsimd
        def _(pool):
            pool.memset(one_row[0:1, :], 1.0).then_inc(prep, 1)
            pool.memset(zero, 0.0).then_inc(zeroed, 1)
            pool.wait_ge(zeroed, 1)
            prepare_constants(pool, g, c2_made, c2_prep)
            pool.wait_ge(eo_out, 16)
            for t in range(NT):
                pool.indirect_dma_start(
                    g.gathered[:, t, :], None, g.eout,
                    bass.IndirectOffsetOnAxis(ap=g.gather_at[:, t:t + 1], axis=0)).then_inc(gathered_in, 16)
            pool.wait_ge(gathered_in, 16 * NT)

        @block.scalar
        def _(act):
            act.wait_ge(rowsT_done, 1)
            act.activation(rowsT[:, 0:512], ps[:, 0, :], ACT.Copy).then_inc(rowsT_kept, 1)
            act.activation(rowsT[:, 512:SLOTS], ps[:, 1, 0:SLOTS - 512], ACT.Copy).then_inc(rowsT_kept, 1)
            for e in range(E):
                act.wait_ge(h_done, e + 1)
                if e >= 2:
                    act.wait_ge(eo_done, e - 1)
                for f in range(FT):
                    act.activation(hT[:, e % 2, f, :], ps[:, 2 + e % 2, f * CAP:(f + 1) * CAP],
                                   ACT.Gelu_apprx_tanh, bias=g.b1_sb[:, e, f:f + 1]).then_inc(h_kept, 1)

            def keep_qk_hi(b, h, first=False):
                act.wait_ge(qk_done, b * H + h + 1)
                if not first or h >= 2:
                    act.wait_ge(s_done, b * STEPS + (h - 1) * TB)
                act.activation(q_parts[0:R, h % 2, :], ps[0:R, PJ, :], ACT.Copy).then_inc(q_hi_kept, 1)
                for half in range(2):
                    act.activation(k_hi[half * R:(half + 1) * R, h % 2, :], ps[R:P, PJ, :], ACT.Copy).then_inc(k_hi_kept, 1)

            def row(b, first=False, drain=False):
                for s in range(DRAIN if drain else STEPS):
                    if s == 0 and not drain:
                        keep_qk_hi(b, 0, first)
                    if not drain:
                        act.wait_ge(nmax_ready, b * STEPS + s + 1)
                        if not first or s >= 4:
                            act.wait_ge(pT_done, b * STEPS + s - 3)
                        act.activation(ex[:, s % 4, :], ps[:, SB[s % 2], :], ACT.Exp, bias=nmax[:, s % 4:s % 4 + 1],
                                       accum_out=den[:, s % 4:s % 4 + 1]).then_inc(exp_ready, 1)
                    if not drain and s % TB == QK_HI and s // TB + 1 < H:
                        keep_qk_hi(b, s // TB + 1, first)
                    late = s - 1
                    if late % TB in ON_ACT and runs(late, first, drain):
                        act.wait_ge(rden_ready, b * STEPS + late + 1)
                        act.activation(ex[:, late % 4, :], ex[:, late % 4, :], ACT.Copy,
                                       scale=rden[:, late % 4:late % 4 + 1]).then_inc(act_p_ready, 1)
                    late = s - LAG_T
                    if runs(late, first, drain):
                        h, t = late // TB, late % TB
                        act.wait_ge(pT_done, b * STEPS + late + 1)
                        if t == 0 and (not first or h >= 2):
                            act.wait_ge(av_done, b * H + h - 1)
                        act.activation(pT_hi[:, h % 2, :, t * P:(t + 1) * P],
                                       ps[:, TBK[late % 2], :].rearrange("p (m n) -> p m n", m=TB),
                                       ACT.Copy).then_inc(pT_kept, 1)
                    if not drain and s in VALUES_AT:
                        j = VALUES_AT[s]
                        act.wait_ge(v_done, b * 2 * TB + VALUES.index(j) + 1)
                        if not first:
                            act.wait_ge(av_done, b * H - (0 if j % 2 else H // 2))
                        act.activation(V_hi[:, j // 2, j % 2 * 512:(j % 2 + 1) * 512], ps[:, VB[VALUES.index(j) % 2], :],
                                       ACT.Copy).then_inc(v_hi_kept, 1)

            row(0, first=True)
            with act.Fori(1, B) as b:
                row(b)
            row(B, drain=True)

        @block.vector
        def _(dve):
            dve.wait_ge(zeroed, 1)
            dve.tensor_copy(k_lo[R:P, :, :], zero[R:P, :].unsqueeze(2).to_broadcast([R, 2, N])).then_inc(k_lo_filled, 1)
            for e in range(E):
                dve.wait_ge(eo_done, e + 1)
                dve.tensor_copy(eo[0:CAP, e, :], ps[0:CAP, 4 + e % 2, 0:D]).then_inc(eo_kept, 1)

            def keep_qk_lo(b, h):
                dve.wait_ge(q_hi_kept, b * H + h + 1)
                dve.wait_ge(k_hi_kept, b * 2 * H + 2 * (h + 1))
                dve.tensor_tensor(q_parts[R:P, h % 2, :], ps[0:R, PJ, :], q_parts[0:R, h % 2, :].bitcast(F32),
                                  ALU.subtract).then_inc(qk_kept, 1)
                dve.tensor_tensor(k_lo[0:R, h % 2, :], ps[R:P, PJ, :], k_hi[0:R, h % 2, :].bitcast(F32),
                                  ALU.subtract).then_inc(qk_kept, 1)

            def row(b, first=False, drain=False):
                for s in range(DRAIN if drain else STEPS):
                    if s == 0 and not drain:
                        if not first:
                            dve.wait_ge(qk_done, b * H)
                        dve.tensor_copy(xTb, g.xnT[:, bass.ds(b * N, N)]).then_inc(row_staged, 1)
                        keep_qk_lo(b, 0)
                    if not drain:
                        dve.wait_ge(s_done, b * STEPS + s + 1)
                        if not first or s >= 4:
                            dve.wait_ge(exp_ready, b * STEPS + s - 3)
                        dve.reduce_max(nmax[:, s % 4:s % 4 + 1], ps[:, SB[s % 2], :], axis=AX.X,
                                       negate=True).then_inc(nmax_ready, 1)
                    late = s - 1
                    if runs(late, first, drain):
                        dve.wait_ge(exp_ready, b * STEPS + late + 1)
                        dve.reciprocal(rden[:, late % 4:late % 4 + 1], den[:, late % 4:late % 4 + 1]).then_inc(rden_ready, 1)
                        if late % TB not in ON_ACT:
                            dve.wait_ge(rden_ready, b * STEPS + late + 1)
                            dve.tensor_scalar(ex[:, late % 4, :], ex[:, late % 4, :], rden[:, late % 4:late % 4 + 1], None,
                                              ALU.mult).then_inc(p_ready, 1)
                    if not drain and s % TB == QK_LO and s // TB + 1 < H:
                        keep_qk_lo(b, s // TB + 1)
                    late = s - LAG_LO
                    if runs(late, first, drain):
                        h, t = late // TB, late % TB
                        dve.wait_ge(pT_kept, b * STEPS + late + 1)
                        dve.tensor_tensor(pT_lo[:, h % 2, :, t * P:(t + 1) * P],
                                          ps[:, TBK[late % 2], :].rearrange("p (m n) -> p m n", m=TB),
                                          pT_hi[:, h % 2, :, t * P:(t + 1) * P].bitcast(F32), ALU.subtract).then_inc(lo_kept, 1)
                    if not drain and s - 1 in VALUES_AT:
                        j = VALUES_AT[s - 1]
                        at = slice(j % 2 * 512, (j % 2 + 1) * 512)
                        dve.wait_ge(v_hi_kept, b * 2 * TB + VALUES.index(j) + 1)
                        dve.tensor_tensor(V_lo[:, j // 2, at], ps[:, VB[VALUES.index(j) % 2], :],
                                          V_hi[:, j // 2, at].bitcast(F32), ALU.subtract).then_inc(v_kept, 1)
                    if not first and s == OUT_AT:
                        dve.wait_ge(av_done, b * H)
                        dve.tensor_copy(oT, ps[:, AV, :]).then_inc(oT_kept, 1)
                    if not first and s == OUT_AT + 2:
                        dve.wait_ge(o_done, b)
                        xr = g.x1[:, bass.ds((b - 1) * TB, TB), :]
                        dve.tensor_tensor(xr, xr, ps[:, VB[0], :].rearrange("p (t d) -> p t d", t=TB),
                                          ALU.add).then_inc(o_added, 1)

            row(0, first=True)
            with dve.Fori(1, B) as b:
                row(b)
            row(B, drain=True)

        @block.tensor
        def _(pe):
            pe.wait_ge(rows_in, 16)
            for t in range(ST):
                ins = pe.transpose(ps[:, t // 4, (t % 4) * P:(t % 4 + 1) * P], rows[:, t, :], g.ident[:])
            ins.then_inc(rowsT_done, 1)
            pe.wait_ge(rowsT_kept, 2)
            pe.wait_ge(prep, 1)

            def up(e):
                if e >= 2:
                    pe.wait_ge(h_kept, FT * (e - 1))
                for f in range(FT):
                    ins = pe.matmul(ps[:, 2 + e % 2, f * CAP:(f + 1) * CAP], g.w1_sb[:, e, f * P:(f + 1) * P],
                                    rowsT[:, e * CAP:(e + 1) * CAP], start=True, stop=True)
                ins.then_inc(h_done, 1)

            def down(e):
                pe.wait_ge(h_kept, FT * (e + 1))
                if e >= 2:
                    pe.wait_ge(eo_kept, e - 1)
                pe.matmul(ps[0:CAP, 4 + e % 2, 0:D], one_row[0:1, 0:CAP], g.b2_sb[0:1, e, :], start=True, stop=False)
                for f in range(FT):
                    ins = pe.matmul(ps[0:CAP, 4 + e % 2, 0:D], hT[:, e % 2, f, :], g.w2_sb[:, e, f, :],
                                    start=False, stop=(f == FT - 1))
                ins.then_inc(eo_done, 1)

            up(0)
            for e in range(E):
                if e + 1 < E:
                    up(e + 1)
                down(e)
            pe.wait_ge(eo_kept, E)
            pe.wait_ge(k_lo_filled, 1)

            def project(b, h, first=False):
                if not first or h:
                    pe.wait_ge(qk_kept, b * 2 * H + 2 * h)
                pe.matmul(ps[:, PJ, :], g.wqk_sb[:, h, :], xTb, start=True, stop=True).then_inc(qk_done, 1)

            def row(b, first=False, drain=False):
                for s in range(DRAIN if drain else STEPS):
                    if s == 0 and not drain:
                        pe.wait_ge(row_staged, b + 1)
                        project(b, 0, first)
                    def scores():
                        h, t = s // TB, s % TB
                        if t == 0:
                            pe.wait_ge(qk_kept, b * 2 * H + 2 * (h + 1))
                        if not first or s >= 2:
                            pe.wait_ge(exp_ready, b * STEPS + s - 1)
                        q = q_parts[:, h % 2, t * P:(t + 1) * P]
                        pe.matmul(ps[:, SB[s % 2], :], q, k_hi[:, h % 2, :], start=True, stop=False)
                        pe.matmul(ps[:, SB[s % 2], :], q, k_lo[:, h % 2, :], start=False, stop=True).then_inc(s_done, 1)

                    if s and not drain:
                        scores()
                    if not drain and s % TB == QK_AT and s // TB + 1 < H:
                        project(b, s // TB + 1, first)
                    late = s - LAG_T
                    if runs(late, first, drain):
                        by_act = [k % TB in ON_ACT for k in range(STEPS)]
                        n = sum(by_act[:late % STEPS + 1]) - (sum(by_act) if late < 0 else 0)
                        if late % TB in ON_ACT:
                            pe.wait_ge(act_p_ready, b * sum(by_act) + n)
                        else:
                            pe.wait_ge(p_ready, b * (STEPS - sum(by_act)) + late + 1 - n)
                        if not first or late >= 2:
                            pe.wait_ge(lo_kept, b * STEPS + late - 1)
                        for m in range(TB):
                            ins = pe.transpose(ps[:, TBK[late % 2], m * P:(m + 1) * P],
                                               ex[:, late % 4, m * P:(m + 1) * P], g.ident[:])
                        ins.then_inc(pT_done, 1)
                    if not drain and s in VALUES_AT:
                        n, j = VALUES.index(VALUES_AT[s]), VALUES_AT[s]
                        if not first or n >= 2:
                            pe.wait_ge(v_kept, b * 2 * TB + n - 1)
                        if not first and n == 4:
                            pe.wait_ge(o_added, b)
                        pe.matmul(ps[:, VB[n % 2], :], xTb[:, (j // 2) * P:(j // 2 + 1) * P],
                                  g.wv_sb[:, (j % 2) * 512:(j % 2 + 1) * 512], start=True, stop=True).then_inc(v_done, 1)
                    if s == 0 and not drain:
                        scores()
                    late = s - LAG_W - (TB - 1)
                    half = late % TB
                    if half < 2 and runs(late - half, first, drain):
                        h = (late - half) // TB
                        if half == 0:
                            pe.wait_ge(lo_kept, b * STEPS + (h + 1) * TB)
                            if h % H == 0 and not first:
                                pe.wait_ge(oT_kept, b)
                        if h == 0 or h == H // 2:
                            pe.wait_ge(v_kept, b * 2 * TB + (h != 0) * TB + 2 * (half + 1))
                        hs = slice(h % H * D, (h % H + 1) * D)
                        for m in (2 * half, 2 * half + 1):
                            begins, ends = h % H == 0 and m == 0, h % H == H - 1 and m == TB - 1
                            pe.matmul(ps[:, AV, :], V_hi[:, m, hs], pT_hi[:, h % 2, m, :], start=begins, stop=False)
                            pe.matmul(ps[:, AV, :], V_lo[:, m, hs], pT_hi[:, h % 2, m, :], start=False, stop=False)
                            ins = pe.matmul(ps[:, AV, :], V_hi[:, m, hs], pT_lo[:, h % 2, m, :], start=False, stop=ends)
                        if half:
                            ins.then_inc(av_done, 1)
                    if not first and s == OUT_AT + 1:
                        pe.wait_ge(oT_kept, b)
                        if not drain:
                            pe.wait_ge(v_kept, b * 2 * TB + 3)
                        for t in range(TB):
                            ins = pe.transpose(ps[:, VB[0], t * P:(t + 1) * P], oT[:, t * P:(t + 1) * P], g.ident[:])
                        ins.then_inc(o_done, 1)

            row(0, first=True)
            with pe.Fori(1, B) as b:
                row(b)
            row(B, drain=True)


def prepare_constants(pool, g, made, prep):
    pool.memset(g.sel[:], 0.0).then_inc(made, 1)
    pool.memset(g.mask_c, 1.0).then_inc(made, 1)
    pool.memset(g.phi_cols[:], 0.0)
    pool.memset(g.weT[:, D:DV], 0.0)
    pool.memset(g.V2[:, :, D:DV], 1.0)
    pool.memset(g.sumsT[:], 0.0)
    pool.memset(g.exT[:], 0.0)
    pool.memset(g.eps[:], EPS_RHO)
    pool.memset(g.ones[:], 1.0)
    pool.memset(g.rho, -math.sqrt(EPS_RHO))
    pool.wait_ge(made, 2)
    v = g.sel[:].rearrange("p g c (h a) -> p g c h a", h=2)
    for gg in range(GROUPS):
        for half in range(2):
            if half:
                pool.wait_ge(prep, gg + 1)
            ins = pool.affine_select(out=v[:, gg], in_=v[:, gg], compare_op=ALU.not_equal, fill=1.0,
                                     base=-2 * gg - 16 * half, pattern=[[-32, QUADS], [-1, 2], [0, A]],
                                     channel_multiplier=1)
            if not half:
                ins.then_inc(prep, 1)
    pool.affine_select(out=g.mask_c, in_=g.mask_c, compare_op=ALU.is_ge, fill=0.0, base=-16,
                       pattern=[[-32, QUADS]], channel_multiplier=1).then_inc(made, 1)
    pool.wait_ge(made, 3)
    pool.affine_select(out=g.mask_c, in_=g.mask_c, compare_op=ALU.is_ge, fill=0.0, base=31,
                       pattern=[[32, QUADS]], channel_multiplier=-1).then_inc(made, 1)


def second_route(nc, g, take):
    with ExitStack() as ctx:
        def sb(name, shape, dt=F32):
            return ctx.enter_context(nc.sbuf_tensor(name, shape, dt))

        def sem(name):
            return ctx.enter_context(nc.semaphore(name))

        xn = take(NT, D)
        shareT = take(TOK)
        gw = take(E)
        b3 = take(D)
        p1 = take(NT)
        p2 = take(NT)
        top2 = take(NT)
        term = take(NT, E)
        psX = ctx.enter_context(nc.psum_tensor("psX1", [P, 4, 512], F32))
        psL = ctx.enter_context(nc.psum_tensor("psL1", [P, NT, E], F32))
        psP = ctx.enter_context(nc.psum_tensor("psP1", [P, 3, 512], F32))
        gate_in, r_steps = sem("gate1_in"), sem("r_steps")
        var_ready, std_ready = sem("var1_ready"), sem("std1_ready")
        xn_ready, xT_done, xT_kept = sem("xn1_ready"), sem("xT1_done"), sem("xT1_kept")
        logits_done, gap_ready, exp_done = sem("logits1_done"), sem("gap_ready"), sem("exp1_done")
        share_ready, shareT_done, shareT_kept = sem("share_ready"), sem("shareT_done"), sem("shareT_kept")
        b3_done, b3_added = sem("b3_done"), sem("b3_added")
        q_done, k_done, v_done, q_kept, k_kept, v_kept = (sem("q2_done"), sem("k2_done"), sem("v2_done"),
                                                          sem("q2_kept"), sem("k2_kept"), sem("v2_kept"))
        bias_done, const_steps = sem("bias_done"), sem("const_steps")
        bias_steps = sem("bias_steps")
        block = ctx.enter_context(nc.Block())

        @block.sync
        def _(sp):
            sp.dma_start(gw, g.gate1_w).then_inc(gate_in, 16)
            sp.dma_start(g.gateb[:], g.gate1_b.partition_broadcast(P)).then_inc(gate_in, 16)
            sp.dma_start(b3[0:E, :], g.e_b3).then_inc(gate_in, 16)

        @block.scalar
        def _(act):
            act.wait_ge(var_ready, 1)
            act.activation(g.std[:], g.std[:], ACT.Sqrt).then_inc(std_ready, 1)
            for c in range(4):
                act.wait_ge(xT_done, c + 1)
                act.activation(g.xnT[:, c * 512:(c + 1) * 512], psX[:, c, :], ACT.Copy).then_inc(xT_kept, 1)
            qv = psP[:, 0, :].rearrange("p (n h) -> p n h", h=2)
            for c in range(B):
                act.wait_ge(q_done, c + 1)
                for h in range(2):
                    act.activation(g.q2[h * A:(h + 1) * A, c * N // 2:(c + 1) * N // 2],
                                   qv[h * A:(h + 1) * A, :, h], ACT.Copy).then_inc(q_kept, 1)
                act.wait_ge(k_done, c + 1)
                act.activation(g.kT2[:, c * N:(c + 1) * N], psP[:, 1, :], ACT.Copy).then_inc(k_kept, 1)
                if c == 1:
                    act.wait_ge(gap_ready, 1)
                    act.activation(p2, p2, ACT.Exp).then_inc(exp_done, 1)
            act.wait_ge(shareT_done, 1)
            act.activation(shareT[0:E, :].rearrange("p (c n) -> p c n", c=4), psX[0:E, :, :],
                           ACT.Copy).then_inc(shareT_kept, 1)

        @block.vector
        def _(dve):
            chain = Chain(dve, r_steps)
            for t in range(NT):
                chain.step(dve.scalar_tensor_tensor(g.x1[:, t, :], g.gathered[:, t, :], g.coef[:, t:t + 1],
                                                    g.x1[:, t, :], ALU.mult, ALU.add))
            chain.done()
            norm_scale(dve, chain, g.x1, g.stats, g.mv, g.std[:], g.rstd[:], var_ready, std_ready)
            for t in range(NT):
                dve.tensor_scalar(xn[:, t, :], g.x1[:, t, :], g.mv[:, t, 0:1], g.rstd[:, t:t + 1],
                                  ALU.subtract, ALU.mult).then_inc(xn_ready, 1)

            def keep_values(c):
                dve.wait_ge(v_done, c + 1)
                dve.tensor_tensor(g.V2[:, c * TB:(c + 1) * TB, 0:D], psP[:, 2, :].rearrange("p (t d) -> p t d", t=TB),
                                  g.value_bias[:].unsqueeze(1).to_broadcast([P, TB, D]), ALU.add).then_inc(v_kept, 1)

            dve.wait_ge(bias_done, 1)
            dve.tensor_tensor(g.value_bias[:], psP[:, 0, 0:D], g.web, ALU.add).then_inc(bias_steps, 1)
            dve.wait_ge(bias_steps, 1)
            dve.tensor_tensor(g.value_bias[:], g.value_bias[:], g.wyb, ALU.add).then_inc(bias_steps, 1)
            flat = g.phi_cols[:].rearrange("p g n -> p (g n)")
            for h in range(2):
                for d in range(2):
                    at = 16 * d + h
                    col = flat[h * A:(h + 1) * A, at:at + 34 * (GROUPS - 1) + 1:34]
                    dve.tensor_copy(col, g.phi[h * A:(h + 1) * A, :].to_broadcast([A, GROUPS])).then_inc(const_steps, 1)
            dve.tensor_reduce(g.split_by[:], g.mask_c, axis=AX.X, op=ALU.add, negate=True).then_inc(const_steps, 1)
            dve.wait_ge(logits_done, 1)
            chain.link(dve.tensor_tensor(g.lg[:], psL[:], g.gateb[:].unsqueeze(1).to_broadcast([P, NT, E]), ALU.add))
            first_max(dve, chain, g.lg[:], g.desc[:], g.top[:], g.tie[:], g.rank[:], g.mask1[:])
            keep_values(0)
            chain.link(dve.scalar_tensor_tensor(g.lg[:], g.mask1[:], -1e30, g.lg[:], ALU.mult, ALU.add))
            first_max(dve, chain, g.lg[:], g.desc[:], top2, g.tie[:], g.rank[:], g.mask2[:])
            dve.tensor_tensor(p2, top2, g.top[:], ALU.subtract).then_inc(gap_ready, 1)
            keep_values(1)
            dve.wait_ge(exp_done, 1)
            chain.link(dve.tensor_scalar(p1, p2, 1.0, None, ALU.add))
            chain.link(dve.reciprocal(p1, p1))
            chain.link(dve.tensor_tensor(p2, p2, p1, ALU.mult))
            chain.link(dve.tensor_tensor(term, g.mask1[:], per_tile(p1, E), ALU.mult))
            chain.link(dve.tensor_tensor(g.mask2[:], g.mask2[:], per_tile(p2, E), ALU.mult))
            dve.tensor_tensor(g.share[:], term, g.mask2[:], ALU.add).then_inc(share_ready, 1)
            keep_values(2)
            keep_values(3)
            dve.wait_ge(shareT_done, 1)
            chain.link(dve.tensor_scalar(g.share[:], g.share[:], 0.5, None, ALU.mult))
            for c in range(4):
                dve.wait_ge(b3_done, c + 1)
                xr = g.x1[:, c * TB:(c + 1) * TB, :]
                dve.tensor_tensor(xr, xr, psX[:, c, :].rearrange("p (t d) -> p t d", t=TB), ALU.add).then_inc(b3_added, 1)

        @block.tensor
        def _(pe):
            pe.matmul(psP[:, 0, 0:D], g.rho[0:A, :], g.weT[0:A, 0:D], start=True, stop=True).then_inc(bias_done, 1)
            for t in range(NT):
                pe.wait_ge(xn_ready, t + 1)
                ins = pe.transpose(psX[:, t // TB, (t % TB) * P:(t % TB + 1) * P], xn[:, t, :], g.ident[:])
                if t % TB == TB - 1:
                    ins.then_inc(xT_done, 1)
            pe.wait_ge(gate_in, 48)
            for t in range(NT):
                if t % TB == 0:
                    pe.wait_ge(xT_kept, t // TB + 1)
                ins = pe.matmul(psL[:, t, :], g.xnT[:, t * P:(t + 1) * P], gw, start=True, stop=True)
            ins.then_inc(logits_done, 1)
            for c in range(B):
                xc = g.xnT[:, c * N:(c + 1) * N]
                if c:
                    pe.wait_ge(q_kept, 2 * c)
                else:
                    pe.wait_ge(bias_steps, 1)
                pe.matmul(psP[:, 0, :], g.wq, xc, start=True, stop=True).then_inc(q_done, 1)
                if c:
                    pe.wait_ge(k_kept, c)
                pe.matmul(psP[:, 1, :], g.wk, xc, start=True, stop=True).then_inc(k_done, 1)
                if c:
                    pe.wait_ge(v_kept, c)
                for i in range(TB):
                    t = c * TB + i
                    ins = pe.matmul(psP[:, 2, i * D:(i + 1) * D], g.xnT[:, t * P:(t + 1) * P], g.wy,
                                    start=True, stop=True)
                ins.then_inc(v_done, 1)
            pe.wait_ge(share_ready, 1)
            for t in range(NT):
                ins = pe.transpose(psX[0:E, t // TB, (t % TB) * P:(t % TB + 1) * P], g.share[:, t, :], g.ident[:])
            ins.then_inc(shareT_done, 1)
            pe.wait_ge(shareT_kept, 1)
            for t in range(NT):
                ins = pe.matmul(psX[:, t // TB, (t % TB) * P:(t % TB + 1) * P], shareT[0:E, t * P:(t + 1) * P],
                                b3[0:E, :], start=True, stop=True)
                if t % TB == TB - 1:
                    ins.then_inc(b3_done, 1)


def second_layer(nc, g, sb):
    x1, xnT, ident = g.x1, g.xnT, g.ident
    share = g.share[:].rearrange("p t e -> p (t e)")
    MB = TOK // BLK
    BB = N // BLK
    ON_ACT = [2, 2, 2, 2, 2, 2, 2, 2]
    ON_DVE = [QUADS - n for n in ON_ACT]
    BANKS = 3
    with ExitStack() as ctx:
        def sem(name):
            return ctx.enter_context(nc.semaphore(name))

        feat = g.arena[:].rearrange("p (s k n) -> p s k n", s=2, k=PAIRS)
        kT, q2, V, exT, sumsT, sel, weT = g.kT2, g.q2, g.V2, g.exT, g.sumsT, g.sel, g.weT
        phi_cols, eps = g.phi_cols, g.eps
        b1, b2, bg, ones = g.b1e, g.b2e, g.bge, g.ones
        ex = sb("ex2", [P, 2, N])
        exh = sb("exh", [P, N], F16)
        spread = sb("spread", [P, 2, N], F16)
        nmax = sb("nmax2", [P, 2])
        shift = sb("shift", [P, 2])
        sums = sb("sums", [P, 2, GROUPS, QUADS])
        den = sb("den2", [P, 1])
        w1, w2, wg, w3 = g.w1e, g.w2e, g.wge, g.w3e
        left = sb("left", [P, GT, N])
        z = sb("z", [P, GT, N])
        s = sb("s", [P, GT, N])

        ps = ctx.enter_context(nc.psum_tensor("ps2", [P, 8, 512], F32))
        psS, psB = ps[:, 0, :], ps[:, 2:5, :]
        psT = psO = ps[:, 5, :]
        psX, psY, psZ = ps[:, 6, :], ps[:, 7, :], ps[:, 1, :]

        feat_ready, act_feat, e_ready = sem("feat_ready"), sem("act_feat"), sem("e_ready")
        s_done, max_ready, shift_ready = sem("s2_done"), sem("max_ready"), sem("shift_ready")
        ex_ready, exh_ready, spread_ready = sem("ex_ready"), sem("exh_ready"), sem("spread_ready")
        bc_done, reduced, placed = sem("bc_done"), sem("reduced"), sem("placed")
        exT_done, exT_kept = sem("exT_done"), sem("exT_kept")
        o_done, fin_steps, fin_ready, out_done = sem("o2_done"), sem("fin_steps"), sem("fin_ready"), sem("out_done")
        w12_in, wg_in, w3_in = sem("w12_in"), sem("wg_in"), sem("w3_in")
        left_done, right_done, left_kept, z_ready = sem("left_done"), sem("right_done"), sem("left_kept"), sem("z_ready")
        gate_done, tanh_ready, s_ready, y_done, y_added = sem("gate_done"), sem("tanh_ready"), sem("s_ready"), sem("y_done"), sem("y_added")
        act_passed, pool_passed = sem("act_passed"), sem("pool_passed")

        FEATURE_LAG = 1
        SCORES_AT = {(6, 2): 0, (7, 0): 1, (7, 2): 2, (0, 0): 3, (0, 2): 4, (1, 0): 5, (2, 2): 6, (3, 2): 7}

        LEFT_AT, EXT_AT = (7, 1), 7

        def behind(m, j, gg, lag):
            if gg >= lag:
                return m + 2, j, gg - lag, 2
            return m + 1, 1 - j, gg - lag + GROUPS, 1

        FEATURES_AHEAD = 2 * (PAIRS - sum(ON_DVE))

        def makes(late, first, last):
            if first and late[1] == 1 and late[3] == 1:
                return False
            return not last or (late[1] == 1 and late[3] == 1)

        SPLIT_AT, SILU_AT = (7, 1), ((6, 2), (6, 3))
        AHEAD_EXP = (3, 0)

        def slot_parts(m):
            return m // BB, m * PAIRS

        with nc.Block() as block:
            @block.vector
            def _(dve):
                def feature(m, j, gg, c, ahead=False):
                    if ahead or c < ON_DVE[gg]:
                        b, pair0 = slot_parts(m)
                        dve.tensor_scalar(feat[:, j, QUADS * gg + c, :], kT[:, bass.ds(b * N, N)],
                                          q2[:, bass.ds(pair0 + GROUPS * c + gg, 1)], 0.0,
                                          ALU.add, ALU.max).then_inc(feat_ready, 1)

                def largest(m, j):
                    dve.wait_ge(s_done, m + 1)
                    dve.reduce_max(nmax[:, j:j + 1], psS, axis=AX.X, negate=True).then_inc(max_ready, 1)
                    dve.wait_ge(max_ready, m + 1)
                    dve.tensor_scalar(shift[:, j:j + 1], nmax[:, j:j + 1], EX_LIFT * math.log(2.0), None,
                                      ALU.add).then_inc(shift_ready, 1)

                def reduce_pair(m, j, gg, c):
                    k = QUADS * gg + c
                    dve.wait_ge(bc_done, m * PAIRS + k + 1)
                    dve.scalar_tensor_tensor(feat[:, j, k, :], feat[:, j, k, :], 1.0, psB[:, k % BANKS, :],
                                             ALU.mult, ALU.mult,
                                             accum_out=sums[:, j, gg, c:c + 1]).then_inc(reduced, 1)

                def finish(m, part):
                    row = x1[:, bass.ds(m // 2, 1), :].rearrange("p t d -> p (t d)")
                    if part == 0:
                        dve.wait_ge(o_done, m + 1)
                    else:
                        dve.wait_ge(fin_steps, m * 2 + part)
                    if part == 0:
                        dve.tensor_scalar(den[:], psO[:, D:DV], EPS_DEN * 2.0 ** EX_LIFT, None,
                                          ALU.add).then_inc(fin_steps, 1)
                    elif part == 1:
                        dve.reciprocal(den[:], den[:]).then_inc(fin_steps, 1)
                    else:
                        dve.scalar_tensor_tensor(row, psO[:, 0:D], den[:], row, ALU.mult, ALU.add).then_inc(fin_ready, 1)

                def product(m, f, first=False):
                    dve.wait_ge(right_done, m * GT + f + 1)
                    dve.wait_ge(left_kept, m * GT + f + 1)
                    if not first:
                        dve.wait_ge(gate_done, m * GT)
                    dve.scalar_tensor_tensor(z[:, f, :], psX, b2[:, f, bass.ds(m % E, 1)], left[:, f, :],
                                             ALU.add, ALU.mult).then_inc(z_ready, 1)

                def silu(m, f):
                    dve.wait_ge(tanh_ready, m * GT + f + 1)
                    dve.scalar_tensor_tensor(s[:, f, :], s[:, f, :], 1.0, (psZ, psX)[f], ALU.add,
                                             ALU.mult).then_inc(s_ready, 1)

                def add_experts(m, i, first=False):
                    if i == 0:
                        if not first:
                            dve.wait_ge(y_added, m * TB)
                        dve.wait_ge(y_done, m + 1)
                        dve.wait_ge(fin_ready, m + 1)
                    row = x1[:, bass.ds(m // E * TB + i, 1), :].rearrange("p t d -> p (t d)")
                    dve.scalar_tensor_tensor(row, psY[:, i * D:(i + 1) * D],
                                             share[:, bass.ds(m // E * (TB * E) + i * E + m % E, 1)], row,
                                             ALU.mult, ALU.add).then_inc(y_added, 1)

                def split(m, j, before=2):
                    dve.wait_ge(exh_ready, m + 1)
                    if before == 2:
                        dve.wait_ge(bc_done, (m - 1) * PAIRS)
                    dve.scalar_tensor_tensor(spread[:, j, :], exh[:], g.split_by[:], ex[:, j, :],
                                             ALU.mult, ALU.add).then_inc(spread_ready, 1)

                def tile(t, first=False, last=False):
                    for j in range(2):
                        m = t * 2 + j
                        none, final = first and j == 0, last and j == 1
                        work = {
                            (1, 2): lambda: product(m, 0, none),
                            (3, 0): lambda: product(m, 1, none),
                            (2, 0): lambda: none or finish(m - 1, 0),
                            (2, 1): lambda: none or finish(m - 1, 1),
                            (2, 2): lambda: none or finish(m - 1, 2),
                            (4, 0): lambda: none or add_experts(m - 1, 0, first),
                            (4, 3): lambda: final or largest(m + 1, 1 - j),
                            (5, 0): lambda: none or add_experts(m - 1, 1),
                            (5, 2): lambda: none or add_experts(m - 1, 2),
                            (5, 3): lambda: none or add_experts(m - 1, 3),
                            SILU_AT[0]: lambda: silu(m, 0),
                            SILU_AT[1]: lambda: silu(m, 1),
                            SPLIT_AT: lambda: final or split(m + 1, 1 - j, before=1 if none else 2),
                        }
                        for gg in range(GROUPS):
                            late = behind(m, j, gg, FEATURE_LAG)
                            for c in range(QUADS):
                                reduce_pair(m, j, gg, c)
                                if (gg, c) in work:
                                    work[gg, c]()
                                if makes(late, first, last):
                                    if c == 0:
                                        dve.wait_ge(reduced, (late[0] - 2) * PAIRS + QUADS * (late[2] + 1))
                                    feature(*late[0:3], c)

                for n in range(2 * GROUPS):
                    for c in range(QUADS):
                        feature(n // GROUPS, n // GROUPS, n % GROUPS, c, ahead=True)
                    if n == GROUPS + AHEAD_EXP[0]:
                        largest(0, 0)
                split(0, 0, before=0)
                tile(0, first=True)
                with dve.Fori(1, NT - 1) as t:
                    tile(t)
                tile(NT - 1, last=True)
                for part in range(3):
                    finish(MB - 1, part)
                for i in range(TB):
                    add_experts(MB - 1, i)

            @block.scalar
            def _(act):
                def roots(m, j, gg, ahead=False):
                    b, pair0 = slot_parts(m)
                    if ahead:
                        if gg % 2:
                            act.wait_ge(feat_ready, m * PAIRS + QUADS * (gg + 1))
                    else:
                        act.wait_ge(reduced, m * PAIRS - 2 * PAIRS + QUADS * (gg + 1))
                        act.sem_inc(act_passed, 1)
                        for c in range(ON_DVE[gg], QUADS):
                            act.activation(feat[:, j, QUADS * gg + c, :], kT[:, bass.ds(b * N, N)], ACT.Relu,
                                           bias=q2[:, bass.ds(pair0 + GROUPS * c + gg, 1)]).then_inc(act_feat, 1)
                        if gg % 2:
                            act.wait_ge(feat_ready, m * sum(ON_DVE) + FEATURES_AHEAD + sum(ON_DVE[:gg + 1]))
                            act.wait_ge(act_feat, (m - 2) * sum(ON_ACT) + sum(ON_ACT[:gg + 1]))
                    if gg % 2:
                        grp = feat[:, j, QUADS * (gg - 1):QUADS * (gg + 1), :].rearrange("p k n -> p (k n)")
                        act.activation(grp, grp, ACT.Sqrt, bias=eps[:]).then_inc(e_ready, 2)

                def exponentials(m, j, before=2):
                    act.wait_ge(shift_ready, m + 1)
                    if before == 2:
                        act.wait_ge(exT_done, m - 1)
                        act.wait_ge(spread_ready, m - 1)
                    act.activation(ex[:, j, :], psS, ACT.Exp, bias=shift[:, j:j + 1]).then_inc(ex_ready, 1)
                    if before:
                        act.wait_ge(spread_ready, m)
                    act.activation(exh[:], psS, ACT.Exp, bias=shift[:, j:j + 1]).then_inc(exh_ready, 1)

                def keep_exT(m, j, warm=True):
                    act.wait_ge(exT_done, m + 1)
                    if warm:
                        act.wait_ge(o_done, m - 1)
                    act.activation(exT[:, j, :, j * BLK:(j + 1) * BLK].rearrange("p t (c r) -> p t c r", c=QUADS),
                                   psT.rearrange("p (t c r) -> p t c r", t=TB, c=QUADS)[:, :, :, 0:16],
                                   ACT.Copy).then_inc(exT_kept, 1)

                def keep_left(m, f, first=False):
                    act.wait_ge(left_done, m * GT + f + 1)
                    if not first:
                        act.wait_ge(z_ready, m * GT - GT + f + 1)
                    act.sem_inc(act_passed, 1)
                    act.activation(left[:, f, :], psY, ACT.Identity, bias=b1[:, f, bass.ds(m % E, 1)]).then_inc(left_kept, 1)

                def tanh_half(m, first=False):
                    if not first:
                        act.wait_ge(y_done, m)
                    for f in range(GT):
                        act.wait_ge(gate_done, m * GT + f + 1)
                        act.activation(s[:, f, :], (psZ, psX)[f], ACT.Tanh, scale=0.5).then_inc(tanh_ready, 1)

                def tile(t, first=False, last=False):
                    for j in range(2):
                        m = t * 2 + j
                        none = first and j == 0
                        for gg in range(GROUPS):
                            if gg == LEFT_AT[0] and not (last and j == 1):
                                keep_left(m + 1, 0)
                            if gg == LEFT_AT[1] and not none:
                                keep_left(m, 1)
                            if gg == EXT_AT:
                                keep_exT(m, j, warm=not first)
                            if gg == 5 and not (last and j == 1):
                                exponentials(m + 1, 1 - j, before=1 if none else 2)
                            if gg == 5:
                                tanh_half(m, none)
                            late = behind(m, j, gg, FEATURE_LAG)
                            if makes(late, first, last):
                                roots(*late[0:3])

                for n in range(2 * GROUPS):
                    roots(n // GROUPS, n // GROUPS, n % GROUPS, ahead=True)
                    if n == GROUPS + AHEAD_EXP[1]:
                        exponentials(0, 0, before=0)
                        keep_left(0, 0, first=True)
                    if n == GROUPS + AHEAD_EXP[1] + 5:
                        keep_left(0, 1, first=True)
                tile(0, first=True)
                with act.Fori(1, NT - 1) as t:
                    tile(t)
                tile(NT - 1, last=True)

            @block.gpsimd
            def _(pool):
                def place(m, j, first=False, warm=True):
                    pool.wait_ge(reduced, (m + 1) * PAIRS)
                    if warm:
                        pool.wait_ge(o_done, m - 1)
                    v = sumsT[:, j, j * BLK:(j + 1) * BLK].rearrange("p (c g h) -> p g c h", c=QUADS, h=2)
                    for h in range(2):
                        if h or not first:
                            pool.wait_ge(placed, 2 * m + h)
                        pool.sem_inc(pool_passed, 1)
                        pool.tensor_copy(v[h * A:(h + 1) * A, :, :, h], sums[h * A:(h + 1) * A, j]).then_inc(placed, 1)

                def tile(t, first=False, last=False):
                    for j in range(2):
                        m = t * 2 + j
                        place(m, j, first and j == 0, warm=not first)

                tile(0, first=True)
                with pool.Fori(1, NT - 1) as t:
                    tile(t)
                tile(NT - 1, last=True)

            @block.tensor
            def _(pe):
                def scores(m, j, gg, first=False):
                    pe.wait_ge(e_ready, m * GROUPS + gg + 1)
                    if gg == 0 and not first:
                        pe.wait_ge(exh_ready, m)
                    for c in range(QUADS):
                        ins = pe.matmul(psS[32 * c:32 * (c + 1), :], phi_cols[:, gg, :],
                                        feat[:, j, QUADS * gg + c, :], start=(gg == 0), stop=(gg == GROUPS - 1))
                    if gg == GROUPS - 1:
                        ins.then_inc(s_done, 1)

                def broadcast(m, j, gg, c, warm=True):
                    k = QUADS * gg + c
                    if warm or k >= BANKS:
                        before = k - BANKS if k >= BANKS else k + PAIRS // BANKS * BANKS - PAIRS
                        before = before - BANKS if before >= 0 and k < BANKS else before
                        pe.wait_ge(reduced, m * PAIRS + before + 1)
                    pe.matmul(psB[:, k % BANKS, :], sel[:, gg, c, :], spread[:, j, :], start=True,
                              stop=True).then_inc(bc_done, 1)

                def transpose_ex(m, j, first=False):
                    pe.wait_ge(ex_ready, m + 1)
                    if not first:
                        pe.wait_ge(fin_ready, m)
                    for i in range(TB):
                        ins = pe.transpose(psT[:, i * P:(i + 1) * P], ex[:, j, i * P:(i + 1) * P], ident[:])
                    ins.then_inc(exT_done, 1)

                def combine(m, j, half):
                    b = m // BB
                    if half == 0:
                        pe.wait_ge(placed, 2 * (m + 1))
                        pe.wait_ge(exT_kept, m + 1)
                    for i in (2 * half, 2 * half + 1):
                        pe.matmul(psO[:, 0:DV], exT[:, j, i, :],
                                  V[:, bass.ds(b * TB + i, 1), :].rearrange("p t d -> p (t d)"),
                                  start=(i == 0), stop=False)
                    if half:
                        pe.matmul(psO[:, 0:DV], sumsT[:, j, :], weT[:], start=False, stop=True).then_inc(o_done, 1)

                def left_product(m, f, first=0):
                    if f == 0:
                        pe.wait_ge(w12_in, (m + 1) * 32)
                        if first < 2:
                            pe.wait_ge(left_kept, m * GT)
                        if first < 1:
                            pe.wait_ge(y_added, (m - 1) * TB)
                    else:
                        pe.wait_ge(left_kept, m * GT + 1)
                    pe.matmul(psY, w1[:, f * P:(f + 1) * P], xnT[:, bass.ds(m // E * N, N)], start=True,
                              stop=True).then_inc(left_done, 1)

                def right_product(m, f, first=0):
                    if f:
                        pe.wait_ge(z_ready, m * GT + 1)
                    elif first < 2:
                        pe.wait_ge(s_ready, m * GT)
                    pe.matmul(psX, w2[:, f * P:(f + 1) * P], xnT[:, bass.ds(m // E * N, N)], start=True,
                              stop=True).then_inc(right_done, 1)

                def gate(m, f, half):
                    if half == 0 and f == 0:
                        pe.wait_ge(z_ready, (m + 1) * GT)
                        pe.wait_ge(wg_in, (m + 1) * 32)
                    if half == 0:
                        pe.matmul((psZ, psX)[f], bg[0:1, f * P:(f + 1) * P], ones[0:1, :], start=True, stop=False)
                    ins = pe.matmul((psZ, psX)[f], wg[:, half * DFF + f * P:half * DFF + (f + 1) * P], z[:, half, :],
                                    start=False, stop=(half == 1))
                    if half:
                        ins.then_inc(gate_done, 1)

                def down(m, half, last=False):
                    if half == 0:
                        pe.wait_ge(s_ready, (m + 1) * GT)
                        pe.wait_ge(w3_in, (m + 1) * 16)
                        if not last:
                            pe.wait_ge(left_kept, (m + 2) * GT)
                    for i in (2 * half, 2 * half + 1):
                        for f in range(GT):
                            ins = pe.matmul(psY[:, i * D:(i + 1) * D], s[:, f, i * P:(i + 1) * P],
                                            w3[:, f * D:(f + 1) * D], start=(f == 0), stop=(f == GT - 1))
                    if half:
                        ins.then_inc(y_done, 1)

                def tile(t, first=False, last=False):
                    for j in range(2):
                        m = t * 2 + j
                        none, final = first and j == 0, last and j == 1
                        work = {
                            (0, 3): lambda: left_product(m, 1),
                            (1, 1): lambda: none or combine(m - 1, 1 - j, 0),
                            (1, 3): lambda: none or combine(m - 1, 1 - j, 1),
                            (2, 1): lambda: right_product(m, 1),
                            (2, 3): lambda: none or down(m - 1, 0),
                            (3, 1): lambda: none or down(m - 1, 1),
                            (3, 3): lambda: gate(m, 0, 0),
                            (4, 1): lambda: gate(m, 0, 1),
                            (4, 3): lambda: gate(m, 1, 0),
                            (5, 1): lambda: gate(m, 1, 1),
                            (6, 1): lambda: transpose_ex(m, j, none),
                            (6, 3): lambda: final or left_product(m + 1, 0, first=1 if none else 0),
                            (7, 1): lambda: final or right_product(m + 1, 0),
                        }
                        pe.wait_ge(spread_ready, m + 1)
                        for gg in range(GROUPS):
                            for c in range(QUADS):
                                broadcast(m, j, gg, c, warm=not none)
                                if (gg, c) in work:
                                    work[gg, c]()
                                if (gg, c) in SCORES_AT:
                                    k = SCORES_AT[gg, c]
                                    if gg >= 6 and not last:
                                        scores(m + 2, j, k)
                                    elif gg < 6 and not final:
                                        scores(m + 1, 1 - j, k)

                for gg in range(GROUPS):
                    scores(0, 0, gg, first=True)
                left_product(0, 0, first=2)
                right_product(0, 0, first=2)
                for (gg, c), k in SCORES_AT.items():
                    if gg >= 6:
                        scores(1, 1, k)
                tile(0, first=True)
                with pe.Fori(1, NT - 1) as t:
                    tile(t)
                tile(NT - 1, last=True)
                down(MB - 1, 0, last=True)
                down(MB - 1, 1)
                combine(MB - 1, 1, 0)
                combine(MB - 1, 1, 1)

            @block.sync
            def _(sp):
                def load_up(e):
                    sp.dma_start(w1[:], g.e_w1[bass.ds(e, 1), :, :].rearrange("e d f -> (e d) f")).then_inc(w12_in, 16)
                    sp.dma_start(w2[:], g.e_w2[bass.ds(e, 1), :, :].rearrange("e d f -> (e d) f")).then_inc(w12_in, 16)

                def load_gate(e):
                    sp.dma_start(wg[:].rearrange("p (t n) -> p t n", t=GT),
                                 g.e_wg[bass.ds(e, 1), :, :].rearrange("e (t p) n -> p (e t) n", p=P)).then_inc(wg_in, 16)
                    sp.dma_start(bg[:], g.e_bg[bass.ds(e, 1), :]).then_inc(wg_in, 16)

                def load_down(e):
                    sp.dma_start(w3[:].rearrange("p (t n) -> p t n", t=GT),
                                 g.e_w3[bass.ds(e, 1), :, :].rearrange("e (t p) n -> p (e t) n", p=P)).then_inc(w3_in, 16)

                load_up(0)
                load_gate(0)
                load_down(0)
                with sp.Fori(1, MB) as u:
                    sp.wait_ge(right_done, u * GT)
                    load_up(u % E)
                    sp.wait_ge(gate_done, u * GT)
                    load_gate(u % E)
                    sp.wait_ge(y_done, u)
                    load_down(u % E)
                for b in range(B):
                    sp.wait_ge(fin_ready, (b + 1) * BB)
                    sp.wait_ge(y_added, (b + 1) * BB * TB)
                    sp.dma_start(g.out_tiles[:, b * TB:(b + 1) * TB, :], x1[:, b * TB:(b + 1) * TB, :]).then_inc(out_done, 16)
                sp.wait_ge(out_done, 16 * B)


def _layout(inputs):
    import numpy as np

    def heads(w, width):
        return np.asarray(w).reshape(8, width, 128).transpose(2, 0, 1)

    def columns(b):
        b = np.asarray(b)
        return b.reshape(b.shape[0], -1, 128).transpose(2, 1, 0)

    def twice(w):
        return np.concatenate([w, w], axis=1)

    i = {k: np.asarray(v) for k, v in inputs.items()}
    return {
        "x": i["L0_attn_x"],
        "wqk": np.concatenate([heads(i["L0_attn_Wq"], 64), heads(i["L0_attn_Wk"], 64)], axis=2),
        "wv": i["L0_attn_Wv"].T,
        "gate0_w": i["L0_ffn_gate_w"], "gate0_b": i["L0_ffn_gate_b"],
        "w1": i["L0_ffn_w1"], "b1": columns(i["L0_ffn_b1"]).transpose(0, 2, 1), "w2": i["L0_ffn_w2"], "b2": i["L0_ffn_b2"],
        "a_wq": twice(i["L1_attn_Wq"].T), "a_wk": twice(i["L1_attn_Wk"].T),
        "a_phi": np.concatenate([i["L1_attn_Wphi"], i["L1_attn_Wphi"]]).reshape(128, 1),
        "a_wy": i["L1_attn_Wy_w"].T, "a_wyb": i["L1_attn_Wy_b"],
        "a_we": np.concatenate([i["L1_attn_We_w"].T, i["L1_attn_We_w"].T], axis=0), "a_web": i["L1_attn_We_b"],
        "gate1_w": i["L1_ffn_gate_w"], "gate1_b": i["L1_ffn_gate_b"],
        "e_w1": i["L1_ffn_w1"], "e_b1": columns(i["L1_ffn_b1"]),
        "e_w2": i["L1_ffn_w2"], "e_b2": columns(i["L1_ffn_b2"]),
        "e_wg": i["L1_ffn_wg"], "e_bg": i["L1_ffn_bg"],
        "e_w3": i["L1_ffn_w3"], "e_b3": i["L1_ffn_b3"],
    }


def kernel(**inputs):
    import numpy as np
    import concourse.bacc as bacc
    from concourse.bass_utils import run_bass_kernel_spmd

    nc = bacc.Bacc("TRN2", target_bir_lowering=False, num_devices=1)
    arrays, args = {}, {}
    for name, a in _layout(inputs).items():
        a = np.ascontiguousarray(a)
        arrays[f"in_{name}"] = a
        args[name] = nc.dram_tensor(f"in_{name}", a.shape, mybir.dt.from_np(a.dtype), kind="ExternalInput").ap()
    out = nc.dram_tensor("out_0", (B, N, D), F32, kind="ExternalOutput").ap()
    layers_kernel(nc, out=out, **args)
    r = run_bass_kernel_spmd(nc, [arrays], core_ids=[0])
    return r.results[0]["out_0"]
```
